# Optimizing a Trainium2 kernel written in Bass

```python
import numpy as np
import jax
import jax.numpy as jnp

def _softmax(x, axis=-1):
    return jax.nn.softmax(x, axis=axis)

def _gelu(x):
    return jax.nn.gelu(x, approximate=True)

def _silu(x):
    return jax.nn.silu(x)

def _sigmoid(x):
    return jax.nn.sigmoid(x)

def _layernorm(x, axis=-1, eps=1e-05):
    m = jnp.mean(x, axis=axis, keepdims=True)
    v = jnp.var(x, axis=axis, keepdims=True)
    return (x - m) / jnp.sqrt(v + eps)

def _scatter_add(tgt, idx, src, axis=0):
    return tgt.at[idx].add(src)

def _segment_sum(src, seg, n):
    return jax.ops.segment_sum(src, seg, n)
kernel_name = 'mk_gnn_ffn_d1_gnn_r32_e16d57'

def setup_inputs(seed: int=0):
    np.random.seed(seed)
    _w = jnp.asarray

    def _rec_inputs():
        import jax
        import jax.numpy as jnp
        _gk = jax.random.key(seed)
        x = -0.0003713 + 1 * jax.random.normal(jax.random.fold_in(_gk, 1), (3125, 256), jnp.float32)
        _s = jax.random.randint(jax.random.fold_in(_gk, 2), (25000,), 0, 3125, jnp.int32)
        _d = jax.random.randint(jax.random.fold_in(_gk, 3), (25000,), 0, 3125, jnp.int32)
        _loop = jnp.arange(3125, dtype=jnp.int32)
        src = jnp.concatenate([_s, _d, _loop])
        dst = jnp.concatenate([_d, _s, _loop])
        _o = jnp.argsort(dst, stable=True)
        src = src[_o]
        dst = dst[_o]
        edge_attr_4 = jax.random.uniform(jax.random.fold_in(_gk, 11), (53125, 4), jnp.float32, 0.0, 0.999999)
        return (x, src, dst, edge_attr_4)
    x, src, dst, edge_attr_4 = _rec_inputs()

    def _L0_gnn_setup():
        import jax, jax.numpy as jnp
        import numpy as np
        N_NODES = 50000
        N_EDGES = 10000
        HIDDEN = 256
        N_LAYERS = 5
        BN_EPS = 1e-05

        def _mpnn(x, edge_index, edge_attr, mlp_w, mlp_b, ew1, ew2, bn_g, bn_b):
            n = x.shape[0]
            row, col = (edge_index[0], edge_index[1])
            deg = jax.ops.segment_sum(jnp.ones((edge_index.shape[1],), x.dtype), col, num_segments=n)
            dinv = jnp.where(deg > 0, deg ** (-0.5), 0.0)
            norm = dinv[row] * dinv[col]
            h = x
            for l in range(N_LAYERS):
                edge_fea = jnp.concatenate([edge_attr[:, 3:] @ ew1[l], edge_attr[:, 0:3] @ ew2[l]], axis=-1)
                msg = norm[:, None] * (h[row] + edge_fea)
                agg = jax.ops.segment_sum(msg, col, num_segments=n)
                h = jax.nn.relu(jnp.concatenate([h, agg], axis=1) @ mlp_w[l] + mlp_b[l])
                mu = h.mean(axis=0)
                var = h.var(axis=0)
                h = (h - mu) * jax.lax.rsqrt(var + BN_EPS) * bn_g[l] + bn_b[l]
                if l != N_LAYERS - 1:
                    h = jax.nn.relu(h)
            return h
        key = jax.random.key(seed)
        ks = jax.random.split(key, 8)
        x = jax.random.normal(ks[0], (N_NODES, HIDDEN), dtype=jnp.float32)
        edge_index = jax.random.randint(ks[1], (2, N_EDGES), 0, N_NODES, dtype=jnp.int64)
        edge_attr = jax.random.uniform(ks[2], (N_EDGES, 4), dtype=jnp.float32)
        mlp_w = jax.random.normal(ks[3], (N_LAYERS, 2 * HIDDEN, HIDDEN), dtype=jnp.float32) * (1.0 / np.sqrt(2 * HIDDEN))
        mlp_b = jnp.zeros((N_LAYERS, HIDDEN), dtype=jnp.float32)
        ew1 = jax.random.normal(ks[4], (N_LAYERS, 1, HIDDEN // 2), dtype=jnp.float32)
        ew2 = jax.random.normal(ks[5], (N_LAYERS, 3, HIDDEN // 2), dtype=jnp.float32) * (1.0 / np.sqrt(3.0))
        bn_g = jnp.ones((N_LAYERS, HIDDEN), dtype=jnp.float32)
        bn_b = jnp.zeros((N_LAYERS, HIDDEN), dtype=jnp.float32)
        return {'x': x, 'edge_index': edge_index, 'edge_attr': edge_attr, 'mlp_w': mlp_w, 'mlp_b': mlp_b, 'ew1': ew1, 'ew2': ew2, 'bn_g': bn_g, 'bn_b': bn_b}
    _L0_gnn_all = _L0_gnn_setup()
    _L0_gnn_in = {k: v for k, v in _L0_gnn_all.items() if k in ('mlp_w', 'mlp_b', 'ew1', 'ew2', 'bn_g', 'bn_b')}
    del _L0_gnn_all

    def _L0_ffn_setup():
        import jax, jax.numpy as jnp
        import numpy as np
        D_MODEL = 256
        EXPERT_DIM = 512
        NUM_EXPERTS = 8
        TOP_K = 2
        SEQ_LEN = 64
        BATCH = 2
        key = jax.random.key(seed)
        ks = jax.random.split(key, 8)
        s = 0.02
        x = jax.random.normal(ks[0], (SEQ_LEN, BATCH, D_MODEL), dtype=jnp.float32)
        Wg = jax.random.normal(ks[1], (D_MODEL, NUM_EXPERTS), dtype=jnp.float32) * s
        bg = jax.random.normal(ks[2], (NUM_EXPERTS,), dtype=jnp.float32) * s
        bias = jnp.zeros((NUM_EXPERTS,), dtype=jnp.float32)
        W1 = jax.random.normal(ks[3], (NUM_EXPERTS, D_MODEL, EXPERT_DIM), dtype=jnp.float32) * s
        b1 = jax.random.normal(ks[4], (NUM_EXPERTS, EXPERT_DIM), dtype=jnp.float32) * s
        W2 = jax.random.normal(ks[5], (NUM_EXPERTS, EXPERT_DIM, D_MODEL), dtype=jnp.float32) * s
        b2 = jax.random.normal(ks[6], (NUM_EXPERTS, D_MODEL), dtype=jnp.float32) * s
        return {'x': x, 'Wg': Wg, 'bg': bg, 'bias': bias, 'W1': W1, 'b1': b1, 'W2': W2, 'b2': b2}
    _L0_ffn_all = _L0_ffn_setup()
    _L0_ffn_in = {k: v for k, v in _L0_ffn_all.items() if k in ('Wg', 'bg', 'bias', 'W1', 'b1', 'W2', 'b2')}
    del _L0_ffn_all
    return {'x': x, 'src': src, 'dst': dst, 'edge_attr_4': edge_attr_4, 'L0_gnn_mlp_w': _L0_gnn_in['mlp_w'], 'L0_gnn_mlp_b': _L0_gnn_in['mlp_b'], 'L0_gnn_ew1': _L0_gnn_in['ew1'], 'L0_gnn_ew2': _L0_gnn_in['ew2'], 'L0_gnn_bn_g': _L0_gnn_in['bn_g'], 'L0_gnn_bn_b': _L0_gnn_in['bn_b'], 'L0_ffn_Wg': _L0_ffn_in['Wg'], 'L0_ffn_bg': _L0_ffn_in['bg'], 'L0_ffn_bias': _L0_ffn_in['bias'], 'L0_ffn_W1': _L0_ffn_in['W1'], 'L0_ffn_b1': _L0_ffn_in['b1'], 'L0_ffn_W2': _L0_ffn_in['W2'], 'L0_ffn_b2': _L0_ffn_in['b2']}

def reference(x, src, dst, edge_attr_4, L0_gnn_mlp_w, L0_gnn_mlp_b, L0_gnn_ew1, L0_gnn_ew2, L0_gnn_bn_g, L0_gnn_bn_b, L0_ffn_Wg, L0_ffn_bg, L0_ffn_bias, L0_ffn_W1, L0_ffn_b1, L0_ffn_W2, L0_ffn_b2):
    import jax
    import jax.numpy as jnp

    def _L0_gnn_ref(x, edge_index, edge_attr, mlp_w, mlp_b, ew1, ew2, bn_g, bn_b):
        import jax, jax.numpy as jnp
        import numpy as np
        N_NODES = 50000
        N_EDGES = 10000
        HIDDEN = 256
        N_LAYERS = 5
        BN_EPS = 1e-05

        def _mpnn(x, edge_index, edge_attr, mlp_w, mlp_b, ew1, ew2, bn_g, bn_b):
            n = x.shape[0]
            row, col = (edge_index[0], edge_index[1])
            deg = jax.ops.segment_sum(jnp.ones((edge_index.shape[1],), x.dtype), col, num_segments=n)
            dinv = jnp.where(deg > 0, deg ** (-0.5), 0.0)
            norm = dinv[row] * dinv[col]
            h = x
            for l in range(N_LAYERS):
                edge_fea = jnp.concatenate([edge_attr[:, 3:] @ ew1[l], edge_attr[:, 0:3] @ ew2[l]], axis=-1)
                msg = norm[:, None] * (h[row] + edge_fea)
                agg = jax.ops.segment_sum(msg, col, num_segments=n)
                h = jax.nn.relu(jnp.concatenate([h, agg], axis=1) @ mlp_w[l] + mlp_b[l])
                mu = h.mean(axis=0)
                var = h.var(axis=0)
                h = (h - mu) * jax.lax.rsqrt(var + BN_EPS) * bn_g[l] + bn_b[l]
                if l != N_LAYERS - 1:
                    h = jax.nn.relu(h)
            return h
        return _mpnn(x, edge_index, edge_attr, mlp_w, mlp_b, ew1, ew2, bn_g, bn_b)

    def _L0_ffn_ref(x, Wg, bg, bias, W1, b1, W2, b2):
        import jax, jax.numpy as jnp
        import numpy as np
        D_MODEL = 256
        EXPERT_DIM = 512
        NUM_EXPERTS = 8
        TOP_K = 2
        SEQ_LEN = 64
        BATCH = 2
        x_flat = x.reshape(-1, D_MODEL)
        gate_logits = x_flat @ Wg + bg + bias
        topk_vals, topk_idx = jax.lax.top_k(gate_logits, TOP_K)
        topk_w = jax.nn.softmax(topk_vals, axis=-1)
        combine = (jax.nn.one_hot(topk_idx, NUM_EXPERTS, dtype=x.dtype) * topk_w[..., None]).sum(axis=1)
        h = jax.nn.relu(jnp.einsum('td,edh->teh', x_flat, W1) + b1)
        y = jnp.einsum('teh,ehd->ted', h, W2) + b2
        out = jnp.einsum('ted,te->td', y, combine)
        return out.reshape(x.shape)
    edge_index = jnp.stack([src, dst])
    x = x + _L0_gnn_ref(_layernorm(x, axis=-1), edge_index, edge_attr_4, L0_gnn_mlp_w, L0_gnn_mlp_b, L0_gnn_ew1, L0_gnn_ew2, L0_gnn_bn_g, L0_gnn_bn_b)
    x = x + _L0_ffn_ref(_layernorm(x, axis=-1)[None], L0_ffn_Wg, L0_ffn_bg, L0_ffn_bias, L0_ffn_W1, L0_ffn_b1, L0_ffn_W2, L0_ffn_b2)[0]
    return x

_drawn_inputs = setup_inputs


def setup_inputs(seed=0):
    import zlib

    import numpy as np

    out = dict(_drawn_inputs(seed))
    spreads = {'L0_gnn_mlp_b': (0.0, 0.1),
     'L0_gnn_bn_g': (1.0, 0.2),
     'L0_gnn_bn_b': (0.0, 0.1),
     'L0_ffn_bias': (0.0, 0.1)}
    factors = {'L0_ffn_bg': 5.982, 'L0_ffn_b1': 8.0, 'L0_ffn_b2': 5.686}
    for name, (base, spread) in spreads.items():
        noise = np.random.default_rng([zlib.crc32(name.encode()), seed]).standard_normal(out[name].shape)
        drawn = base * np.exp(spread * noise) if base else spread * noise
        out[name] = jnp.asarray(drawn.astype(out[name].dtype))
    for name, factor in factors.items():
        out[name] = (out[name] * factor).astype(out[name].dtype)
    return out
```

```python
import concourse.bass as bass
from concourse import mybir
from contextlib import ExitStack

F32 = mybir.dt.float32
I32 = mybir.dt.int32
U32 = mybir.dt.uint32
I16 = mybir.dt.int16
U8 = mybir.dt.uint8
BF16 = mybir.dt.bfloat16
F16 = mybir.dt.float16
F8 = mybir.dt.float8e4
SIZE = {F32: 4, I32: 4, U32: 4, I16: 2, U8: 1, BF16: 2, F16: 2, F8: 1}
ALU = mybir.AluOpType
ACT = mybir.ActivationFunctionType
XYZ = mybir.AxisListType.X

N = 3125
D = 256
E = 53125
L = 5
P = 125
NT = N // P
H = D // 128
CH = 128
NCH = 416
NB = 4
CB = NCH // NB
U = 4
MIN_TURNS = 3
MAX_FIRST = NCH - U * MIN_TURNS
MAX_TURNS = NCH // U
NCHP = NCH + U
DST_PAD = 3500
FIELDS = 3
GROUPS = (NT + FIELDS - 1) // FIELDS
GW = GROUPS * P
GB = 3
GC = GW // GB
KEY = 3584
MAGIC = 12582912.0
BIG = 1000.0
CQ = 500
COLS = [(q, min(CQ, N - q)) for q in range(0, N, CQ)]
NQ = len(COLS)
LN_EPS = 1e-5
BN_EPS = 1e-5
H0_EXP = 11
LB = 26
NLB = NCH // LB
LG = 13
NE = 8
F = 512
FK = F // 128
TT = 128
J = (2 * N + NE * (TT - 1)) // TT
assert J % 2 == 0
GS = 4


def gnn_ffn_program(nc, x, src, dst, edge_attr, mlp_w, mlp_b, ew1, ew2, bn_g, bn_b,
                    wg, bg, gbias, w1, b1, w2, b2, out, stop=None):
    ctx = ExitStack()
    with ctx:
        base = (nc.sbuf_base + 31) // 32 * 32

        class Region:
            def __init__(self, start):
                self.at = start

            def __call__(self, name, shape, dt):
                n = SIZE[dt]
                for s in shape[1:]:
                    n *= s
                t = nc.alloc_sbuf_tensor_at(name, shape, dt, offset=base + self.at)
                self.at = (self.at + n + 31) // 32 * 32
                assert base + self.at <= nc.sbuf_usable_end, name
                return t

        def sem(name):
            return ctx.enter_context(nc.semaphore(name))

        bank = [ctx.enter_context(nc.psum_tensor(f"bank{i}", [128, 512], F32)) for i in range(8)]

        keep = Region(0)
        at = keep("at", [P, NT, N], F8)
        hT_at = keep.at
        hT = keep("hT", [128, H, N], F32)
        dinvB = keep("dinvB", [128, N], F32)
        s4T = keep("s4T", [4, N], F32)
        ident = keep("ident", [128, 128], F32)
        ones = keep("ones", [128, 128], F32)
        ones16 = keep("ones16", [P, 128], BF16)
        dinvP = keep("dinvP", [P, NT], F32)
        zt_at = keep.at
        keep.at += 4 * 1024
        xstart = keep.at

        r = Region(xstart)
        dstE = r("dstE", [128, NCHP], F32)
        keyE = r("keyE", [128, NCHP], F32)
        powE = r("powE", [128, NCHP], I32)
        sl16 = r("sl16", [128, NCHP], I16)
        s16 = r("s16", [128, NCH], I16)
        eaE = r("eaE", [128, NCH, 4], F32)
        iotaK = r("iotaK", [128, GW + 1], I16)
        iotaS = r("iotaS", [128, 128, 2], I16)
        iotaD = r("iotaD", [128, P + 1], I16)
        iota25 = r("iota25", [128, NT], I16)
        iotaP = r("iotaP", [128, 1], F32)
        rng = r("rng", [1, 2 * NT], I32)
        common = r.at
        dstI = r("dstI", [CB, NB, CH], I32)
        srcI = r("srcI", [CB, NB, CH], I32)
        eaC = r("eaC", [CB, NB, CH * 4], F32)
        dstC = r("dstC", [CB, NB, CH], F32)
        srcC = r("srcC", [CB, NB, CH], F32)
        slC = r("slC", [CB, NB, CH], I16)
        ta = r("ta", [128, NB * CH], F32)
        tb = r("tb", [128, NB * CH], F32)
        tg = r("tg", [128, NCH], F32)
        cmm = r("cmm", [CB, 2, NB], F32)
        cmmB = r("cmmB", [CB, 2 * NB, NT], F32)
        cidx = r("cidx", [NT, NCH], F32)
        tlo = r("tlo", [NT, 1], F32)
        m1 = r("m1", [NT, NCH], F32)
        m2 = r("m2", [NT, NCH], F32)
        lohi = r("lohi", [NT, 2], F32)
        lohi2 = r("lohi2", [NT, 2], F32)
        xr = r
        xin = xr("xin", [P, NT, D], F32)
        xst = xr("xst", [P, NT, 6], F32)
        xmv = xr("xmv", [P, NT, 2], F32)
        xrs = xr("xrs", [P, NT], F32)
        xve = xr("xve", [P, NT], F32)
        xsd = xr("xsd", [P, NT], F32)
        xt1 = xr("xt1", [P, NT], F32)

        r = Region(common)
        cnt1 = r("cnt1", [128, U, GW + 1], BF16)
        ohS = r("ohS", [128, U // 2, 128, 2], BF16)
        encI = r("encI", [P, 2, GW], I32)
        orI = r("orI", [P, GW], I32)
        deg = r("deg", [P, NT], F32)
        deg1 = r("deg1", [P, NT], F32)
        dsd = r("dsd", [P, NT], F32)
        dt1 = r("dt1", [P, NT], F32)
        ddg = r("ddg", [P, 2, P], F32)

        r = Region(common)
        w12 = r("w12", [128, NCHP, 12], BF16)
        slrow = r("slrow", [P, 2, LB * CH], I16)
        ohT = r("ohT", [P, 2, LB * CH], BF16)
        dpart = r("dpart", [P, 3, NT], BF16)
        drem = r("drem", [P, 2, NT], F32)
        ohs = r("ohs", [128, 2, LB, NT], BF16)
        lkt = r("lkt", [128, 2, LG * NT], F32)
        dsrc = r("dsrc", [128, NCH], F32)
        v4 = r("v4", [128, NCH, 4], F32)
        v4b = r("v4b", [128, NCH, 4], F32)
        ohD = r("ohD", [128, U, P + 1], BF16)
        s4s = r("s4s", [P, NT, 4], F32)
        s4P = r("s4P", [P, NT, 4], F32)

        r = Region(xstart)
        aggT = r("aggT", [128, H, N], F32)
        wcur = r("wcur", [128, 2 * H, D], F32)
        wraw = r("wraw", [128, 2 * H, D], F32)
        ewT = r("ewT", [128, H, 4], F32)
        ewm = r("ewm", [4, D], F32)
        prm = r("prm", [128, 3, H], F32)
        zst = r("zst", [128, H, NQ, 6], F32)
        zmv = r("zmv", [128, H, 2], F32)
        cf = r("cf", [128, 6, H], F32)
        cfi = r("cfi", [128, 2, H], I32)
        inv = r("inv", [128, H], F32)
        m_at = r.at
        m = r("m", [P, NT, 2, D], F16)

        r = Region(0)
        x2 = r("x2", [P, NT, D], F32)
        xn = r("xn", [P, NT, D], F32)
        b1B = r("b1B", [128, NE, F], F32)
        b2B = r("b2B", [128, NE, D], F32)
        r = Region(hT_at)
        w2s = r("w2s", [128, NE, FK, D], F32)
        fst = r("fst", [P, NT, 6], F32)
        fmv = r("fmv", [P, NT, 2], F32)
        fve = r("fve", [P, NT], F32)
        fsd = r("fsd", [P, NT], F32)
        frs = r("frs", [P, NT], F32)
        ft1 = r("ft1", [P, NT], F32)
        lgt = r("lgt", [P, NT, NE], F32)
        top = r("top", [P, NT, 8], F32)
        tix = r("tix", [P, NT, 8], U32)
        ef = r("ef", [P, 2, NT], F32)
        oh1 = r("oh1", [P, NT, NE], F32)
        oh2 = r("oh2", [P, NT, NE], F32)
        msk = r("msk", [P, NT, NE], F32)
        cnt = r("cnt", [P, NT, NE], F32)
        incl = r("incl", [P, NT, NE], F32)
        slm = r("slm", [P, NT, NE], F32)
        nte = r("nte", [P, 4, NE], F32)
        slf = r("slf", [P, 2, NT], F32)
        sli = r("sli", [P, 2, NT], I32)
        wts = r("wts", [P, 3, NT], F32)
        cmpJ = r("cmpJ", [1, J, NE], F32)
        teF = r("teF", [1, J], F32)
        te = r("te", [1, J], I32)
        assert r.at <= zt_at - 1600
        r = Region(m_at)
        w1s = r("w1s", [128, NE, H, F], F32)
        xtb = r("xtb", [TT, 2, D], F32)
        xtT = r("xtT", [128, 2, H, TT], F32)
        h1 = r("h1", [TT, 2, F], F32)
        r = Region(xstart)
        h1T = r("h1T", [128, 2, FK, TT], F32)
        ytb = r("ytb", [TT, 2, D], F32)
        gat = r("gat", [P, GS, 2, D], F32)
        otb = r("otb", [P, GS, D], F32)
        xnT = r("xnT", [128, 2, H, P], F32)
        assert r.at <= xstart + 25000
        r = Region(zt_at)
        zt = r("zt", [128, 2 * D], F32)
        wgs = r("wgs", [128, H, NE], F32)
        gbr = r("gbr", [1, 2, NE], F32)
        gbs = r("gbs", [1, NE], F32)
        tri = r("tri", [P, P], F32)
        iota8 = r("iota8", [P, NE], F32)
        iotaJ = r("iotaJ", [1, J], F32)
        assert r.at <= xstart

        xs = nc.dram_tensor("xs", (J * TT, D), F32, kind="Internal").ap()
        ys = nc.dram_tensor("ys", (J * TT, D), F32, kind="Internal").ap()
        sl_dram = nc.dram_tensor("sl_dram", (NCH * CH,), I16, kind="Internal").ap()

        s_mem = sem("s_mem")
        s_src = sem("s_src")
        s_dst = sem("s_dst")
        s_ea = sem("s_ea")
        s_tail = sem("s_tail")
        s_x = sem("s_x")
        s_edges = sem("s_edges")
        s_cmm = sem("s_cmm")
        s_tp = sem("s_tp")
        s_tpx = sem("s_tpx")
        s_minmax = sem("s_minmax")
        s_lohi = sem("s_lohi")
        s_rngp = sem("s_rngp")
        s_rng = sem("s_rng")
        s_prep = sem("s_prep")
        s_slC = sem("s_slC")
        s_sld = sem("s_sld")
        s_dv = sem("s_dv")
        s_po = sem("s_po")
        s_var = sem("s_var")
        s_std = sem("s_std")
        s_xn = sem("s_xn")
        s_xT = sem("s_xT")
        s_xTe = sem("s_xTe")
        s_oh = sem("s_oh")
        s_free = sem("s_free")
        s_cnt = sem("s_cnt")
        s_enc = sem("s_enc")
        s_or = sem("s_or")
        s_at = sem("s_at")
        s_deg = sem("s_deg")
        s_dg = sem("s_dg")
        s_bc = sem("s_bc")
        s_dB = sem("s_dB")
        s_dpart = sem("s_dpart")
        s_slr = [sem(f"s_slr{i}") for i in range(2)]
        s_ohT = sem("s_ohT")
        s_lk = sem("s_lk")
        s_lke = sem("s_lke")
        s_w12 = sem("s_w12")
        s_ohD = sem("s_ohD")
        s_freeD = sem("s_freeD")
        s_s4 = sem("s_s4")
        s_s4e = sem("s_s4e")
        s_s4T = sem("s_s4T")
        s_s4Te = sem("s_s4Te")
        s_w = sem("s_w")
        s_wfree = sem("s_wfree")
        s_wc = sem("s_wc")
        s_ewp = sem("s_ewp")
        s_ewm = sem("s_ewm")
        s_tr = sem("s_tr")
        s_hi = sem("s_hi")
        s_lo = sem("s_lo")
        s_agg = sem("s_agg")
        s_agge = sem("s_agge")
        s_mlp = sem("s_mlp")
        s_z = sem("s_z")
        s_bv = sem("s_bv")
        s_bs = sem("s_bs")
        s_bn = sem("s_bn")
        s_h = sem("s_h")
        s_ls = sem("s_ls")
        s_ez = sem("s_ez")
        s_apart = sem("s_apart")
        s_cst = sem("s_cst")
        s_zero = sem("s_zero")
        s_x2 = sem("s_x2")
        s_fw = sem("s_fw")
        s_w1 = sem("s_w1")
        s_w2 = sem("s_w2")
        s_oT = sem("s_oT")
        s_oTe = sem("s_oTe")
        s_fve = sem("s_fve")
        s_fsd = sem("s_fsd")
        s_fn = sem("s_fn")
        s_gT = sem("s_gT")
        s_gTe = sem("s_gTe")
        s_gate = sem("s_gate")
        s_gbs = sem("s_gbs")
        s_msk = sem("s_msk")
        s_rank = sem("s_rank")
        s_ex = sem("s_ex")
        s_exd = sem("s_exd")
        s_slot = sem("s_slot")
        s_sc = sem("s_sc")
        s_xt = [sem(f"s_xt{i}") for i in range(2)]
        s_xtT = sem("s_xtT")
        s_xtc = sem("s_xtc")
        s_h1 = sem("s_h1")
        s_h1b = sem("s_h1b")
        s_hT = sem("s_hT")
        s_hTc = sem("s_hTc")
        s_y = sem("s_y")
        s_yb = sem("s_yb")
        s_yst = [sem(f"s_yst{i}") for i in range(2)]
        s_ga = [sem(f"s_ga{i}") for i in range(GS)]
        s_o1 = sem("s_o1")
        s_o2 = sem("s_o2")
        s_out = [sem(f"s_out{i}") for i in range(GS)]
        s_dbg = sem("s_dbg")

        if stop == "layers":
            dbg_h = nc.dram_tensor("dbg_h", (128, H, N), F32, kind="ExternalOutput").ap()
        if stop == "build":
            dbg_at = nc.dram_tensor("dbg_at", (P, NT, N), F8, kind="ExternalOutput").ap()
            dbg_d = nc.dram_tensor("dbg_d", (128, N), F32, kind="ExternalOutput").ap()
            dbg_p = nc.dram_tensor("dbg_p", (P, NT), F32, kind="ExternalOutput").ap()
            dbg_s = nc.dram_tensor("dbg_s", (4, N), F32, kind="ExternalOutput").ap()
            dbg_h = nc.dram_tensor("dbg_h", (128, H, N), F32, kind="ExternalOutput").ap()

        block = ctx.enter_context(nc.Block())

        def tail_dmas(sp, tile, dram, width, s):
            full = (NB - 1) * CB * CH
            last = (CB - 1) * CH
            sp.dma_start(tile[:, 0:NB - 1, :], dram[0:full * width].rearrange("(b p e) -> p b e", b=NB - 1, p=CB)).then_inc(s, 16)
            sp.wait_ge(s_mem, 1)
            sp.dma_start(tile[0:CB - 1, NB - 1, :], dram[full * width:(full + last) * width].rearrange("(p e) -> p e", p=CB - 1)).then_inc(s, 16)
            rest = E - full - last
            sp.dma_start(tile[CB - 1:CB, NB - 1, 0:rest * width], dram[(full + last) * width:E * width].rearrange("(p e) -> p e", p=1)).then_inc(s, 16)

        def s4_out(dve, t):
            dve.wait_ge(s_s4, t + 1)
            dve.tensor_reduce(s4s[:, t, :], bank[3 + t % 2][0:P, 0:12].rearrange("p (k j) -> p j k", j=4), axis=XYZ, op=ALU.add).then_inc(s_s4e, 1)
            dve.wait_ge(s_s4e, 2 * t + 1)
            dve.tensor_scalar(s4P[:, t, :], s4s[:, t, :], dinvP[:, t:t + 1], None, ALU.mult).then_inc(s_s4e, 1)

        def chunk_of(first, i):
            return nc.s_assert_within(first + U * i, 0, NCH - 1, skip_runtime_bounds_check_because="a tile's turns start before its last chunk")



        def load_layer(sp, l):
            row = lambda a: a[bass.ds(l, 1), :]
            sp.dma_start(wraw[:, :, :], mlp_w[bass.ds(l, 1), :, :].rearrange("a (k p) c -> p (a k) c", p=128)).then_inc(s_w, 16)
            with nc.allow_non_contiguous_dma(reason="a few values for each channel"):
                for n, a in enumerate((mlp_b, bn_g, bn_b)):
                    sp.dma_start(prm[:, n, :], row(a).rearrange("a (h p) -> p (a h)", p=128)).then_inc(s_w, 16)
                sp.dma_start(ewT[:, 0, 3:4], ew1[bass.ds(l, 1), :, :].rearrange("a j c -> c (a j)")).then_inc(s_w, 16)
                sp.dma_start(ewT[:, 1, 0:3], ew2[bass.ds(l, 1), :, :].rearrange("a j c -> c (a j)")).then_inc(s_w, 16)

        LOADS = 6

        def m_rows_dve(dve, base):
            for t in range(NT):
                dve.wait_ge(s_hi, base(NT) + t + 1)
                dve.scalar_tensor_tensor(m[:, t, 1, :], bank[t % 4][0:P, 0:D], dinvP[:, t:t + 1], m[:, t, 0, :],
                                         ALU.mult, ALU.subtract).then_inc(s_lo, 1)

        def m_rows_act(act, base, chunk=None):
            for t in range(NT):
                if chunk and t % (CQ // P) == 0:
                    chunk(t // (CQ // P))
                act.wait_ge(s_tr, base(NT) + t + 1)
                act.activation(m[:, t, 0, :], bank[t % 4][0:P, 0:D], ACT.Copy, scale=dinvP[:, t:t + 1]).then_inc(s_hi, 1)

        def m_rows_pe(pe, base, ready):
            for t in range(NT):
                ready(t)
                if t >= 4:
                    pe.wait_ge(s_lo, base(NT) + t - 3)
                for h in range(H):
                    last = pe.transpose(bank[t % 4][0:P, h * 128:(h + 1) * 128], hT[:, h, t * P:(t + 1) * P], ident[:, :])
                last.then_inc(s_tr, 1)

        def layer_pe(pe, base):
            pe.wait_ge(s_wc, base(1) + 1)
            for h in range(H):
                last = pe.matmul(bank[7][0:4, 0:D], ewT[:, h, :], wraw[:, H + h, :], start=h == 0, stop=h == H - 1)
            last.then_inc(s_ewp, 1)
            pe.wait_ge(s_lo, base(NT) + NT)
            for q, (a, w) in enumerate(COLS):
                for h in range(H):
                    g = H * q + h
                    if g >= 4:
                        pe.wait_ge(s_agge, base(H * NQ) + g - 3)
                    pe.sem_inc(s_apart, 1)
                    for s in range(NT):
                        for k in range(2):
                            last = pe.matmul(bank[g % 4][:, 0:w], m[:, s, k, h * 128:(h + 1) * 128], at[:, s, a:a + w],
                                             start=s == 0 and k == 0, stop=s == NT - 1 and k == 1)
                    last.then_inc(s_agg, 1)
            pe.wait_ge(s_ewm, base(1) + 1)
            for q, (a, w) in enumerate(COLS):
                pe.wait_ge(s_agge, base(H * NQ) + H * (q + 1))
                if q >= 2:
                    pe.wait_ge(s_z, base(NQ) + q - 1)
                for h in range(H):
                    o = bank[4 + 2 * (q % 2) + h][:, 0:w]
                    for k in range(2 * H):
                        rhs = (hT if k < H else aggT)[:, k % H, a:a + w]
                        pe.matmul(o, wcur[:, k, h * 128:(h + 1) * 128], rhs, start=k == 0, stop=False)
                    last = pe.matmul(o, ewm[:, h * 128:(h + 1) * 128], s4T[:, a:a + w], start=False, stop=True)
                last.then_inc(s_mlp, 1)

        def layer_dve(dve, base, loads, last_layer):
            count = [0]

            def step(ins):
                count[0] += 1
                ins.then_inc(s_ls, 1)
                dve.wait_ge(s_ls, base(LAYER_STEPS) + count[0])

            dve.wait_ge(s_w, 16 * loads)
            for k in range(2 * H):
                last = dve.tensor_scalar(wcur[:, k, :], wraw[:, k, :], inv[:, k % H:k % H + 1], None, ALU.mult)
            last.then_inc(s_wc, 1)
            dve.wait_ge(s_ewp, base(1) + 1)
            dve.tensor_copy(ewm[:, :], bank[7][0:4, 0:D]).then_inc(s_ewm, 1)
            for q, (a, w) in enumerate(COLS):
                for h in range(H):
                    g = H * q + h
                    dve.wait_ge(s_agg, base(H * NQ) + g + 1)
                    dve.tensor_tensor(aggT[:, h, a:a + w], bank[g % 4][:, 0:w], dinvB[:, a:a + w], ALU.mult).then_inc(s_agge, 1)
            for q, (a, w) in enumerate(COLS):
                dve.wait_ge(s_z, base(NQ) + q + 1)
                for h in range(H):
                    last = dve.bn_stats(zst[:, h, q, :], hT[:, h, a:a + w])
            step(last)
            dve.sem_inc(s_apart, 1)
            for h in range(H):
                last = dve.bn_aggr(zmv[:, h, :], zst[:, h, :, :].rearrange("p q s -> p (q s)"))
            step(last)
            gain, offset = prm[:, 1, :], prm[:, 2, :]
            ve, sd, rt, tmp = (cf[:, n, :] for n in (0, 1, 2, 3))
            dve.tensor_scalar(ve, zmv[:, :, 1], BN_EPS, None, ALU.add).then_inc(s_bv, 1)
            dve.wait_ge(s_bs, base(1) + 1)
            step(dve.reciprocal(rt, sd))
            step(dve.tensor_tensor(tmp, rt, rt, ALU.mult))
            step(dve.tensor_tensor(tmp, tmp, ve, ALU.mult))
            step(dve.tensor_scalar(tmp, tmp, -0.5, 1.5, ALU.mult, ALU.add))
            step(dve.tensor_tensor(rt, rt, tmp, ALU.mult))
            slope, shift = cf[:, 4, :], cf[:, 5, :]
            step(dve.tensor_tensor(slope, rt, gain, ALU.mult))
            step(dve.tensor_tensor(tmp, zmv[:, :, 0], slope, ALU.mult))
            step(dve.tensor_tensor(shift, offset, tmp, ALU.subtract))
            if not last_layer:
                step(dve.scalar_tensor_tensor(tmp, gain, -1.0, gain, ALU.mult, ALU.max))
                step(dve.scalar_tensor_tensor(sd, offset, -1.0, offset, ALU.mult, ALU.max))
                step(dve.scalar_tensor_tensor(tmp, tmp, 56.0, sd, ALU.mult, ALU.add))
                step(dve.tensor_scalar(tmp, tmp, 2.0 ** -80, 2.0 ** 100, ALU.max, ALU.min))
                step(dve.tensor_scalar(cfi[:, 0, :], tmp.bitcast(I32), 0x7F800000, None, ALU.bitwise_and))
                step(dve.tensor_scalar(cfi[:, 1, :], cfi[:, 0, :], -1.0, float((254 + 14) << 23), ALU.mult, ALU.add))
                step(dve.tensor_scalar(inv[:, :].bitcast(I32), cfi[:, 0, :], float(-(14 << 23)), None, ALU.add))
                step(dve.tensor_tensor(slope, slope, cfi[:, 1, :].bitcast(F32), ALU.mult))
                step(dve.tensor_tensor(shift, shift, cfi[:, 1, :].bitcast(F32), ALU.mult))
                assert count[0] == LAYER_STEPS, count
            dve.sem_inc(s_bn, 1)
            if not last_layer:
                m_rows_dve(dve, lambda n: base(n) + n)

        def layer_act(act, base, last_layer):
            for q, (a, w) in enumerate(COLS):
                act.wait_ge(s_mlp, base(NQ) + q + 1)
                for h in range(H):
                    last = act.activation(hT[:, h, a:a + w], bank[4 + 2 * (q % 2) + h][:, 0:w], ACT.Relu, bias=prm[:, 0, h:h + 1])
                last.then_inc(s_z, 1)
            act.wait_ge(s_bv, base(1) + 1)
            act.activation(cf[:, 1, :], cf[:, 0, :], ACT.Sqrt).then_inc(s_bs, 1)
            act.wait_ge(s_bn, base(1) + 1)

            def normalise(q):
                a, w = COLS[q]
                for h in range(H):
                    last = act.activation(hT[:, h, a:a + w], hT[:, h, a:a + w], ACT.Identity if last_layer else ACT.Relu,
                                          bias=cf[:, 5, h:h + 1], scale=cf[:, 4, h:h + 1])
                last.then_inc(s_h, 1)

            if last_layer:
                for q in range(NQ):
                    normalise(q)
            else:
                m_rows_act(act, lambda n: base(n) + n, normalise)

        LAYER_STEPS = 19



        def experts_sp(sp):
            sp.wait_ge(s_agg, L * H * NQ)
            sp.dma_start(x2[:, :, :], x.rearrange("(t p) d -> p t d", p=P)).then_inc(s_x2, 16)
            sp.dma_start(b1B[:, :, :], b1.rearrange("(a e) f -> a e f", a=1).to_broadcast([128, NE, F])).then_inc(s_fw, 16)
            sp.dma_start(b2B[:, :, :], b2.rearrange("(a e) f -> a e f", a=1).to_broadcast([128, NE, D])).then_inc(s_fw, 16)
            sp.wait_ge(s_h, L * NQ)
            sp.dma_start(w1s[:, :, :, :].rearrange("p e k f -> p (e k) f"), w1.rearrange("e (k p) f -> p (e k) f", p=128)).then_inc(s_w1, 16)
            sp.wait_ge(s_oT, NT)
            sp.dma_start(w2s[:, :, :, :].rearrange("p e k d -> p (e k) d"), w2.rearrange("e (k p) d -> p (e k) d", p=128)).then_inc(s_w2, 16)
            sp.wait_ge(s_sc, 16 * 2 * NT)
            xst_ = xs.rearrange("(j p) d -> p j d", p=TT)
            yst_ = ys.rearrange("(j p) d -> p j d", p=TT)
            for u in range(2):
                sp.dma_start(xtb[:, u, :], xst_[:, u, :]).then_inc(s_xt[u], 16)

            def store(j, u):
                sp.wait_ge(s_yb, j + 1)
                sp.dma_start(yst_[:, bass.ds(j, 1), :].rearrange("p a d -> p (a d)"), ytb[:, u, :]).then_inc(s_yst[u], 16)

            with sp.Fori(0, J // 2 - 1) as i:
                for u in range(2):
                    j = sp.snap(2 * i + u)
                    sp.wait_ge(s_xtT, j + 1)
                    sp.dma_start(xtb[:, u, :], xst_[:, bass.ds(j + 2, 1), :].rearrange("p a d -> p (a d)")).then_inc(s_xt[u], 16)
                    store(j, u)
            for u in range(2):
                store(J - 2 + u, u)
            for t in range(NT):
                sp.wait_ge(s_o2, t + 1)
                sp.dma_start(out[t * P:(t + 1) * P, :], otb[:, t % GS, :]).then_inc(s_out[t % GS], 16)
            for g in range(GS):
                sp.wait_ge(s_out[g], 16 * ((NT - g + GS - 1) // GS))

        def experts_pool(pool):
            pool.wait_ge(s_zero, 16 * (J // 4))
            pool.wait_ge(s_slot, 1)
            for t in range(NT):
                for n in range(2):
                    pool.indirect_dma_start(xs[:, :], bass.IndirectOffsetOnAxis(ap=sli[:, n, t:t + 1], axis=0), xn[:, t, :], None).then_inc(s_sc, 16)
            for u in range(2):
                pool.wait_ge(s_yst[u], 16 * (J // 2))
            for t in range(NT):
                if t >= GS:
                    pool.wait_ge(s_o2, t - GS + 1)
                for n in range(2):
                    pool.indirect_dma_start(gat[:, t % GS, n, :], None, ys[:, :], bass.IndirectOffsetOnAxis(ap=sli[:, n, t:t + 1], axis=0)).then_inc(s_ga[t % GS], 16)

        def experts_act(act):
            act.wait_ge(s_fve, 1)
            act.activation(fsd[:, :], fve[:, :], ACT.Sqrt).then_inc(s_fsd, 1)
            for t in range(NT):
                act.wait_ge(s_gT, t + 1)
                act.activation(xnT[:, t % 2, :, :], bank[4 + t % 2][:, 0:H * P].rearrange("p (h n) -> p h n", h=H), ACT.Copy).then_inc(s_gTe, 1)
            act.wait_ge(s_ex, 1)
            act.activation(wts[:, 1, :], wts[:, 0, :], ACT.Exp).then_inc(s_exd, 1)

            def rows(j, u):
                act.wait_ge(s_xtT, j + 1)
                act.activation(xtT[:, u, :, :], bank[u][:, 0:H * TT].rearrange("p (h n) -> p h n", h=H), ACT.Copy).then_inc(s_xtc, 1)

            def hidden(j, u):
                act.wait_ge(s_hT, j + 1)
                act.activation(h1T[:, u, :, :], bank[4 + u][:, 0:FK * TT].rearrange("p (h n) -> p h n", h=FK), ACT.Relu).then_inc(s_hTc, 1)

            rows(0, 0)
            with act.Fori(0, J // 2 - 1) as i:
                for u in range(2):
                    j = act.snap(2 * i + u)
                    rows(j + 1, 1 - u)
                    hidden(j, u)
            rows(J - 1, 1)
            hidden(J - 2, 0)
            hidden(J - 1, 1)

        def experts_dve(dve, step, rounded, inverse_root):
            dve.wait_ge(s_x2, 16)
            for t in range(NT):
                dve.wait_ge(s_oT, t + 1)
                dve.tensor_tensor(x2[:, t, :], x2[:, t, :], bank[t % 4][0:P, 0:D], ALU.add).then_inc(s_oTe, 1)
                if t:
                    dve.wait_ge(s_oTe, t)
                    dve.bn_stats(fst[:, t - 1, :], x2[:, t - 1, :])
            dve.wait_ge(s_oTe, NT)
            step(dve.bn_stats(fst[:, NT - 1, :], x2[:, NT - 1, :]))
            for t in range(NT):
                last = dve.bn_aggr(fmv[:, t, :], fst[:, t, :])
            step(last)
            dve.tensor_scalar(fve[:, :], fmv[:, :, 1], LN_EPS, None, ALU.add).then_inc(s_fve, 1)
            dve.wait_ge(s_fsd, 1)
            inverse_root(frs[:, :], fve[:, :], fsd[:, :], ft1[:, :])
            dve.wait_ge(s_fw, 16 * 5)
            dve.tensor_tensor(gbs[:, :], gbr[:, 0, :], gbr[:, 1, :], ALU.add).then_inc(s_gbs, 1)
            for t in range(NT):
                dve.tensor_scalar(xn[:, t, :], x2[:, t, :], fmv[:, t, 0:1], frs[:, t:t + 1], ALU.subtract, ALU.mult).then_inc(s_fn, 1)
            dve.wait_ge(s_cst, 2)
            dve.wait_ge(s_gate, 1)
            step(dve.tensor_copy(lgt[:, :, :].rearrange("p t e -> p (t e)"), bank[6][0:P, 0:NT * NE]))
            for t in range(NT):
                last = dve.max(top[:, t, :], lgt[:, t, :])
            step(last)
            for t in range(NT):
                last = dve.max_index(tix[:, t, :], top[:, t, :], lgt[:, t, :])
            step(last)
            dve.tensor_tensor(wts[:, 0, :], top[:, :, 1], top[:, :, 0], ALU.subtract).then_inc(s_ex, 1)
            step(dve.tensor_copy(ef[:, 0, :], tix[:, :, 0]))
            step(dve.tensor_copy(ef[:, 1, :], tix[:, :, 1]))
            by8 = iota8[:, :].unsqueeze(1).to_broadcast([P, NT, NE])
            for n, o in enumerate((oh1, oh2)):
                step(dve.tensor_tensor(o[:, :, :], ef[:, n, :].unsqueeze(2).to_broadcast([P, NT, NE]), by8, ALU.is_equal))
            dve.tensor_tensor(msk[:, :, :], oh1[:, :, :], oh2[:, :, :], ALU.add).then_inc(s_msk, 1)
            dve.wait_ge(s_exd, 1)
            step(dve.tensor_scalar(wts[:, 0, :], wts[:, 1, :], 1.0, None, ALU.add))
            step(dve.reciprocal(wts[:, 2, :], wts[:, 0, :]))
            step(dve.tensor_tensor(wts[:, 1, :], wts[:, 1, :], wts[:, 2, :], ALU.mult))
            dve.wait_ge(s_rank, 1)
            step(dve.tensor_copy(cnt[:, :, :].rearrange("p t e -> p (t e)"), bank[1][0:P, 0:NT * NE]))
            for e in range(NE):
                last = dve.tensor_tensor_scan(incl[:, :, e], ones[0:P, 0:NT], cnt[:, :, e], 0.0, ALU.mult, ALU.add)
            step(last)
            total, tiles, end, spare = (nte[:, n, :] for n in range(4))
            step(dve.tensor_scalar(total, incl[:, NT - 1, :], 1.0 / TT, (TT - 1) / (2 * TT), ALU.mult, ALU.add))
            rounded(tiles, total, spare)
            step(dve.tensor_tensor_scan(end, ones[0:P, 0:NE], tiles, 0.0, ALU.mult, ALU.add))
            step(dve.tensor_tensor(spare, end, tiles, ALU.subtract))
            step(dve.tensor_scalar(spare, spare, float(TT), None, ALU.mult))
            step(dve.tensor_tensor(slm[:, :, :], incl[:, :, :], cnt[:, :, :], ALU.subtract))
            step(dve.tensor_tensor(slm[:, :, :].rearrange("p t e -> p (t e)"), slm[:, :, :].rearrange("p t e -> p (t e)"), bank[0][0:P, 0:NT * NE], ALU.add))
            step(dve.tensor_tensor(slm[:, :, :], slm[:, :, :], spare.unsqueeze(1).to_broadcast([P, NT, NE]), ALU.add))
            for n, o in enumerate((oh1, oh2)):
                step(dve.tensor_tensor(o[:, :, :], o[:, :, :], slm[:, :, :], ALU.mult))
                step(dve.tensor_reduce(slf[:, n, :], o[:, :, :], axis=XYZ, op=ALU.add))
            step(dve.tensor_copy(sli[:, :, :], slf[:, :, :]))
            step(dve.tensor_tensor(cmpJ[:, :, :], nte[0:1, 2, :].unsqueeze(1).to_broadcast([1, J, NE]),
                                   iotaJ[:, :].unsqueeze(2).to_broadcast([1, J, NE]), ALU.is_le))
            step(dve.tensor_reduce(teF[:, :], cmpJ[:, :, :], axis=XYZ, op=ALU.add))
            dve.tensor_scalar(te[:, :], teF[:, :], float(NE - 1), None, ALU.min).then_inc(s_slot, 1)
            dve.wait_ge(s_slot, 1)

            def hidden(j, u):
                e = dve.value_load(te[0:1, bass.ds(j, 1)], min_val=0, max_val=NE - 1)
                dve.wait_ge(s_h1, j + 1)
                dve.tensor_tensor(h1[:, u, :], bank[2 + u][:, :], b1B[:, bass.ds(e, 1), :].rearrange("p a f -> p (a f)"), ALU.add).then_inc(s_h1b, 1)

            def result(j, u, stores):
                e = dve.value_load(te[0:1, bass.ds(j, 1)], min_val=0, max_val=NE - 1)
                dve.wait_ge(s_y, j + 1)
                if stores is not None:
                    dve.wait_ge(s_yst[u], stores)
                dve.tensor_tensor(ytb[:, u, :], bank[6 + u][:, 0:D], b2B[:, bass.ds(e, 1), :].rearrange("p a f -> p (a f)"), ALU.add).then_inc(s_yb, 1)

            hidden(0, 0)
            hidden(1, 1)
            result(0, 0, None)
            hidden(2, 0)
            result(1, 1, None)
            with dve.Fori(1, J // 2 - 1) as i:
                hidden(2 * i + 1, 1)
                result(2 * i, 0, 16 * i)
                hidden(2 * i + 2, 0)
                result(2 * i + 1, 1, 16 * i)
            hidden(J - 1, 1)
            result(J - 2, 0, 16 * (J // 2 - 1))
            result(J - 1, 1, 16 * (J // 2 - 1))
            for t in range(NT):
                dve.wait_ge(s_ga[t % GS], 32 * (t // GS + 1))
                dve.scalar_tensor_tensor(x2[:, t, :], gat[:, t % GS, 0, :], wts[:, 2, t:t + 1], x2[:, t, :], ALU.mult, ALU.add).then_inc(s_o1, 1)
                dve.wait_ge(s_o1, t + 1)
                if t >= GS:
                    dve.wait_ge(s_out[t % GS], 16 * (t // GS))
                dve.scalar_tensor_tensor(otb[:, t % GS, :], gat[:, t % GS, 1, :], wts[:, 1, t:t + 1], x2[:, t, :], ALU.mult, ALU.add).then_inc(s_o2, 1)

        def experts_pe(pe):
            for t in range(NT):
                if t % (CQ // P) == 0:
                    pe.wait_ge(s_h, NQ * (L - 1) + t // (CQ // P) + 1)
                if t >= 4:
                    pe.wait_ge(s_oTe, t - 3)
                for h in range(H):
                    last = pe.transpose(bank[t % 4][0:P, h * 128:(h + 1) * 128], hT[:, h, t * P:(t + 1) * P], ident[:, :])
                last.then_inc(s_oT, 1)

            def rows_up(t):
                pe.wait_ge(s_fn, t + 1)
                for h in range(H):
                    last = pe.transpose(bank[4 + t % 2][:, h * P:(h + 1) * P], xn[:, t, h * 128:(h + 1) * 128], ident[0:P, 0:P])
                last.then_inc(s_gT, 1)

            rows_up(0)
            pe.wait_ge(s_gbs, 1)
            for t in range(NT):
                if t + 1 < NT:
                    rows_up(t + 1)
                pe.wait_ge(s_gTe, t + 1)
                o = bank[6][0:P, t * NE:(t + 1) * NE]
                for h in range(H):
                    pe.matmul(o, xnT[:, t % 2, h, :], wgs[:, h, :], start=h == 0, stop=False)
                last = pe.matmul(o, ones[0:1, 0:P], gbs[:, :], start=False, stop=True)
            last.then_inc(s_gate, 1)
            pe.wait_ge(s_msk, 1)
            flat = msk[:, :, :].rearrange("p t e -> p (t e)")
            pe.matmul(bank[0][0:P, 0:NT * NE], tri[:, :], flat, start=True, stop=True)
            pe.matmul(bank[1][0:P, 0:NT * NE], ones[0:P, 0:P], flat, start=True, stop=True).then_inc(s_rank, 1)
            pe.wait_ge(s_slot, 1)
            pe.wait_ge(s_w1, 16)
            pe.wait_ge(s_w2, 16)

            def rows(i, j, u):
                pe.wait_ge(s_xt[u], 16 * (i + 1))
                for h in range(H):
                    last = pe.transpose(bank[u][:, h * TT:(h + 1) * TT], xtb[:, u, h * 128:(h + 1) * 128], ident[:, :])
                last.then_inc(s_xtT, 1)

            def up(j, u):
                e = pe.value_load(te[0:1, bass.ds(j, 1)], min_val=0, max_val=NE - 1)
                pe.wait_ge(s_xtc, j + 1)
                for h in range(H):
                    last = pe.matmul(bank[2 + u][:, :], xtT[:, u, h, :], w1s[:, bass.ds(e, 1), h, :].rearrange("p a f -> p (a f)"), start=h == 0, stop=h == H - 1)
                last.then_inc(s_h1, 1)

            def across(j, u):
                pe.wait_ge(s_h1b, j + 1)
                for k in range(FK):
                    last = pe.transpose(bank[4 + u][:, k * TT:(k + 1) * TT], h1[:, u, k * 128:(k + 1) * 128], ident[:, :])
                last.then_inc(s_hT, 1)

            def down(j, u, free):
                e = pe.value_load(te[0:1, bass.ds(j, 1)], min_val=0, max_val=NE - 1)
                pe.wait_ge(s_hTc, j + 1)
                if free is not None:
                    pe.wait_ge(s_yb, free)
                for k in range(FK):
                    last = pe.matmul(bank[6 + u][:, 0:D], h1T[:, u, k, :], w2s[:, bass.ds(e, 1), k, :].rearrange("p a f -> p (a f)"), start=k == 0, stop=k == FK - 1)
                last.then_inc(s_y, 1)

            rows(0, 0, 0)
            up(0, 0)
            rows(0, 1, 1)
            across(0, 0)
            up(1, 1)
            down(0, 0, None)
            rows(1, 2, 0)
            across(1, 1)
            up(2, 0)
            down(1, 1, None)
            rows(1, 3, 1)
            across(2, 0)
            with pe.Fori(1, J // 2 - 1) as i:
                j = pe.snap(2 * i)
                up(j + 1, 1)
                down(j, 0, j - 1)
                rows(i + 1, j + 2, 0)
                across(j + 1, 1)
                up(j + 2, 0)
                down(j + 1, 1, j)
                rows(i + 1, j + 3, 1)
                across(j + 2, 0)
            up(J - 1, 1)
            down(J - 2, 0, J - 3)
            across(J - 1, 1)
            down(J - 1, 1, J - 2)

        @block.sync
        def _(sp):
            tail_dmas(sp, dstI, dst, 1, s_dst)
            tail_dmas(sp, srcI, src, 1, s_src)
            tail_dmas(sp, eaC, edge_attr.rearrange("e j -> (e j)"), 4, s_ea)
            sp.dma_start(xin[:, :, :], x.rearrange("(t p) d -> p t d", p=P)).then_inc(s_x, 16)
            sp.wait_ge(s_cst, 1)
            xz = xs.rearrange("(p r) d -> p (r d)", p=128)
            for k in range(J // 2 // 2):
                sp.dma_start(xz[:, k * 4 * D:(k + 1) * 4 * D].rearrange("p (a c) -> p a c", a=2),
                             zt[:, :].unsqueeze(1).to_broadcast([128, 2, 2 * D])).then_inc(s_zero, 16)
            sp.dma_start(wgs[:, :, :], wg.rearrange("(h p) e -> p h e", p=128)).then_inc(s_fw, 16)
            sp.dma_start(gbr[:, 0, :], bg.rearrange("(a e) -> a e", a=1)).then_inc(s_fw, 16)
            sp.dma_start(gbr[:, 1, :], gbias.rearrange("(a e) -> a e", a=1)).then_inc(s_fw, 16)
            sp.wait_ge(s_slC, 1)
            sp.dma_start(sl_dram.rearrange("(b p e) -> p b e", b=NB, p=CB), slC[:, :, :]).then_inc(s_sld, 16)
            sp.wait_ge(s_sld, 16)
            sp.wait_ge(s_dpart, 1)
            row = sl_dram.rearrange("(b e) -> b e", b=NLB)
            for b in range(NLB):
                if b >= 2:
                    sp.wait_ge(s_ohT, b - 1)
                sp.dma_start(slrow[:, b % 2, :], row[b:b + 1, :].to_broadcast([P, LB * CH])).then_inc(s_slr[b % 2], 16)
            sp.wait_ge(s_s4Te, NQ)
            sp.wait_ge(s_ez, 1)
            load_layer(sp, 0)
            with sp.Fori(1, L) as l:
                sp.wait_ge(s_bn, l)
                load_layer(sp, l)
            if stop is None:
                experts_sp(sp)
            if stop == "layers":
                sp.wait_ge(s_h, NQ * L)
                sp.dma_start(dbg_h, hT[:, :, :]).then_inc(s_dbg, 16)
                sp.wait_ge(s_dbg, 16)
            if stop == "build":
                sp.dma_start(dbg_at, at[:, :, :]).then_inc(s_dbg, 16)
                sp.dma_start(dbg_d, dinvB[:, :]).then_inc(s_dbg, 16)
                sp.dma_start(dbg_p, dinvP[:, :]).then_inc(s_dbg, 16)
                sp.dma_start(dbg_s, s4T[:, :]).then_inc(s_dbg, 16)
                sp.dma_start(dbg_h, hT[:, :, :]).then_inc(s_dbg, 16)
                sp.wait_ge(s_dbg, 80)

        @block.gpsimd
        def _(pool):
            done = [0]

            def step(ins):
                done[0] += 1
                ins.then_inc(s_po, 1)
                pool.wait_ge(s_po, done[0])

            pool.memset(dstI[:, NB - 1, :], DST_PAD)
            pool.memset(srcI[:, NB - 1, :], 0)
            pool.memset(eaC[:, NB - 1, :], 0.0).then_inc(s_mem, 1)
            step(pool.memset(ident[:, :], 0.0))
            pool.affine_select(out=ident[:, :], in_=ident[:, :], compare_op=ALU.not_equal, fill=1.0, base=0,
                               pattern=[[-1, 128]], channel_multiplier=1)
            pool.memset(ones[:, :], 1.0)
            pool.memset(ones16[:, :], 1.0)
            pool.iota(cidx[:, :], pattern=[[1, NCH]], base=0, channel_multiplier=0, allow_small_or_imprecise_dtypes=True)
            pool.iota(tlo[:, :], pattern=[[0, 1]], base=0, channel_multiplier=P, allow_small_or_imprecise_dtypes=True)
            pool.iota(iotaP[:, :], pattern=[[0, 1]], base=0, channel_multiplier=1, allow_small_or_imprecise_dtypes=True)
            pool.iota(iotaK[:, 0:GW], pattern=[[KEY, GROUPS], [1, P]], base=0, channel_multiplier=0)
            pool.memset(iotaK[:, GW:GW + 1], -32000)
            pool.iota(iotaS[:, :, :], pattern=[[1, 128], [0, 2]], base=0, channel_multiplier=0)
            pool.iota(iotaD[:, :], pattern=[[1, P + 1]], base=0, channel_multiplier=0)
            pool.iota(iota25[:, :], pattern=[[1, NT]], base=0, channel_multiplier=0).then_inc(s_mem, 1)
            pool.memset(zt[:, :], 0.0).then_inc(s_cst, 1)
            step(pool.memset(tri[:, :], 1.0))
            pool.affine_select(out=tri[:, :], in_=tri[:, :], compare_op=ALU.is_gt, fill=0.0, base=0,
                               pattern=[[1, P]], channel_multiplier=-1)
            pool.iota(iota8[:, :], pattern=[[1, NE]], base=0, channel_multiplier=0, allow_small_or_imprecise_dtypes=True)
            pool.iota(iotaJ[:, :], pattern=[[1, J]], base=0, channel_multiplier=0, allow_small_or_imprecise_dtypes=True).then_inc(s_cst, 1)
            if stop is None:
                experts_pool(pool)

        @block.vector
        def _(dve):
            done = [0]

            def step(ins):
                done[0] += 1
                ins.then_inc(s_dv, 1)
                dve.wait_ge(s_dv, done[0])

            def inverse_root(root, v, sd, tmp):
                step(dve.reciprocal(root, sd))
                step(dve.tensor_tensor(tmp, root, root, ALU.mult))
                step(dve.tensor_tensor(tmp, tmp, v, ALU.mult))
                step(dve.tensor_scalar(tmp, tmp, -0.5, 1.5, ALU.mult, ALU.add))
                step(dve.tensor_tensor(root, root, tmp, ALU.mult))

            def rounded(dst_ap, src_ap, tmp):
                step(dve.tensor_scalar(tmp, src_ap, MAGIC, None, ALU.add))
                step(dve.tensor_scalar(dst_ap, tmp, MAGIC, None, ALU.subtract))

            dve.wait_ge(s_dst, 48)
            dve.tensor_copy(dstC[:, :, :], dstI[:, :, :]).then_inc(s_edges, 1)
            dve.wait_ge(s_src, 48)
            dve.tensor_copy(srcC[:, :, :], srcI[:, :, :]).then_inc(s_edges, 1)
            dve.wait_ge(s_edges, 2)
            dve.tensor_reduce(cmm[:, 0, :], dstC[:, :, :], axis=XYZ, op=ALU.min)
            step(dve.tensor_reduce(cmm[:, 1, :], dstC[:, :, :], axis=XYZ, op=ALU.max))
            dve.tensor_copy(cmmB[:, :, :], cmm[:, :, :].rearrange("p a b -> p (a b)").unsqueeze(2).to_broadcast([CB, 2 * NB, NT])).then_inc(s_cmm, 1)
            sc = srcC[:, :, :].rearrange("p b e -> p (b e)")
            step(dve.tensor_scalar(ta[0:CB, :], sc, float(-(P // 2)), 1.0 / P, ALU.add, ALU.mult))
            rounded(tb[0:CB, :], ta[0:CB, :], ta[0:CB, :])
            dve.scalar_tensor_tensor(slC[:, :, :].rearrange("p b e -> p (b e)"), tb[0:CB, :], float(-P), sc, ALU.mult, ALU.add).then_inc(s_slC, 1)
            dve.wait_ge(s_tp, 8)
            srcE = ta[:, 0:NCH]
            tileE = tb[:, 0:NCH]
            step(dve.memset(dstE[:, NCH:NCHP], float(DST_PAD)))
            step(dve.memset(keyE[:, NCH:NCHP], float(DST_PAD)))
            step(dve.memset(powE[:, NCH:NCHP], 0))
            step(dve.memset(sl16[:, NCH:NCHP], 0))
            step(dve.tensor_copy(dstE[:, 0:NCH], bank[0][:, 0:NCH]))
            step(dve.tensor_copy(srcE, bank[1][:, 0:NCH]))
            step(dve.tensor_scalar(tg[:, :], srcE, float(-(P // 2)), 1.0 / P, ALU.add, ALU.mult))
            rounded(tileE, tg[:, :], tg[:, :])
            step(dve.scalar_tensor_tensor(sl16[:, 0:NCH], tileE, float(-P), srcE, ALU.mult, ALU.add))
            step(dve.tensor_copy(s16[:, :], tileE))
            step(dve.tensor_scalar(srcE, tileE, -(FIELDS - 1) / 2, 1.0 / FIELDS, ALU.add, ALU.mult))
            rounded(tg[:, :], srcE, srcE)
            step(dve.scalar_tensor_tensor(keyE[:, 0:NCH], tg[:, :], float(KEY), dstE[:, 0:NCH], ALU.mult, ALU.add))
            step(dve.scalar_tensor_tensor(srcE, tg[:, :], float(-FIELDS), tileE, ALU.mult, ALU.add))
            step(dve.tensor_scalar(srcE, srcE, 8.0, 127.0, ALU.mult, ALU.add))
            step(dve.tensor_scalar(powE[:, 0:NCH], srcE, float(2 ** 23), None, ALU.mult))
            dve.wait_ge(s_tp, 12)
            for j in range(4):
                dve.wait_ge(s_tp, 9 + j)
                dve.tensor_copy(eaE[:, :, j], bank[2 + j][:, 0:NCH])
            dve.wait_ge(s_minmax, 2)
            step(dve.tensor_scalar(lohi2[:, 0:1], tlo[:, :], float(P - 1), None, ALU.add))
            step(dve.tensor_scalar(m1[:, :], bank[6][0:NT, 0:NCH], lohi2[:, 0:1], None, ALU.is_le))
            step(dve.tensor_scalar(m2[:, :], bank[7][0:NT, 0:NCH], tlo[:, :], None, ALU.is_ge))
            step(dve.tensor_tensor(m1[:, :], m1[:, :], m2[:, :], ALU.mult))
            step(dve.scalar_tensor_tensor(m2[:, :], m1[:, :], -BIG, cidx[:, :], ALU.mult, ALU.add))
            step(dve.tensor_reduce(lohi[:, 0:1], m2[:, :], axis=XYZ, op=ALU.min))
            step(dve.scalar_tensor_tensor(m2[:, :], cidx[:, :], 1.0, m1[:, :], ALU.add, ALU.mult))
            step(dve.tensor_reduce(lohi[:, 1:2], m2[:, :], axis=XYZ, op=ALU.max))
            step(dve.tensor_scalar(lohi2[:, 0:1], lohi[:, 0:1], BIG, float(MAX_FIRST), ALU.add, ALU.min))
            step(dve.tensor_tensor(lohi[:, 1:2], lohi[:, 1:2], lohi2[:, 0:1], ALU.subtract))
            step(dve.tensor_scalar(lohi[:, 1:2], lohi[:, 1:2], 1.0 / U, (U - 1) / (2 * U) - 1.0, ALU.mult, ALU.add))
            rounded(lohi2[:, 1:2], lohi[:, 1:2], lohi[:, 1:2])
            dve.tensor_scalar(lohi2[:, 1:2], lohi2[:, 1:2], float(MIN_TURNS - 1), None, ALU.max).then_inc(s_lohi, 1)
            dve.wait_ge(s_rngp, 1)
            dve.tensor_copy(rng[:, :], bank[0][0:1, 0:2 * NT]).then_inc(s_rng, 1)
            dve.wait_ge(s_x, 16)
            for t in range(NT):
                last = dve.bn_stats(xst[:, t, :], xin[:, t, :])
            step(last)
            for t in range(NT):
                last = dve.bn_aggr(xmv[:, t, :], xst[:, t, :])
            step(last)
            dve.tensor_scalar(xve[:, :], xmv[:, :, 1], LN_EPS, None, ALU.add).then_inc(s_var, 1)
            dve.wait_ge(s_std, 1)
            inverse_root(xrs[:, :], xve[:, :], xsd[:, :], xt1[:, :])
            step(dve.tensor_scalar(xrs[:, :], xrs[:, :], float(2 ** H0_EXP), None, ALU.mult))
            for t in range(NT):
                dve.tensor_scalar(xin[:, t, :], xin[:, t, :], xmv[:, t, 0:1], xrs[:, t:t + 1], ALU.subtract, ALU.mult).then_inc(s_xn, 1)

            dve.wait_ge(s_rng, 1)
            dve.wait_ge(s_mem, 2)
            dve.wait_ge(s_xTe, NT)
            dve.wait_ge(s_sld, 16)
            dve.sem_inc(s_free, U)
            dve.sem_inc(s_freeD, U)
            step(dve.memset(orI[:, :], 0))
            turns_before = 0
            for t in range(NT + 1):
                if t < NT:
                    first = dve.value_load(rng[0:1, t:t + 1], min_val=0, max_val=MAX_FIRST)
                    last_turn = dve.value_load(rng[0:1, NT + t:NT + t + 1], min_val=MIN_TURNS - 1, max_val=MAX_TURNS - 1)
                    if t:
                        step(dve.tensor_scalar(iotaK[:, 0:GW + 1], iotaK[:, 0:GW + 1], float(P), None, ALU.add))
                    with dve.Fori(0, last_turn + 1) as i:
                        k = dve.snap(U * (turns_before + i))
                        c = dve.snap(chunk_of(first, i))
                        for j in range(U):
                            if j % 2 == 0:
                                dve.wait_ge(s_free, k + j + 2)
                                dve.tensor_tensor(ohS[:, j // 2, :, :], iotaS[:, :, :],
                                                  sl16[:, bass.ds(c + j, 2)].unsqueeze(1).to_broadcast([128, 128, 2]), ALU.is_equal)
                            dve.tensor_scalar(cnt1[:, j, :], iotaK[:, :], keyE[:, bass.ds(c + j, 1)],
                                              powE[:, bass.ds(c + j, 1)].bitcast(F32), ALU.is_equal, ALU.mult).then_inc(s_oh, 1)
                    turns_before = dve.snap(turns_before + last_turn + 1)
                if t:
                    dve.wait_ge(s_enc, t)
                    if t >= 2:
                        dve.wait_ge(s_or, t - 1)
                    dve.tensor_tensor(orI[:, :], orI[:, :], encI[:, (t - 1) % 2, :], ALU.bitwise_or).then_inc(s_or, 1)
            dve.wait_ge(s_deg, NT)
            step(dve.tensor_copy(deg[:, :], bank[6][0:P, 0:NT]))
            step(dve.tensor_scalar(deg1[:, :], deg[:, :], 1.0, None, ALU.max))
            dve.sem_inc(s_var, 1)
            dve.wait_ge(s_std, 2)
            inverse_root(dinvP[:, :], deg1[:, :], dsd[:, :], dt1[:, :])
            step(dve.scalar_tensor_tensor(dinvP[:, :], deg[:, :], 1.0, dinvP[:, :], ALU.min, ALU.mult))
            for t in range(NT):
                if t >= 2:
                    dve.wait_ge(s_bc, t - 1)
                dve.tensor_scalar(ddg[:, t % 2, :], ident[0:P, 0:P], dinvP[:, t:t + 1], None, ALU.mult).then_inc(s_dg, 1)
            dve.wait_ge(s_bc, NT)
            step(dve.tensor_copy(dpart[:, 0, :], dinvP[:, :]))
            step(dve.tensor_tensor(drem[:, 0, :], dinvP[:, :], dpart[:, 0, :], ALU.subtract))
            step(dve.tensor_copy(dpart[:, 1, :], drem[:, 0, :]))
            step(dve.tensor_tensor(drem[:, 1, :], drem[:, 0, :], dpart[:, 1, :], ALU.subtract))
            dve.tensor_copy(dpart[:, 2, :], drem[:, 1, :]).then_inc(s_dpart, 1)
            for b in range(NLB):
                dve.wait_ge(s_slr[b % 2], 16 * (b // 2 + 1))
                if b >= 2:
                    dve.wait_ge(s_lk, 2 * (b - 1))
                dve.tensor_scalar(ohT[:, b % 2, :], slrow[:, b % 2, :], iotaP[0:P, :], None, ALU.is_equal).then_inc(s_ohT, 1)
                step(dve.tensor_tensor(ohs[:, b % 2, :, :], s16[:, b * LB:(b + 1) * LB].unsqueeze(2).to_broadcast([128, LB, NT]),
                                       iota25[:, :].unsqueeze(1).to_broadcast([128, LB, NT]), ALU.is_equal))
                for g in range(2):
                    dve.wait_ge(s_lk, 2 * b + g + 1)
                    step(dve.tensor_tensor(lkt[:, g, :], bank[1 + g][:, 0:LG * NT],
                                           ohs[:, b % 2, g * LG:(g + 1) * LG, :].rearrange("p c s -> p (c s)"), ALU.mult))
                    dve.tensor_reduce(dsrc[:, b * LB + g * LG:b * LB + (g + 1) * LG],
                                      lkt[:, g, :].rearrange("p (c s) -> p c s", s=NT), axis=XYZ, op=ALU.add).then_inc(s_lke, 1)
            dve.wait_ge(s_lke, 2 * NLB)
            step(dve.tensor_tensor(v4[:, :, :], eaE[:, :, :], dsrc[:, :].unsqueeze(2).to_broadcast([128, NCH, 4]), ALU.mult))
            step(dve.memset(w12[:, NCH:NCHP, :], 0.0))
            step(dve.tensor_copy(w12[:, 0:NCH, 0:4], v4[:, :, :]))
            step(dve.tensor_tensor(v4b[:, :, :], v4[:, :, :], w12[:, 0:NCH, 0:4], ALU.subtract))
            step(dve.tensor_copy(w12[:, 0:NCH, 4:8], v4b[:, :, :]))
            step(dve.tensor_tensor(v4[:, :, :], v4b[:, :, :], w12[:, 0:NCH, 4:8], ALU.subtract))
            dve.tensor_copy(w12[:, 0:NCH, 8:12], v4[:, :, :]).then_inc(s_w12, 1)
            turns_before = 0
            for t in range(NT):
                first = dve.value_load(rng[0:1, t:t + 1], min_val=0, max_val=MAX_FIRST)
                last_turn = dve.value_load(rng[0:1, NT + t:NT + t + 1], min_val=MIN_TURNS - 1, max_val=MAX_TURNS - 1)
                if t:
                    step(dve.tensor_scalar(iotaD[:, :], iotaD[:, :], float(P), None, ALU.add))
                with dve.Fori(0, last_turn + 1) as i:
                    k = dve.snap(U * (turns_before + i))
                    c = dve.snap(chunk_of(first, i))
                    for j in range(U):
                        dve.wait_ge(s_freeD, k + 1 + j)
                        dve.tensor_scalar(ohD[:, j, :], iotaD[:, :], dstE[:, bass.ds(c + j, 1)], None, ALU.is_equal).then_inc(s_ohD, 1)
                turns_before = dve.snap(turns_before + last_turn + 1)
                if t:
                    s4_out(dve, t - 1)
            s4_out(dve, NT - 1)
            dve.wait_ge(s_s4Te, NQ)
            dve.memset(ewT[:, :, :], 0.0)
            dve.memset(inv[:, :], 2.0 ** -H0_EXP).then_inc(s_ez, 1)
            dve.wait_ge(s_ez, 1)
            m_rows_dve(dve, lambda n: 0)
            with dve.Fori(0, L - 1) as l:
                layer_dve(dve, lambda n: dve.snap(l * n), LOADS * (l + 1), False)
            layer_dve(dve, lambda n: (L - 1) * n, LOADS * L, True)
            if stop is None:
                experts_dve(dve, step, rounded, inverse_root)

        @block.scalar
        def _(act):
            act.wait_ge(s_var, 1)
            act.activation(xsd[:, :], xve[:, :], ACT.Sqrt).then_inc(s_std, 1)
            for t in range(NT):
                act.wait_ge(s_xT, t + 1)
                act.activation(hT[:, :, t * P:(t + 1) * P], bank[2 + t % 2][:, 0:H * P].rearrange("p (h n) -> p h n", h=H), ACT.Copy).then_inc(s_xTe, 1)
            act.wait_ge(s_xTe, NT)
            for t in range(NT + 1):
                if t < NT:
                    act.wait_ge(s_cnt, t + 1)
                    if t >= 2:
                        act.wait_ge(s_or, t - 1)
                        act.wait_ge(s_at, t - 1)
                    for b in range(GB):
                        last = act.activation(encI[:, t % 2, b * GC:(b + 1) * GC], bank[GB * (t % 2) + b][0:P, 0:GC], ACT.Copy)
                    last.then_inc(s_enc, 1)
                if 1 <= t <= NT:
                    u = t - 1
                    act.wait_ge(s_enc, u + 1)
                    byte = encI[:, u % 2, :].bitcast(U8).rearrange("p (g n k) -> p k g n", g=GROUPS, k=4)
                    for f in range(FIELDS):
                        n = (NT - f + FIELDS - 1) // FIELDS
                        last = act.activation(at[:, f:f + FIELDS * (n - 1) + 1:FIELDS, u * P:(u + 1) * P], byte[:, f, 0:n, :], ACT.Copy, saturate=False)
                    last.then_inc(s_at, 1)
            act.wait_ge(s_var, 2)
            act.activation(dsd[:, :], deg1[:, :], ACT.Sqrt).then_inc(s_std, 1)
            for q, (a, w) in enumerate(COLS):
                act.wait_ge(s_bc, (a + w) // P)
                act.activation(dinvB[:, a:a + w], bank[q % 2][:, 0:w], ACT.Copy).then_inc(s_dB, 1)
            for q, (a, w) in enumerate(COLS):
                act.wait_ge(s_s4T, q + 1)
                act.activation(s4T[:, a:a + w], bank[q % 2][0:4, 0:w], ACT.Copy).then_inc(s_s4Te, 1)
            m_rows_act(act, lambda n: 0)
            with act.Fori(0, L - 1) as l:
                layer_act(act, lambda n: act.snap(l * n), False)
            layer_act(act, lambda n: (L - 1) * n, True)
            if stop is None:
                experts_act(act)

        @block.tensor
        def _(pe):
            pe.wait_ge(s_mem, 2)
            for n, tile in enumerate((dstC, srcC)):
                pe.wait_ge(s_edges, n + 1)
                for b in range(NB):
                    pe.transpose(bank[n][:, b * CB:(b + 1) * CB], tile[:, b, :], ident[0:CB, 0:CB]).then_inc(s_tp, 1)
            pe.wait_ge(s_ea, 48)
            for j in range(4):
                for b in range(NB):
                    last = pe.transpose(bank[2 + j][:, b * CB:(b + 1) * CB], eaC[:, b, j:j + 4 * (CH - 1) + 1:4], ident[0:CB, 0:CB])
                last.then_inc(s_tp, 1)
            pe.wait_ge(s_cmm, 1)
            for n in range(2):
                for b in range(NB):
                    last = pe.matmul(bank[6 + n][0:NT, b * CB:(b + 1) * CB], cmmB[:, n * NB + b, :], ident[0:CB, 0:CB], start=True, stop=True)
                last.then_inc(s_minmax, 1)
            pe.wait_ge(s_lohi, 1)
            for n in range(2):
                last = pe.matmul(bank[0][0:1, n * NT:(n + 1) * NT], lohi2[:, n:n + 1], ident[0:NT, 0:NT], start=True, stop=True)
            last.then_inc(s_rngp, 1)
            for t in range(NT):
                pe.wait_ge(s_xn, t + 1)
                if t >= 2:
                    pe.wait_ge(s_xTe, t - 1)
                for h in range(H):
                    last = pe.transpose(bank[2 + t % 2][:, h * P:(h + 1) * P], xin[:, t, h * 128:(h + 1) * 128], ident[0:P, 0:P])
                last.then_inc(s_xT, 1)
            pe.wait_ge(s_rng, 1)
            pe.wait_ge(s_xTe, NT)

            def degrees(t):
                pe.wait_ge(s_at, t + 1)
                for s in range(NT):
                    last = pe.matmul(bank[6][0:P, t:t + 1], at[:, s, t * P:(t + 1) * P], ones16[:, 0:1], start=s == 0, stop=s == NT - 1)
                last.then_inc(s_deg, 1)

            turns_before = 0
            for t in range(NT):
                last_turn = pe.value_load(rng[0:1, NT + t:NT + t + 1], min_val=MIN_TURNS - 1, max_val=MAX_TURNS - 1)
                if t >= 2:
                    pe.wait_ge(s_enc, t - 1)

                def turn(i, start, stop_):
                    k = pe.snap(U * (turns_before + i))
                    for j in range(U):
                        pe.wait_ge(s_oh, k + 1 + j)
                        for b in range(GB):
                            last = pe.matmul(bank[GB * (t % 2) + b][:, 0:GC], ohS[:, j // 2, :, j % 2],
                                             cnt1[:, j, b * GC:(b + 1) * GC], start=start and j == 0, stop=stop_ and j == U - 1)
                        last.then_inc(s_cnt if stop_ and j == U - 1 else s_free, 1)
                    if stop_:
                        pe.wait_ge(s_cnt, t + 1)
                        pe.sem_inc(s_free, 1)

                turn(0, True, False)
                with pe.Fori(1, last_turn) as i:
                    turn(i, False, False)
                turn(last_turn, False, True)
                turns_before = pe.snap(turns_before + last_turn + 1)
                if t >= 2:
                    degrees(t - 2)
            degrees(NT - 2)
            degrees(NT - 1)
            pe.wait_ge(s_enc, NT)
            for q, (a, w) in enumerate(COLS):
                if q >= 2:
                    pe.wait_ge(s_dB, q - 1)
                for t in range(a // P, (a + w) // P):
                    pe.wait_ge(s_dg, t + 1)
                    pe.matmul(bank[q % 2][:, t * P - a:(t + 1) * P - a], ones[0:P, :], ddg[:, t % 2, :], start=True, stop=True).then_inc(s_bc, 1)
            pe.wait_ge(s_dpart, 1)
            pe.wait_ge(s_dB, NQ)
            for b in range(NLB):
                pe.wait_ge(s_ohT, b + 1)
                for g in range(2):
                    if b:
                        pe.wait_ge(s_lke, 2 * b + g - 1)
                    for c in range(LG):
                        for k in range(3):
                            last = pe.matmul(bank[1 + g][:, c * NT:(c + 1) * NT], ohT[:, b % 2, (g * LG + c) * CH:(g * LG + c + 1) * CH],
                                             dpart[:, k, :], start=k == 0, stop=k == 2)
                    last.then_inc(s_lk, 1)
            pe.wait_ge(s_w12, 1)
            turns_before = 0
            for t in range(NT):
                first = pe.value_load(rng[0:1, t:t + 1], min_val=0, max_val=MAX_FIRST)
                last_turn = pe.value_load(rng[0:1, NT + t:NT + t + 1], min_val=MIN_TURNS - 1, max_val=MAX_TURNS - 1)
                if t >= 2:
                    pe.wait_ge(s_s4e, 2 * (t - 1) - 1)

                def turn4(i, start, stop_):
                    k = pe.snap(U * (turns_before + i))
                    c = pe.snap(chunk_of(first, i))
                    for j in range(U):
                        pe.wait_ge(s_ohD, k + 1 + j)
                        last = pe.matmul(bank[3 + t % 2][0:P, 0:12], ohD[:, j, 0:P], w12[:, bass.ds(c + j, 1), :].rearrange("p a w -> p (a w)"),
                                         start=start and j == 0, stop=stop_ and j == U - 1)
                        last.then_inc(s_s4 if stop_ and j == U - 1 else s_freeD, 1)
                    if stop_:
                        pe.wait_ge(s_s4, t + 1)
                        pe.sem_inc(s_freeD, 1)

                turn4(0, True, False)
                with pe.Fori(1, last_turn) as i:
                    turn4(i, False, False)
                turn4(last_turn, False, True)
                turns_before = pe.snap(turns_before + last_turn + 1)
            pe.wait_ge(s_s4e, 2 * NT)
            for q, (a, w) in enumerate(COLS):
                if q >= 2:
                    pe.wait_ge(s_s4Te, q - 1)
                for t in range(a // P, (a + w) // P):
                    last = pe.transpose(bank[q % 2][0:4, t * P - a:(t + 1) * P - a], s4P[:, t, :], ident[0:P, 0:P])
                last.then_inc(s_s4T, 1)
            pe.wait_ge(s_s4Te, NQ)
            m_rows_pe(pe, lambda n: 0, lambda t: None)

            def layer(l, last_layer):
                base = (lambda n: (L - 1) * n) if last_layer else (lambda n: pe.snap(l * n))
                layer_pe(pe, base)
                if not last_layer:
                    def ready(t):
                        if t % (CQ // P) == 0:
                            pe.wait_ge(s_h, base(NQ) + t // (CQ // P) + 1)
                    m_rows_pe(pe, lambda n: base(n) + n, ready)

            with pe.Fori(0, L - 1) as l:
                layer(l, False)
            layer(L - 1, True)
            if stop is None:
                experts_pe(pe)


INPUTS = ["x", "src", "dst", "edge_attr_4", "L0_gnn_mlp_w", "L0_gnn_mlp_b", "L0_gnn_ew1", "L0_gnn_ew2", "L0_gnn_bn_g",
          "L0_gnn_bn_b", "L0_ffn_Wg", "L0_ffn_bg", "L0_ffn_bias", "L0_ffn_W1", "L0_ffn_b1", "L0_ffn_W2", "L0_ffn_b2"]


def kernel(**inputs):
    import numpy as np
    from concourse import bacc
    from concourse.bass_utils import run_bass_kernel_spmd

    nc = bacc.Bacc("TRN2", target_bir_lowering=False, num_devices=1)
    arrays, args = {}, []
    for name in INPUTS:
        a = np.ascontiguousarray(inputs[name])
        arrays["in_" + name] = a
        args.append(nc.dram_tensor("in_" + name, a.shape, mybir.dt.from_np(a.dtype), kind="ExternalInput").ap())
    out = nc.dram_tensor("out_rows", (N, D), F32, kind="ExternalOutput").ap()
    gnn_ffn_program(nc, *args, out)
    done = run_bass_kernel_spmd(nc, [arrays], core_ids=[0])
    return done.results[0]["out_rows"]
```

```python
import concourse.bass as bass
from concourse import mybir
from contextlib import ExitStack

F32 = mybir.dt.float32
I32 = mybir.dt.int32
U32 = mybir.dt.uint32
I16 = mybir.dt.int16
U8 = mybir.dt.uint8
BF16 = mybir.dt.bfloat16
F16 = mybir.dt.float16
F8 = mybir.dt.float8e4
SIZE = {F32: 4, I32: 4, U32: 4, I16: 2, U8: 1, BF16: 2, F16: 2, F8: 1}
ALU = mybir.AluOpType
ACT = mybir.ActivationFunctionType
XYZ = mybir.AxisListType.X

N = 3125
D = 256
E = 53125
L = 5
P = 125
NT = N // P
H = D // 128
CH = 128
NCH = 416
NB = 4
CB = NCH // NB
U = 6
MIN_TURNS = 3
MAX_FIRST = NCH - U * MIN_TURNS
MAX_TURNS = (NCH + U - 1) // U
HU = U // 2
NCHP = NCH + U
DST_PAD = 3500
FIELDS = 5
GROUPS = (NT + FIELDS - 1) // FIELDS
assert GROUPS * FIELDS == NT
GB = 2
GC = (GROUPS * P + GB - 1) // GB
GW = GB * GC
NIBBLES = 0x0F0F0F
KEY = 3584
MAGIC = 12582912.0
BIG = 1000.0
CQ = 500
COLS = [(q, min(CQ, N - q)) for q in range(0, N, CQ)]
NQ = len(COLS)
LN_EPS = 1e-5
BN_EPS = 1e-5
H0_EXP = 11
LB = 13
NLB = NCH // LB
DENSE = H * NQ * NT
DENSE_L = 3
DENSE_S = 9
NE = 8
F = 512
FK = F // 128
TT = 128
J = (2 * N + NE * (TT - 1)) // TT
assert J % 2 == 0
GS = 4


def gnn_ffn_program(nc, x, src, dst, edge_attr, mlp_w, mlp_b, ew1, ew2, bn_g, bn_b,
                    wg, bg, gbias, w1, b1, w2, b2, out, stop=None):
    ctx = ExitStack()
    with ctx:
        base = (nc.sbuf_base + 31) // 32 * 32

        class Region:
            def __init__(self, start):
                self.at = start

            def __call__(self, name, shape, dt):
                n = SIZE[dt]
                for s in shape[1:]:
                    n *= s
                t = nc.alloc_sbuf_tensor_at(name, shape, dt, offset=base + self.at)
                self.at = (self.at + n + 31) // 32 * 32
                assert base + self.at <= nc.sbuf_usable_end, name
                return t

        def sem(name):
            return ctx.enter_context(nc.semaphore(name))

        bank = [ctx.enter_context(nc.psum_tensor(f"bank{i}", [128, 512], F32)) for i in range(8)]

        keep = Region(0)
        at = keep("at", [P, NT, N], F8)
        hT_at = keep.at
        hT = keep("hT", [128, H, N], F32)
        dinvB_at = keep.at
        dinvB = keep("dinvB", [128, N], F32)
        s4T = keep("s4T", [4, N], F32)
        ident = keep("ident", [128, 128], F32)
        ones = keep("ones", [128, 128], F32)
        ones16 = keep("ones16", [128, 1], BF16)
        dinvP = keep("dinvP", [P, NT], F32)
        dstE = keep("dstE", [128, NCHP], F32)
        srcX = keep("srcX", [128, NCHP], I32)
        iotaD0 = keep("iotaD0", [128, P + 1], I16)
        iotaD = keep("iotaD", [128, P + 1], I16)
        rng = keep("rng", [1, 3 * NT + 1], I32)
        flag = keep("flag", [1, 1], I32)
        zt_at = keep.at
        keep.at += 4 * 1024
        xstart = keep.at

        r = Region(xstart)
        aggT = r("aggT", [128, H, N], F32)
        w_at = r.at
        wcur = r("wcur", [128, 2 * H, D], F32)
        wraw = r("wraw", [128, 2 * H, D], F32)
        ewm = r("ewm", [4, D], F32)
        r.at = max(r.at, (w_at + NCHP * 12 * SIZE[BF16] + 31) // 32 * 32)
        w_end = r.at
        ewT = r("ewT", [128, H, 4], F32)
        prm = r("prm", [128, 3, H], F32)
        zst = r("zst", [128, H, NQ, 6], F32)
        zmv = r("zmv", [128, H, 2], F32)
        cf = r("cf", [128, 6, H], F32)
        cfi = r("cfi", [128, 2, H], I32)
        inv = r("inv", [128, H], F32)
        m_at = r.at
        m = r("m", [P, NT, 2, D], F16)

        dst3 = r("dst3", [128, NCHP], I16)
        s16 = r("s16", [128, NCH], I16)
        iota25 = r("iota25", [128, NT], I16)
        iotaP = r("iotaP", [128, 1], F32)
        iotaD3 = r("iotaD3", [128, P, HU], I16)
        ohD = r("ohD", [128, 2, P, HU], BF16)
        gsel = r("gsel", [128, U, P + 1], BF16)
        s4s = r("s4s", [P, NT, 4], F32)
        s4P = r("s4P", [P, NT, 4], F32)
        dpart = r("dpart", [P, 3, NT], BF16)
        drem = r("drem", [P, 2, NT], F32)

        r = Region(xstart)
        eaE = r("eaE", [128, NCH, 4], F32)
        pass1 = r.at
        slrow_at = r.at
        slrow = r("slrow", [P, 2, LB * CH], I16)
        ohT_at = r.at
        ohT = r("ohT", [P, 2, LB * CH], BF16)
        ohs = r("ohs", [128, 2, LB, NT], BF16)
        lkt = r("lkt", [128, LB * NT], F32)
        dsrc = r("dsrc", [128, NCH], F32)
        assert r.at <= w_at
        r = Region(slrow_at)
        v4 = r("v4", [128, NCH, 4], F32)
        r = Region(ohT_at)
        v4b = r("v4b", [128, NCH, 4], F32)
        r = Region(w_at)
        w12 = r("w12", [128, NCHP, 12], BF16)
        assert r.at <= w_end

        r = Region(pass1)
        keyE = r("keyE", [128, NCHP], F32)
        powE = r("powE", [128, NCHP], I32)
        sl16 = r("sl16", [128, NCHP], I16)
        iotaK = r("iotaK", [128, GW], I16)
        iotaS = r("iotaS", [128, 128, HU], I16)
        cnt1 = r("cnt1", [128, U, GW], BF16)
        ohS = r("ohS", [128, 2, 128, HU], BF16)
        deg = r("deg", [P, NT], F32)
        deg1 = r("deg1", [P, NT], F32)
        dsd = r("dsd", [P, NT], F32)
        dt1 = r("dt1", [P, NT], F32)
        ddg = r("ddg", [P, 2, P], F32)
        bad = r("bad", [P, 1], F32)
        xin = r("xin", [P, NT, D], F32)
        xrs = r("xrs", [P, NT], F32)
        xsh = r("xsh", [P, NT], F32)
        assert r.at <= m_at + NT * 2 * D * 2
        r = Region(dinvB_at)
        encI = r("encI", [P, 2, GW], I32)
        encB = r("encB", [P, 2, 2, GW], I32)
        assert r.at <= dinvB_at + 2 * 4 * N
        r = Region(0)
        dstI = r("dstI", [CB, NB, CH], I32)
        srcI = r("srcI", [CB, NB, CH], I32)
        eaC = r("eaC", [CB, NB, CH * 4], F32)
        dstC = r("dstC", [CB, NB, CH], F32)
        srcC = r("srcC", [CB, NB, CH], F32)
        slC = r("slC", [CB, NB, CH], I16)
        ta = r("ta", [128, NB * CH], F32)
        tb = r("tb", [128, NB * CH], F32)
        tg = r("tg", [128, NCH], F32)
        cmm = r("cmm", [CB, 2, NB], F32)
        cmmB = r("cmmB", [CB, 2 * NB, NT], F32)
        cidx = r("cidx", [NT, NCH], F32)
        tlo = r("tlo", [NT, 1], F32)
        m1 = r("m1", [NT, NCH], F32)
        m2 = r("m2", [NT, NCH], F32)
        lohi = r("lohi", [NT, 2], F32)
        lohi2 = r("lohi2", [NT, 2], F32)
        rngf = r("rngf", [1, 3, NT], F32)
        xst = r("xst", [P, NT, 6], F32)
        xmv = r("xmv", [P, NT, 2], F32)
        xve = r("xve", [P, NT], F32)
        xsd = r("xsd", [P, NT], F32)
        xt1 = r("xt1", [P, NT], F32)

        r = Region(0)
        x2 = r("x2", [P, NT, D], F32)
        xn = r("xn", [P, NT, D], F32)
        b1B = r("b1B", [128, NE, F], F32)
        b2B = r("b2B", [128, NE, D], F32)
        r = Region(hT_at)
        w2s = r("w2s", [128, NE, FK, D], F32)
        fst = r("fst", [P, NT, 6], F32)
        fmv = r("fmv", [P, NT, 2], F32)
        fve = r("fve", [P, NT], F32)
        fsd = r("fsd", [P, NT], F32)
        frs = r("frs", [P, NT], F32)
        ft1 = r("ft1", [P, NT], F32)
        lgt = r("lgt", [P, NT, NE], F32)
        top = r("top", [P, NT, 8], F32)
        tix = r("tix", [P, NT, 8], U32)
        ef = r("ef", [P, 2, NT], F32)
        oh1 = r("oh1", [P, NT, NE], F32)
        oh2 = r("oh2", [P, NT, NE], F32)
        msk = r("msk", [P, NT, NE], F32)
        cnt = r("cnt", [P, NT, NE], F32)
        incl = r("incl", [P, NT, NE], F32)
        slm = r("slm", [P, NT, NE], F32)
        nte = r("nte", [P, 4, NE], F32)
        slf = r("slf", [P, 2, NT], F32)
        sli = r("sli", [P, 2, NT], I32)
        wts = r("wts", [P, 3, NT], F32)
        cmpJ = r("cmpJ", [1, J, NE], F32)
        teF = r("teF", [1, J], F32)
        te = r("te", [1, J], I32)
        assert r.at <= zt_at - 1600
        r = Region(m_at)
        w1s = r("w1s", [128, NE, H, F], F32)
        xtb = r("xtb", [TT, 2, D], F32)
        xtT = r("xtT", [128, 2, H, TT], F32)
        r = Region(xstart)
        h1T = r("h1T", [128, 2, FK, TT], F32)
        ytb = r("ytb", [TT, 2, D], F32)
        gat = r("gat", [P, GS, 2, D], F32)
        otb = r("otb", [P, GS, D], F32)
        xnT = r("xnT", [128, 2, H, P], F32)
        h1 = r("h1", [TT, 2, F], F32)
        assert r.at <= xstart + 25000
        r = Region(zt_at)
        zt = r("zt", [128, 2 * D], F32)
        wgs = r("wgs", [128, H, NE], F32)
        gbr = r("gbr", [1, 2, NE], F32)
        gbs = r("gbs", [1, NE], F32)
        tri = r("tri", [P, P], F32)
        iota8 = r("iota8", [P, NE], F32)
        iotaJ = r("iotaJ", [1, J], F32)
        assert r.at <= xstart

        xs = nc.dram_tensor("xs", (J * TT, D), F32, kind="Internal").ap()
        ys = nc.dram_tensor("ys", (J * TT, D), F32, kind="Internal").ap()
        r = Region(0)
        gix = r("gix", [128, U], I32)
        grow = r("grow", [128, U, 2, D], F16)
        m_dram = nc.dram_tensor("m_dram", (N, 2 * D), F16, kind="Internal").ap()
        sl_dram = nc.dram_tensor("sl_dram", (NCH * CH,), I16, kind="Internal").ap()

        s_mem = sem("s_mem")
        s_src = sem("s_src")
        s_dst = sem("s_dst")
        s_ea = sem("s_ea")
        s_tail = sem("s_tail")
        s_x = sem("s_x")
        s_edges = sem("s_edges")
        s_cmm = sem("s_cmm")
        s_tp = sem("s_tp")
        s_tpx = sem("s_tpx")
        s_minmax = sem("s_minmax")
        s_lohi = sem("s_lohi")
        s_rngp = sem("s_rngp")
        s_rng = sem("s_rng")
        s_prep = sem("s_prep")
        s_slC = sem("s_slC")
        s_sld = sem("s_sld")
        s_dv = sem("s_dv")
        s_po = sem("s_po")
        s_var = sem("s_var")
        s_std = sem("s_std")
        s_xn = sem("s_xn")
        s_xT = sem("s_xT")
        s_xTe = sem("s_xTe")
        s_oh = sem("s_oh")
        s_free = sem("s_free")
        s_cnt = sem("s_cnt")
        s_enc = sem("s_enc")
        s_nib = sem("s_nib")
        s_xf = sem("s_xf")
        s_ds = sem("s_ds")
        s_at = sem("s_at")
        s_deg = sem("s_deg")
        s_dg = sem("s_dg")
        s_bc = sem("s_bc")
        s_dB = sem("s_dB")
        s_dpart = sem("s_dpart")
        s_slr = [sem(f"s_slr{i}") for i in range(2)]
        s_ohT = sem("s_ohT")
        s_lk = sem("s_lk")
        s_lke = sem("s_lke")
        s_w12 = sem("s_w12")
        s_ohD = sem("s_ohD")
        s_freeD = sem("s_freeD")
        s_s4 = sem("s_s4")
        s_s4e = sem("s_s4e")
        s_s4T = sem("s_s4T")
        s_s4Te = sem("s_s4Te")
        s_w = sem("s_w")
        s_wfree = sem("s_wfree")
        s_wc = sem("s_wc")
        s_ewp = sem("s_ewp")
        s_ewm = sem("s_ewm")
        s_tr = sem("s_tr")
        s_hi = sem("s_hi")
        s_lo = sem("s_lo")
        s_agg = sem("s_agg")
        s_agge = sem("s_agge")
        s_mlp = sem("s_mlp")
        s_z = sem("s_z")
        s_bv = sem("s_bv")
        s_bs = sem("s_bs")
        s_bn = sem("s_bn")
        s_h = sem("s_h")
        s_ls = sem("s_ls")
        s_ez = sem("s_ez")
        s_flagp = sem("s_flagp")
        s_flag = sem("s_flag")
        s_flag2 = sem("s_flag2")
        s_md = sem("s_md")
        s_ix = sem("s_ix")
        s_gr = [[sem(f"s_gr{l}_{j}") for j in range(U)] for l in range(L)]
        s_got = sem("s_got")
        s_gi = sem("s_gi")
        s_gs = sem("s_gs")
        s_gf = sem("s_gf")
        s_gt = sem("s_gt")
        s_ge = sem("s_ge")
        s_apart = sem("s_apart")
        s_cst = sem("s_cst")
        s_zero = sem("s_zero")
        s_x2 = sem("s_x2")
        s_fw = sem("s_fw")
        s_w1 = sem("s_w1")
        s_w2 = sem("s_w2")
        s_oT = sem("s_oT")
        s_oTe = sem("s_oTe")
        s_fve = sem("s_fve")
        s_fsd = sem("s_fsd")
        s_fn = sem("s_fn")
        s_gT = sem("s_gT")
        s_gTe = sem("s_gTe")
        s_gate = sem("s_gate")
        s_gbs = sem("s_gbs")
        s_msk = sem("s_msk")
        s_rank = sem("s_rank")
        s_ex = sem("s_ex")
        s_exd = sem("s_exd")
        s_slot = sem("s_slot")
        s_sc = sem("s_sc")
        s_xt = [sem(f"s_xt{i}") for i in range(2)]
        s_xtT = sem("s_xtT")
        s_xtc = sem("s_xtc")
        s_h1 = sem("s_h1")
        s_h1b = sem("s_h1b")
        s_hT = sem("s_hT")
        s_hTc = sem("s_hTc")
        s_y = sem("s_y")
        s_yb = sem("s_yb")
        s_yst = [sem(f"s_yst{i}") for i in range(2)]
        s_ga = [sem(f"s_ga{i}") for i in range(GS)]
        s_o1 = sem("s_o1")
        s_o2 = sem("s_o2")
        s_out = [sem(f"s_out{i}") for i in range(GS)]
        s_dbg = sem("s_dbg")

        if stop == "layers":
            dbg_h = nc.dram_tensor("dbg_h", (128, H, N), F32, kind="ExternalOutput").ap()
        if stop == "build":
            dbg_at = nc.dram_tensor("dbg_at", (P, NT, N), F8, kind="ExternalOutput").ap()
            dbg_d = nc.dram_tensor("dbg_d", (128, N), F32, kind="ExternalOutput").ap()
            dbg_p = nc.dram_tensor("dbg_p", (P, NT), F32, kind="ExternalOutput").ap()
            dbg_s = nc.dram_tensor("dbg_s", (4, N), F32, kind="ExternalOutput").ap()
            dbg_h = nc.dram_tensor("dbg_h", (128, H, N), F32, kind="ExternalOutput").ap()

        block = ctx.enter_context(nc.Block())

        def tail_dmas(sp, tile, dram, width, s):
            full = (NB - 1) * CB * CH
            last = (CB - 1) * CH
            sp.dma_start(tile[:, 0:NB - 1, :], dram[0:full * width].rearrange("(b p e) -> p b e", b=NB - 1, p=CB)).then_inc(s, 16)
            sp.wait_ge(s_mem, 1)
            sp.dma_start(tile[0:CB - 1, NB - 1, :], dram[full * width:(full + last) * width].rearrange("(p e) -> p e", p=CB - 1)).then_inc(s, 16)
            rest = E - full - last
            sp.dma_start(tile[CB - 1:CB, NB - 1, 0:rest * width], dram[(full + last) * width:E * width].rearrange("(p e) -> p e", p=1)).then_inc(s, 16)

        S4_BANKS = (3, 0)

        def s4_out(dve, t):
            dve.wait_ge(s_s4, t + 1)
            dve.tensor_reduce(s4s[:, t, :], bank[S4_BANKS[t % 2]][0:P, 0:12].rearrange("p (k j) -> p j k", j=4), axis=XYZ, op=ALU.add).then_inc(s_s4e, 1)
            dve.wait_ge(s_s4e, 2 * t + 1)
            dve.tensor_scalar(s4P[:, t, :], s4s[:, t, :], dinvP[:, t:t + 1], None, ALU.mult).then_inc(s_s4e, 1)

        def dense_before(t):
            return 4 * NT + DENSE_S * max(t, 0)

        def chunk_of(first, i):
            return nc.s_assert_within(first + U * i, 0, NCH - 1, skip_runtime_bounds_check_because="a tile's turns start before its last chunk")



        def tile_turns(eng, t):
            return (eng.value_load(rng[0:1, bass.ds(t, 1)], min_val=0, max_val=MAX_FIRST),
                    eng.value_load(rng[0:1, bass.ds(NT + t, 1)], min_val=MIN_TURNS - 1, max_val=MAX_TURNS - 1),
                    eng.value_load(rng[0:1, bass.ds(2 * NT + t, 1)], min_val=0, max_val=NT * MAX_TURNS),
                    eng.value_load(rng[0:1, 3 * NT:3 * NT + 1], min_val=0, max_val=NT * MAX_TURNS))

        def gather_pool(pool):
            pool.wait_ge(s_flag, 1)
            with pool.If(pool.value_load(flag[0:1, 0:1], min_val=0, max_val=1) == 1):
                for l in range(L):
                    pool.wait_ge(s_lo, NT * (l + 1))
                    if l == 0:
                        pool.wait_ge(s_agg, H * NQ)
                    pool.dma_start(m_dram.rearrange("(t p) c -> p t c", p=P), m[:, :, :, :].rearrange("p t k c -> p t (k c)")).then_inc(s_md, 16)
                    pool.wait_ge(s_md, 16 * (l + 1))
                    with pool.Fori(0, NT) as t:
                        first, last_turn, before, total = tile_turns(pool, t)
                        with pool.Fori(0, last_turn + 1) as i:
                            n = pool.snap(l * total + before + i)
                            for j in range(U):
                                pool.wait_ge(s_gf, U * (n + total) + j + 1)
                                pool.tensor_copy(gix[:, j:j + 1], srcX[:, bass.ds(chunk_of(first, i) + j, 1)]).then_inc(s_ix, 1)
                                pool.wait_ge(s_ix, U * n + j + 1)
                                pool.sem_inc(s_apart, 1)
                                pool.indirect_dma_start(grow[:, j, :, :].rearrange("p k c -> p (k c)"), None, m_dram[:, :],
                                                        bass.IndirectOffsetOnAxis(ap=gix[:, j:j + 1], axis=0)).then_inc(s_gr[l][j], 16)
                            for j in range(U):
                                pool.wait_ge(s_gr[l][j], 16 * (before + i + 1))
                                pool.sem_inc(s_got, 1)

        def gather_dve(dve, phase, l):
            use = phase + (0 if l is None else l)
            if phase == 0:
                dve.sem_inc(s_gf, U)
                dve.sem_inc(s_ge, 1)
            dve.tensor_copy(iotaD[:, :], iotaD0[:, :]).then_inc(s_gi, 1)
            with dve.Fori(0, NT) as t:
                first, last_turn, before, total = tile_turns(dve, t)
                dve.wait_ge(s_gi, (NT + 1) * use + t + 1)
                dve.tensor_scalar(iotaD[:, :], iotaD[:, :], float(P), None, ALU.add).then_inc(s_gi, 1)
                dve.wait_ge(s_gi, (NT + 1) * use + t + 2)
                dve.sem_inc(s_apart, 1)
                with dve.Fori(0, last_turn + 1) as i:
                    n = dve.snap(use * total + before + i)
                    c = chunk_of(first, i)
                    for j in range(U):
                        dve.wait_ge(s_gf, U * n + j + 1)
                        dve.tensor_scalar(gsel[:, j, :], iotaD[:, :], dstE[:, bass.ds(c + j, 1)], None, ALU.is_equal).then_inc(s_gs, 1)
                dve.wait_ge(s_gt, NT * use + t + 1)
                if phase:
                    tile = bass.ds(t * P, P)
                    dve.tensor_tensor(aggT[:, 0, tile], bank[0][:, 0:P], dinvB[:, tile], ALU.mult)
                    dve.tensor_tensor(aggT[:, 1, tile], bank[1][:, 0:P], dinvB[:, tile], ALU.mult).then_inc(s_ge, 1)
                else:
                    dve.sem_inc(s_ge, 1)

        def gather_pe(pe, phase, l):
            use = phase + (0 if l is None else l)
            with pe.Fori(0, NT) as t:
                first, last_turn, before, total = tile_turns(pe, t)
                pe.wait_ge(s_ge, NT * use + t + 1)

                def turn(i, start, stop_):
                    n = pe.snap(use * total + before + i)
                    for j in range(U):
                        a, b = start and j == 0, stop_ and j == U - 1
                        pe.wait_ge(s_gs, U * n + j + 1)
                        if phase:
                            pe.wait_ge(s_got, U * (l * total + before + i) + j + 1)
                            for h in range(H):
                                for k in range(2):
                                    last = pe.matmul(bank[h][:, 0:P], grow[:, j, k, h * 128:(h + 1) * 128], gsel[:, j, 0:P],
                                                     start=a and k == 0, stop=b and k == 1)
                        else:
                            last = pe.matmul(bank[6][0:P, bass.ds(t, 1)], gsel[:, j, 0:P], ones16[:, :], start=a, stop=b)
                        last.then_inc(s_gt if b else s_gf, 1)
                    if stop_:
                        pe.wait_ge(s_gt, NT * use + t + 1)
                        pe.sem_inc(s_gf, 1)

                turn(0, True, False)
                with pe.Fori(1, last_turn) as i:
                    turn(i, False, False)
                turn(last_turn, False, True)
            if phase:
                pe.wait_ge(s_ge, NT * (use + 1) + 1)


        def load_layer(sp, l):
            row = lambda a: a[bass.ds(l, 1), :]
            sp.dma_start(wraw[:, :, :], mlp_w[bass.ds(l, 1), :, :].rearrange("a (k p) c -> p (a k) c", p=128)).then_inc(s_w, 16)
            with nc.allow_non_contiguous_dma(reason="a few values for each channel"):
                for n, a in enumerate((mlp_b, bn_g, bn_b)):
                    sp.dma_start(prm[:, n, :], row(a).rearrange("a (h p) -> p (a h)", p=128)).then_inc(s_w, 16)
                sp.dma_start(ewT[:, 0, 3:4], ew1[bass.ds(l, 1), :, :].rearrange("a j c -> c (a j)")).then_inc(s_w, 16)
                sp.dma_start(ewT[:, 1, 0:3], ew2[bass.ds(l, 1), :, :].rearrange("a j c -> c (a j)")).then_inc(s_w, 16)

        LOADS = 6

        def m_rows_dve(dve, base):
            for t in range(NT):
                dve.wait_ge(s_hi, base(NT) + t + 1)
                dve.scalar_tensor_tensor(m[:, t, 1, :], bank[t % 4][0:P, 0:D], dinvP[:, t:t + 1], m[:, t, 0, :],
                                         ALU.mult, ALU.subtract).then_inc(s_lo, 1)

        def m_rows_act(act, base, normalise=None):
            for t in range(NT):
                if normalise and t % (CQ // P) == 0:
                    normalise(t // (CQ // P))
                act.wait_ge(s_tr, base(NT) + t + 1)
                act.activation(m[:, t, 0, :], bank[t % 4][0:P, 0:D], ACT.Copy, scale=dinvP[:, t:t + 1]).then_inc(s_hi, 1)

        def row_pe(pe, base, prev, t):
            if prev and t % (CQ // P) == 0:
                pe.wait_ge(s_h, prev(NQ) + t // (CQ // P) + 1)
            if t >= 4:
                pe.wait_ge(s_lo, base(NT) + t - 3)
            for h in range(H):
                last = pe.transpose(bank[t % 4][0:P, h * 128:(h + 1) * 128], hT[:, h, t * P:(t + 1) * P], ident[:, :])
            last.then_inc(s_tr, 1)

        def dense(pe, g, s):
            (a, w), h = COLS[g // H], g % H
            for k in range(2):
                last = pe.matmul(bank[4 + g % 4][:, 0:w], m[:, s, k, h * 128:(h + 1) * 128], at[:, s, a:a + w],
                                 start=s == 0 and k == 0, stop=s == NT - 1 and k == 1)
            if s == NT - 1:
                last.then_inc(s_agg, 1)

        def evict(dve, base, g):
            (a, w), h = COLS[g // H], g % H
            dve.wait_ge(s_agg, base(H * NQ) + g + 1)
            dve.tensor_tensor(aggT[:, h, a:a + w], bank[4 + g % 4][:, 0:w], dinvB[:, a:a + w], ALU.mult).then_inc(s_agge, 1)

        def attributes_pe(pe, base):
            pe.wait_ge(s_wc, base(1) + 1)
            for h in range(H):
                last = pe.matmul(bank[3][0:4, 0:D], ewT[:, h, :], wraw[:, H + h, :], start=h == 0, stop=h == H - 1)
            last.then_inc(s_ewp, 1)

        def attributes_dve(dve, base):
            dve.wait_ge(s_ewp, base(1) + 1)
            dve.tensor_copy(ewm[:, :], bank[3][0:4, 0:D]).then_inc(s_ewm, 1)

        def aggregate_pe(pe, base, prev, l):
            gathers = pe.value_load(flag[0:1, 0:1], min_val=0, max_val=1)
            with pe.If(gathers == 1):
                for t in range(NT):
                    row_pe(pe, base, prev, t)
                pe.wait_ge(s_lo, base(NT) + NT)
                pe.sem_inc(s_apart, 1)
                gather_pe(pe, 1, l)
                attributes_pe(pe, base)
                pe.sem_inc(s_agg, H * NQ)
            with pe.If(gathers == 0):
                behind = 2
                for t in range(NT + behind):
                    if t < NT:
                        row_pe(pe, base, prev, t)
                    if t >= behind:
                        pe.wait_ge(s_lo, base(NT) + t - behind + 1)
                        pe.sem_inc(s_apart, 1)
                        for g in range(4):
                            dense(pe, g, t - behind)
                attributes_pe(pe, base)
                for g in range(4, H * NQ):
                    pe.wait_ge(s_agge, base(H * NQ) + g - 3)
                    pe.sem_inc(s_apart, 1)
                    for t in range(NT):
                        dense(pe, g, t)

        def linear_pe(pe, base):
            pe.wait_ge(s_ewm, base(1) + 1)
            for q, (a, w) in enumerate(COLS):
                pe.wait_ge(s_agge, base(H * NQ) + H * (q + 1))
                if q >= 2:
                    pe.wait_ge(s_z, base(NQ) + q - 1)
                for h in range(H):
                    o = bank[2 * (q % 2) + h][:, 0:w]
                    for k in range(2 * H):
                        rhs = (hT if k < H else aggT)[:, k % H, a:a + w]
                        pe.matmul(o, wcur[:, k, h * 128:(h + 1) * 128], rhs, start=k == 0, stop=False)
                    last = pe.matmul(o, ewm[:, h * 128:(h + 1) * 128], s4T[:, a:a + w], start=False, stop=True)
                last.then_inc(s_mlp, 1)

        def weights_dve(dve, loads, l):
            dve.wait_ge(s_w, 16 * loads)
            for k in range(2 * H):
                last = dve.tensor_scalar(wcur[:, k, :], wraw[:, k, :], inv[:, k % H:k % H + 1], None, ALU.mult)
            last.then_inc(s_wc, 1)

        def aggregate_dve(dve, base, l, loads):
            m_rows_dve(dve, base)
            weights_dve(dve, loads, l)
            gathers = dve.value_load(flag[0:1, 0:1], min_val=0, max_val=1)
            with dve.If(gathers == 1):
                gather_dve(dve, 1, l)
                attributes_dve(dve, base)
                dve.sem_inc(s_agge, H * NQ)
            with dve.If(gathers == 0):
                for g in range(H * NQ):
                    evict(dve, base, g)
                    if g == 3:
                        attributes_dve(dve, base)

        def statistics_dve(dve, base, last_layer):
            count = [0]

            def step(ins):
                count[0] += 1
                ins.then_inc(s_ls, 1)
                dve.wait_ge(s_ls, base(LAYER_STEPS) + count[0])

            for q, (a, w) in enumerate(COLS):
                dve.wait_ge(s_z, base(NQ) + q + 1)
                for h in range(H):
                    last = dve.bn_stats(zst[:, h, q, :], hT[:, h, a:a + w])
            step(last)
            dve.sem_inc(s_apart, 1)
            for h in range(H):
                last = dve.bn_aggr(zmv[:, h, :], zst[:, h, :, :].rearrange("p q s -> p (q s)"))
            step(last)
            gain, offset = prm[:, 1, :], prm[:, 2, :]
            ve, sd, rt, tmp = (cf[:, n, :] for n in (0, 1, 2, 3))
            dve.tensor_scalar(ve, zmv[:, :, 1], BN_EPS, None, ALU.add).then_inc(s_bv, 1)
            dve.wait_ge(s_bs, base(1) + 1)
            step(dve.reciprocal(rt, sd))
            step(dve.tensor_tensor(tmp, rt, rt, ALU.mult))
            step(dve.tensor_tensor(tmp, tmp, ve, ALU.mult))
            step(dve.tensor_scalar(tmp, tmp, -0.5, 1.5, ALU.mult, ALU.add))
            step(dve.tensor_tensor(rt, rt, tmp, ALU.mult))
            slope, shift = cf[:, 4, :], cf[:, 5, :]
            step(dve.tensor_tensor(slope, rt, gain, ALU.mult))
            step(dve.tensor_tensor(tmp, zmv[:, :, 0], slope, ALU.mult))
            step(dve.tensor_tensor(shift, offset, tmp, ALU.subtract))
            if not last_layer:
                step(dve.scalar_tensor_tensor(tmp, gain, -1.0, gain, ALU.mult, ALU.max))
                step(dve.scalar_tensor_tensor(sd, offset, -1.0, offset, ALU.mult, ALU.max))
                step(dve.scalar_tensor_tensor(tmp, tmp, 56.0, sd, ALU.mult, ALU.add))
                step(dve.tensor_scalar(tmp, tmp, 2.0 ** -80, 2.0 ** 100, ALU.max, ALU.min))
                step(dve.tensor_scalar(cfi[:, 0, :], tmp.bitcast(I32), 0x7F800000, None, ALU.bitwise_and))
                step(dve.tensor_scalar(cfi[:, 1, :], cfi[:, 0, :], -1.0, float((254 + 14) << 23), ALU.mult, ALU.add))
                step(dve.tensor_scalar(inv[:, :].bitcast(I32), cfi[:, 0, :], float(-(14 << 23)), None, ALU.add))
                step(dve.tensor_tensor(slope, slope, cfi[:, 1, :].bitcast(F32), ALU.mult))
                step(dve.tensor_tensor(shift, shift, cfi[:, 1, :].bitcast(F32), ALU.mult))
                assert count[0] == LAYER_STEPS, count
            dve.sem_inc(s_bn, 1)

        def normalise_act(act, prev, last_layer):
            def normalise(q):
                if q == 0:
                    act.wait_ge(s_bn, prev(1) + 1)
                a, w = COLS[q]
                for h in range(H):
                    last = act.activation(hT[:, h, a:a + w], hT[:, h, a:a + w], ACT.Identity if last_layer else ACT.Relu,
                                          bias=cf[:, 5, h:h + 1], scale=cf[:, 4, h:h + 1])
                last.then_inc(s_h, 1)
            return normalise

        def linear_act(act, base):
            for q, (a, w) in enumerate(COLS):
                act.wait_ge(s_mlp, base(NQ) + q + 1)
                for h in range(H):
                    last = act.activation(hT[:, h, a:a + w], bank[2 * (q % 2) + h][:, 0:w], ACT.Relu, bias=prm[:, 0, h:h + 1])
                last.then_inc(s_z, 1)
            act.wait_ge(s_bv, base(1) + 1)
            act.activation(cf[:, 1, :], cf[:, 0, :], ACT.Sqrt).then_inc(s_bs, 1)

        LAYER_STEPS = 19



        def experts_sp(sp):
            sp.wait_ge(s_agg, L * H * NQ)
            sp.dma_start(x2[:, :, :], x.rearrange("(t p) d -> p t d", p=P)).then_inc(s_x2, 16)
            sp.dma_start(b1B[:, :, :], b1.rearrange("(a e) f -> a e f", a=1).to_broadcast([128, NE, F])).then_inc(s_fw, 16)
            sp.dma_start(b2B[:, :, :], b2.rearrange("(a e) f -> a e f", a=1).to_broadcast([128, NE, D])).then_inc(s_fw, 16)
            sp.wait_ge(s_h, L * NQ)
            sp.dma_start(w1s[:, :, :, :].rearrange("p e k f -> p (e k) f"), w1.rearrange("e (k p) f -> p (e k) f", p=128)).then_inc(s_w1, 16)
            sp.wait_ge(s_oT, NT)
            sp.dma_start(w2s[:, :, :, :].rearrange("p e k d -> p (e k) d"), w2.rearrange("e (k p) d -> p (e k) d", p=128)).then_inc(s_w2, 16)
            sp.wait_ge(s_sc, 16 * 2 * NT)
            xst_ = xs.rearrange("(j p) d -> p j d", p=TT)
            yst_ = ys.rearrange("(j p) d -> p j d", p=TT)
            for u in range(2):
                sp.dma_start(xtb[:, u, :], xst_[:, u, :]).then_inc(s_xt[u], 16)

            def store(j, u):
                sp.wait_ge(s_yb, j + 1)
                sp.dma_start(yst_[:, bass.ds(j, 1), :].rearrange("p a d -> p (a d)"), ytb[:, u, :]).then_inc(s_yst[u], 16)

            with sp.Fori(0, J // 2 - 1) as i:
                for u in range(2):
                    j = sp.snap(2 * i + u)
                    sp.wait_ge(s_xtT, j + 1)
                    sp.dma_start(xtb[:, u, :], xst_[:, bass.ds(j + 2, 1), :].rearrange("p a d -> p (a d)")).then_inc(s_xt[u], 16)
                    store(j, u)
            for u in range(2):
                store(J - 2 + u, u)
            for t in range(NT):
                sp.wait_ge(s_o2, t + 1)
                sp.dma_start(out[t * P:(t + 1) * P, :], otb[:, t % GS, :]).then_inc(s_out[t % GS], 16)
            for g in range(GS):
                sp.wait_ge(s_out[g], 16 * ((NT - g + GS - 1) // GS))

        def experts_pool(pool):
            pool.wait_ge(s_zero, 16 * (J // 4))
            pool.wait_ge(s_slot, 1)
            for t in range(NT):
                for n in range(2):
                    pool.indirect_dma_start(xs[:, :], bass.IndirectOffsetOnAxis(ap=sli[:, n, t:t + 1], axis=0), xn[:, t, :], None).then_inc(s_sc, 16)
            for u in range(2):
                pool.wait_ge(s_yst[u], 16 * (J // 2))
            for t in range(NT):
                if t >= GS:
                    pool.wait_ge(s_o2, t - GS + 1)
                for n in range(2):
                    pool.indirect_dma_start(gat[:, t % GS, n, :], None, ys[:, :], bass.IndirectOffsetOnAxis(ap=sli[:, n, t:t + 1], axis=0)).then_inc(s_ga[t % GS], 16)

        def experts_act(act):
            act.wait_ge(s_fve, 1)
            act.activation(fsd[:, :], fve[:, :], ACT.Sqrt).then_inc(s_fsd, 1)
            for t in range(NT):
                act.wait_ge(s_gT, t + 1)
                act.activation(xnT[:, t % 2, :, :], bank[4 + t % 2][:, 0:H * P].rearrange("p (h n) -> p h n", h=H), ACT.Copy).then_inc(s_gTe, 1)
            act.wait_ge(s_ex, 1)
            act.activation(wts[:, 1, :], wts[:, 0, :], ACT.Exp).then_inc(s_exd, 1)

            def rows(j, u):
                act.wait_ge(s_xtT, j + 1)
                act.activation(xtT[:, u, :, :], bank[u][:, 0:H * TT].rearrange("p (h n) -> p h n", h=H), ACT.Copy).then_inc(s_xtc, 1)

            def hidden(j, u):
                act.wait_ge(s_hT, j + 1)
                act.activation(h1T[:, u, :, :], bank[4 + u][:, 0:FK * TT].rearrange("p (h n) -> p h n", h=FK), ACT.Relu).then_inc(s_hTc, 1)

            rows(0, 0)
            with act.Fori(0, J // 2 - 1) as i:
                for u in range(2):
                    j = act.snap(2 * i + u)
                    rows(j + 1, 1 - u)
                    hidden(j, u)
            rows(J - 1, 1)
            hidden(J - 2, 0)
            hidden(J - 1, 1)

        def experts_dve(dve, step, rounded, inverse_root):
            dve.wait_ge(s_x2, 16)
            for t in range(NT):
                dve.wait_ge(s_oT, t + 1)
                dve.tensor_tensor(x2[:, t, :], x2[:, t, :], bank[t % 4][0:P, 0:D], ALU.add).then_inc(s_oTe, 1)
                if t:
                    dve.wait_ge(s_oTe, t)
                    dve.bn_stats(fst[:, t - 1, :], x2[:, t - 1, :])
            dve.wait_ge(s_oTe, NT)
            step(dve.bn_stats(fst[:, NT - 1, :], x2[:, NT - 1, :]))
            for t in range(NT):
                last = dve.bn_aggr(fmv[:, t, :], fst[:, t, :])
            step(last)
            dve.tensor_scalar(fve[:, :], fmv[:, :, 1], LN_EPS, None, ALU.add).then_inc(s_fve, 1)
            dve.wait_ge(s_fsd, 1)
            inverse_root(frs[:, :], fve[:, :], fsd[:, :], ft1[:, :])
            dve.wait_ge(s_fw, 16 * 5)
            dve.tensor_tensor(gbs[:, :], gbr[:, 0, :], gbr[:, 1, :], ALU.add).then_inc(s_gbs, 1)
            for t in range(NT):
                dve.tensor_scalar(xn[:, t, :], x2[:, t, :], fmv[:, t, 0:1], frs[:, t:t + 1], ALU.subtract, ALU.mult).then_inc(s_fn, 1)
            dve.wait_ge(s_cst, 2)
            dve.wait_ge(s_gate, 1)
            step(dve.tensor_copy(lgt[:, :, :].rearrange("p t e -> p (t e)"), bank[6][0:P, 0:NT * NE]))
            for t in range(NT):
                last = dve.max(top[:, t, :], lgt[:, t, :])
            step(last)
            for t in range(NT):
                last = dve.max_index(tix[:, t, :], top[:, t, :], lgt[:, t, :])
            step(last)
            dve.tensor_tensor(wts[:, 0, :], top[:, :, 1], top[:, :, 0], ALU.subtract).then_inc(s_ex, 1)
            step(dve.tensor_copy(ef[:, 0, :], tix[:, :, 0]))
            step(dve.tensor_copy(ef[:, 1, :], tix[:, :, 1]))
            by8 = iota8[:, :].unsqueeze(1).to_broadcast([P, NT, NE])
            for n, o in enumerate((oh1, oh2)):
                step(dve.tensor_tensor(o[:, :, :], ef[:, n, :].unsqueeze(2).to_broadcast([P, NT, NE]), by8, ALU.is_equal))
            dve.tensor_tensor(msk[:, :, :], oh1[:, :, :], oh2[:, :, :], ALU.add).then_inc(s_msk, 1)
            dve.wait_ge(s_exd, 1)
            step(dve.tensor_scalar(wts[:, 0, :], wts[:, 1, :], 1.0, None, ALU.add))
            step(dve.reciprocal(wts[:, 2, :], wts[:, 0, :]))
            step(dve.tensor_tensor(wts[:, 1, :], wts[:, 1, :], wts[:, 2, :], ALU.mult))
            dve.wait_ge(s_rank, 1)
            step(dve.tensor_copy(cnt[:, :, :].rearrange("p t e -> p (t e)"), bank[1][0:P, 0:NT * NE]))
            for e in range(NE):
                last = dve.tensor_tensor_scan(incl[:, :, e], ones[0:P, 0:NT], cnt[:, :, e], 0.0, ALU.mult, ALU.add)
            step(last)
            total, tiles, end, spare = (nte[:, n, :] for n in range(4))
            step(dve.tensor_scalar(total, incl[:, NT - 1, :], 1.0 / TT, (TT - 1) / (2 * TT), ALU.mult, ALU.add))
            rounded(tiles, total, spare)
            step(dve.tensor_tensor_scan(end, ones[0:P, 0:NE], tiles, 0.0, ALU.mult, ALU.add))
            step(dve.tensor_tensor(spare, end, tiles, ALU.subtract))
            step(dve.tensor_scalar(spare, spare, float(TT), None, ALU.mult))
            step(dve.tensor_tensor(slm[:, :, :], incl[:, :, :], cnt[:, :, :], ALU.subtract))
            step(dve.tensor_tensor(slm[:, :, :].rearrange("p t e -> p (t e)"), slm[:, :, :].rearrange("p t e -> p (t e)"), bank[0][0:P, 0:NT * NE], ALU.add))
            step(dve.tensor_tensor(slm[:, :, :], slm[:, :, :], spare.unsqueeze(1).to_broadcast([P, NT, NE]), ALU.add))
            for n, o in enumerate((oh1, oh2)):
                step(dve.tensor_tensor(o[:, :, :], o[:, :, :], slm[:, :, :], ALU.mult))
                step(dve.tensor_reduce(slf[:, n, :], o[:, :, :], axis=XYZ, op=ALU.add))
            step(dve.tensor_copy(sli[:, :, :], slf[:, :, :]))
            step(dve.tensor_tensor(cmpJ[:, :, :], nte[0:1, 2, :].unsqueeze(1).to_broadcast([1, J, NE]),
                                   iotaJ[:, :].unsqueeze(2).to_broadcast([1, J, NE]), ALU.is_le))
            step(dve.tensor_reduce(teF[:, :], cmpJ[:, :, :], axis=XYZ, op=ALU.add))
            dve.tensor_scalar(te[:, :], teF[:, :], float(NE - 1), None, ALU.min).then_inc(s_slot, 1)
            dve.wait_ge(s_slot, 1)

            def hidden(j, u):
                e = dve.value_load(te[0:1, bass.ds(j, 1)], min_val=0, max_val=NE - 1)
                dve.wait_ge(s_h1, j + 1)
                dve.tensor_tensor(h1[:, u, :], bank[2 + u][:, :], b1B[:, bass.ds(e, 1), :].rearrange("p a f -> p (a f)"), ALU.add).then_inc(s_h1b, 1)

            def result(j, u, stores):
                e = dve.value_load(te[0:1, bass.ds(j, 1)], min_val=0, max_val=NE - 1)
                dve.wait_ge(s_y, j + 1)
                if stores is not None:
                    dve.wait_ge(s_yst[u], stores)
                dve.tensor_tensor(ytb[:, u, :], bank[6 + u][:, 0:D], b2B[:, bass.ds(e, 1), :].rearrange("p a f -> p (a f)"), ALU.add).then_inc(s_yb, 1)

            hidden(0, 0)
            hidden(1, 1)
            result(0, 0, None)
            hidden(2, 0)
            result(1, 1, None)
            with dve.Fori(1, J // 2 - 1) as i:
                hidden(2 * i + 1, 1)
                result(2 * i, 0, 16 * i)
                hidden(2 * i + 2, 0)
                result(2 * i + 1, 1, 16 * i)
            hidden(J - 1, 1)
            result(J - 2, 0, 16 * (J // 2 - 1))
            result(J - 1, 1, 16 * (J // 2 - 1))
            for t in range(NT):
                dve.wait_ge(s_ga[t % GS], 32 * (t // GS + 1))
                dve.scalar_tensor_tensor(x2[:, t, :], gat[:, t % GS, 0, :], wts[:, 2, t:t + 1], x2[:, t, :], ALU.mult, ALU.add).then_inc(s_o1, 1)
                dve.wait_ge(s_o1, t + 1)
                if t >= GS:
                    dve.wait_ge(s_out[t % GS], 16 * (t // GS))
                dve.scalar_tensor_tensor(otb[:, t % GS, :], gat[:, t % GS, 1, :], wts[:, 1, t:t + 1], x2[:, t, :], ALU.mult, ALU.add).then_inc(s_o2, 1)

        def experts_pe(pe):
            for t in range(NT):
                if t % (CQ // P) == 0:
                    pe.wait_ge(s_h, NQ * (L - 1) + t // (CQ // P) + 1)
                if t >= 4:
                    pe.wait_ge(s_oTe, t - 3)
                for h in range(H):
                    last = pe.transpose(bank[t % 4][0:P, h * 128:(h + 1) * 128], hT[:, h, t * P:(t + 1) * P], ident[:, :])
                last.then_inc(s_oT, 1)

            def rows_up(t):
                pe.wait_ge(s_fn, t + 1)
                for h in range(H):
                    last = pe.transpose(bank[4 + t % 2][:, h * P:(h + 1) * P], xn[:, t, h * 128:(h + 1) * 128], ident[0:P, 0:P])
                last.then_inc(s_gT, 1)

            rows_up(0)
            pe.wait_ge(s_gbs, 1)
            for t in range(NT):
                if t + 1 < NT:
                    rows_up(t + 1)
                pe.wait_ge(s_gTe, t + 1)
                o = bank[6][0:P, t * NE:(t + 1) * NE]
                for h in range(H):
                    pe.matmul(o, xnT[:, t % 2, h, :], wgs[:, h, :], start=h == 0, stop=False)
                last = pe.matmul(o, ones[0:1, 0:P], gbs[:, :], start=False, stop=True)
            last.then_inc(s_gate, 1)
            pe.wait_ge(s_msk, 1)
            flat = msk[:, :, :].rearrange("p t e -> p (t e)")
            pe.matmul(bank[0][0:P, 0:NT * NE], tri[:, :], flat, start=True, stop=True)
            pe.matmul(bank[1][0:P, 0:NT * NE], ones[0:P, 0:P], flat, start=True, stop=True).then_inc(s_rank, 1)
            pe.wait_ge(s_slot, 1)
            pe.wait_ge(s_w1, 16)
            pe.wait_ge(s_w2, 16)

            def rows(i, j, u):
                pe.wait_ge(s_xt[u], 16 * (i + 1))
                for h in range(H):
                    last = pe.transpose(bank[u][:, h * TT:(h + 1) * TT], xtb[:, u, h * 128:(h + 1) * 128], ident[:, :])
                last.then_inc(s_xtT, 1)

            def up(j, u):
                e = pe.value_load(te[0:1, bass.ds(j, 1)], min_val=0, max_val=NE - 1)
                pe.wait_ge(s_xtc, j + 1)
                for h in range(H):
                    last = pe.matmul(bank[2 + u][:, :], xtT[:, u, h, :], w1s[:, bass.ds(e, 1), h, :].rearrange("p a f -> p (a f)"), start=h == 0, stop=h == H - 1)
                last.then_inc(s_h1, 1)

            def across(j, u):
                pe.wait_ge(s_h1b, j + 1)
                for k in range(FK):
                    last = pe.transpose(bank[4 + u][:, k * TT:(k + 1) * TT], h1[:, u, k * 128:(k + 1) * 128], ident[:, :])
                last.then_inc(s_hT, 1)

            def down(j, u, free):
                e = pe.value_load(te[0:1, bass.ds(j, 1)], min_val=0, max_val=NE - 1)
                pe.wait_ge(s_hTc, j + 1)
                if free is not None:
                    pe.wait_ge(s_yb, free)
                for k in range(FK):
                    last = pe.matmul(bank[6 + u][:, 0:D], h1T[:, u, k, :], w2s[:, bass.ds(e, 1), k, :].rearrange("p a f -> p (a f)"), start=k == 0, stop=k == FK - 1)
                last.then_inc(s_y, 1)

            rows(0, 0, 0)
            up(0, 0)
            rows(0, 1, 1)
            across(0, 0)
            up(1, 1)
            down(0, 0, None)
            rows(1, 2, 0)
            across(1, 1)
            up(2, 0)
            down(1, 1, None)
            rows(1, 3, 1)
            across(2, 0)
            with pe.Fori(1, J // 2 - 1) as i:
                j = pe.snap(2 * i)
                up(j + 1, 1)
                down(j, 0, j - 1)
                rows(i + 1, j + 2, 0)
                across(j + 1, 1)
                up(j + 2, 0)
                down(j + 1, 1, j)
                rows(i + 1, j + 3, 1)
                across(j + 2, 0)
            up(J - 1, 1)
            down(J - 2, 0, J - 3)
            across(J - 1, 1)
            down(J - 1, 1, J - 2)

        @block.sync
        def _(sp):
            tail_dmas(sp, dstI, dst, 1, s_dst)
            tail_dmas(sp, srcI, src, 1, s_src)
            tail_dmas(sp, eaC, edge_attr.rearrange("e j -> (e j)"), 4, s_ea)
            sp.dma_start(xin[:, :, :], x.rearrange("(t p) d -> p t d", p=P)).then_inc(s_x, 16)
            sp.wait_ge(s_cst, 1)
            xz = xs.rearrange("(p r) d -> p (r d)", p=128)
            for k in range(J // 2 // 2):
                sp.dma_start(xz[:, k * 4 * D:(k + 1) * 4 * D].rearrange("p (a c) -> p a c", a=2),
                             zt[:, :].unsqueeze(1).to_broadcast([128, 2, 2 * D])).then_inc(s_zero, 16)
            sp.dma_start(wgs[:, :, :], wg.rearrange("(h p) e -> p h e", p=128)).then_inc(s_fw, 16)
            sp.dma_start(gbr[:, 0, :], bg.rearrange("(a e) -> a e", a=1)).then_inc(s_fw, 16)
            sp.dma_start(gbr[:, 1, :], gbias.rearrange("(a e) -> a e", a=1)).then_inc(s_fw, 16)
            sp.wait_ge(s_slC, 1)
            sp.dma_start(sl_dram.rearrange("(b p e) -> p b e", b=NB, p=CB), slC[:, :, :]).then_inc(s_sld, 16)
            sp.wait_ge(s_sld, 16)
            sp.wait_ge(s_dpart, 1)
            row = sl_dram.rearrange("(b e) -> b e", b=NLB)
            for b in range(NLB):
                if b >= 2:
                    sp.wait_ge(s_ohT, b - 1)
                sp.dma_start(slrow[:, b % 2, :], row[b:b + 1, :].to_broadcast([P, LB * CH])).then_inc(s_slr[b % 2], 16)
            sp.wait_ge(s_s4, NT)
            sp.wait_ge(s_ez, 1)
            load_layer(sp, 0)
            with sp.Fori(1, L) as l:
                sp.wait_ge(s_bn, l)
                load_layer(sp, l)
            if stop is None:
                experts_sp(sp)
            if stop == "layers":
                sp.wait_ge(s_h, NQ * L)
                sp.dma_start(dbg_h, hT[:, :, :]).then_inc(s_dbg, 16)
                sp.wait_ge(s_dbg, 16)
            if stop == "build":
                sp.dma_start(dbg_at, at[:, :, :]).then_inc(s_dbg, 16)
                sp.dma_start(dbg_d, dinvB[:, :]).then_inc(s_dbg, 16)
                sp.dma_start(dbg_p, dinvP[:, :]).then_inc(s_dbg, 16)
                sp.dma_start(dbg_s, s4T[:, :]).then_inc(s_dbg, 16)
                sp.dma_start(dbg_h, hT[:, :, :]).then_inc(s_dbg, 16)
                sp.wait_ge(s_dbg, 80)

        @block.gpsimd
        def _(pool):
            done = [0]

            def step(ins):
                done[0] += 1
                ins.then_inc(s_po, 1)
                pool.wait_ge(s_po, done[0])

            pool.memset(dstI[:, NB - 1, :], DST_PAD)
            pool.memset(srcI[:, NB - 1, :], 0)
            pool.memset(eaC[:, NB - 1, :], 0.0).then_inc(s_mem, 1)
            step(pool.memset(ident[:, :], 0.0))
            pool.affine_select(out=ident[:, :], in_=ident[:, :], compare_op=ALU.not_equal, fill=1.0, base=0,
                               pattern=[[-1, 128]], channel_multiplier=1)
            pool.memset(ones[:, :], 1.0)
            pool.memset(ones16[:, :], 1.0)
            pool.iota(cidx[:, :], pattern=[[1, NCH]], base=0, channel_multiplier=0, allow_small_or_imprecise_dtypes=True)
            pool.iota(tlo[:, :], pattern=[[0, 1]], base=0, channel_multiplier=P, allow_small_or_imprecise_dtypes=True)
            pool.iota(iotaP[:, :], pattern=[[0, 1]], base=0, channel_multiplier=1, allow_small_or_imprecise_dtypes=True)
            pool.iota(iotaK[:, 0:GROUPS * P], pattern=[[KEY, GROUPS], [1, P]], base=0, channel_multiplier=0)
            pool.memset(iotaK[:, GROUPS * P:GW], -32000)
            pool.iota(iotaS[:, :, :], pattern=[[1, 128], [0, HU]], base=0, channel_multiplier=0)
            pool.iota(iotaD3[:, :, :], pattern=[[1, P], [0, HU]], base=-P, channel_multiplier=0)
            pool.iota(iotaD0[:, :], pattern=[[1, P + 1]], base=-P, channel_multiplier=0)
            pool.iota(iota25[:, :], pattern=[[1, NT]], base=0, channel_multiplier=0).then_inc(s_mem, 1)
            pool.memset(zt[:, :], 0.0).then_inc(s_cst, 1)
            step(pool.memset(tri[:, :], 1.0))
            pool.affine_select(out=tri[:, :], in_=tri[:, :], compare_op=ALU.is_gt, fill=0.0, base=0,
                               pattern=[[1, P]], channel_multiplier=-1)
            pool.iota(iota8[:, :], pattern=[[1, NE]], base=0, channel_multiplier=0, allow_small_or_imprecise_dtypes=True)
            pool.iota(iotaJ[:, :], pattern=[[1, J]], base=0, channel_multiplier=0, allow_small_or_imprecise_dtypes=True).then_inc(s_cst, 1)
            gather_pool(pool)
            if stop is None:
                experts_pool(pool)

        @block.vector
        def _(dve):
            done = [0]

            def step(ins):
                done[0] += 1
                ins.then_inc(s_dv, 1)
                dve.wait_ge(s_dv, done[0])

            def inverse_root(root, v, sd, tmp):
                step(dve.reciprocal(root, sd))
                step(dve.tensor_tensor(tmp, root, root, ALU.mult))
                step(dve.tensor_tensor(tmp, tmp, v, ALU.mult))
                step(dve.tensor_scalar(tmp, tmp, -0.5, 1.5, ALU.mult, ALU.add))
                step(dve.tensor_tensor(root, root, tmp, ALU.mult))

            def rounded(dst_ap, src_ap, tmp):
                step(dve.tensor_scalar(tmp, src_ap, MAGIC, None, ALU.add))
                step(dve.tensor_scalar(dst_ap, tmp, MAGIC, None, ALU.subtract))

            dve.wait_ge(s_mem, 2)
            dve.wait_ge(s_dst, 48)
            dve.tensor_copy(dstC[:, :, :], dstI[:, :, :]).then_inc(s_edges, 1)
            dve.wait_ge(s_src, 48)
            dve.tensor_copy(srcC[:, :, :], srcI[:, :, :]).then_inc(s_edges, 1)
            dve.wait_ge(s_edges, 2)
            dve.tensor_reduce(cmm[:, 0, :], dstC[:, :, :], axis=XYZ, op=ALU.min)
            step(dve.tensor_reduce(cmm[:, 1, :], dstC[:, :, :], axis=XYZ, op=ALU.max))
            dve.tensor_copy(cmmB[:, :, :], cmm[:, :, :].rearrange("p a b -> p (a b)").unsqueeze(2).to_broadcast([CB, 2 * NB, NT])).then_inc(s_cmm, 1)
            sc = srcC[:, :, :].rearrange("p b e -> p (b e)")
            step(dve.tensor_scalar(ta[0:CB, :], sc, float(-(P // 2)), 1.0 / P, ALU.add, ALU.mult))
            rounded(tb[0:CB, :], ta[0:CB, :], ta[0:CB, :])
            dve.scalar_tensor_tensor(slC[:, :, :].rearrange("p b e -> p (b e)"), tb[0:CB, :], float(-P), sc, ALU.mult, ALU.add).then_inc(s_slC, 1)
            dve.wait_ge(s_tp, 8)
            srcE = ta[:, 0:NCH]
            step(dve.memset(srcX[:, NCH:NCHP], 0))
            step(dve.tensor_copy(srcX[:, 0:NCH], bank[1][:, 0:NCH]))
            tileE = tb[:, 0:NCH]
            step(dve.memset(dstE[:, NCH:NCHP], float(DST_PAD)))
            step(dve.memset(keyE[:, NCH:NCHP], float(DST_PAD)))
            step(dve.memset(powE[:, NCH:NCHP], 0))
            step(dve.memset(sl16[:, NCH:NCHP], 0))
            step(dve.memset(dst3[:, NCH:NCHP], DST_PAD))
            step(dve.tensor_copy(dst3[:, 0:NCH], bank[0][:, 0:NCH]))
            step(dve.tensor_copy(dstE[:, 0:NCH], bank[0][:, 0:NCH]))
            step(dve.tensor_copy(srcE, bank[1][:, 0:NCH]))
            step(dve.tensor_scalar(tg[:, :], srcE, float(-(P // 2)), 1.0 / P, ALU.add, ALU.mult))
            rounded(tileE, tg[:, :], tg[:, :])
            step(dve.scalar_tensor_tensor(sl16[:, 0:NCH], tileE, float(-P), srcE, ALU.mult, ALU.add))
            step(dve.tensor_copy(s16[:, :], tileE))
            step(dve.tensor_scalar(srcE, tileE, -(FIELDS - 1) / 2, 1.0 / FIELDS, ALU.add, ALU.mult))
            rounded(tg[:, :], srcE, srcE)
            step(dve.scalar_tensor_tensor(keyE[:, 0:NCH], tg[:, :], float(KEY), dstE[:, 0:NCH], ALU.mult, ALU.add))
            step(dve.scalar_tensor_tensor(srcE, tg[:, :], float(-FIELDS), tileE, ALU.mult, ALU.add))
            step(dve.tensor_scalar(srcE, srcE, 4.0, 127.0, ALU.mult, ALU.add))
            step(dve.tensor_scalar(powE[:, 0:NCH], srcE, float(2 ** 23), None, ALU.mult))
            dve.wait_ge(s_tp, 12)
            for j in range(4):
                dve.wait_ge(s_tp, 9 + j)
                dve.tensor_copy(eaE[:, :, j], bank[2 + j][:, 0:NCH])
            dve.wait_ge(s_minmax, 2)
            step(dve.tensor_scalar(lohi2[:, 0:1], tlo[:, :], float(P - 1), None, ALU.add))
            step(dve.tensor_scalar(m1[:, :], bank[6][0:NT, 0:NCH], lohi2[:, 0:1], None, ALU.is_le))
            step(dve.tensor_scalar(m2[:, :], bank[7][0:NT, 0:NCH], tlo[:, :], None, ALU.is_ge))
            step(dve.tensor_tensor(m1[:, :], m1[:, :], m2[:, :], ALU.mult))
            step(dve.scalar_tensor_tensor(m2[:, :], m1[:, :], -BIG, cidx[:, :], ALU.mult, ALU.add))
            step(dve.tensor_reduce(lohi[:, 0:1], m2[:, :], axis=XYZ, op=ALU.min))
            step(dve.scalar_tensor_tensor(m2[:, :], cidx[:, :], 1.0, m1[:, :], ALU.add, ALU.mult))
            step(dve.tensor_reduce(lohi[:, 1:2], m2[:, :], axis=XYZ, op=ALU.max))
            step(dve.tensor_scalar(lohi2[:, 0:1], lohi[:, 0:1], BIG, float(MAX_FIRST), ALU.add, ALU.min))
            step(dve.tensor_tensor(lohi[:, 1:2], lohi[:, 1:2], lohi2[:, 0:1], ALU.subtract))
            step(dve.tensor_scalar(lohi[:, 1:2], lohi[:, 1:2], 1.0 / U, (U - 1) / (2 * U) - 1.0, ALU.mult, ALU.add))
            rounded(lohi2[:, 1:2], lohi[:, 1:2], lohi[:, 1:2])
            dve.tensor_scalar(lohi2[:, 1:2], lohi2[:, 1:2], float(MIN_TURNS - 1), None, ALU.max).then_inc(s_lohi, 1)
            dve.wait_ge(s_rngp, 1)
            row = rngf[:, :, :].rearrange("p a t -> p (a t)")
            step(dve.tensor_copy(row[:, 0:2 * NT], bank[0][0:1, 0:2 * NT]))
            step(dve.tensor_copy(rng[:, 0:2 * NT], row[:, 0:2 * NT]))
            step(dve.tensor_scalar(rngf[:, 0, :], rngf[:, 1, :], 1.0, None, ALU.add))
            step(dve.tensor_tensor_scan(rngf[:, 2, :], ones[0:1, 0:NT], rngf[:, 0, :], 0.0, ALU.mult, ALU.add))
            step(dve.tensor_copy(rng[:, 3 * NT:3 * NT + 1], rngf[:, 2, NT - 1:NT]))
            dve.tensor_tensor(rng[:, 2 * NT:3 * NT], rngf[:, 2, :], rngf[:, 0, :], ALU.subtract).then_inc(s_rng, 1)
            dve.wait_ge(s_x, 16)
            for t in range(NT):
                last = dve.bn_stats(xst[:, t, :], xin[:, t, :])
            step(last)
            for t in range(NT):
                last = dve.bn_aggr(xmv[:, t, :], xst[:, t, :])
            step(last)
            dve.tensor_scalar(xve[:, :], xmv[:, :, 1], LN_EPS, None, ALU.add).then_inc(s_var, 1)
            dve.wait_ge(s_std, 1)
            inverse_root(xrs[:, :], xve[:, :], xsd[:, :], xt1[:, :])
            step(dve.tensor_scalar(xrs[:, :], xrs[:, :], float(2 ** H0_EXP), None, ALU.mult))
            dve.scalar_tensor_tensor(xsh[:, :], xmv[:, :, 0], -1.0, xrs[:, :], ALU.mult, ALU.mult).then_inc(s_xf, 1)

            dve.wait_ge(s_rng, 1)
            dve.wait_ge(s_xf, 1)
            dve.sem_inc(s_free, 2)
            dve.sem_inc(s_freeD, 2)
            turns_before = 0
            for t in range(NT + 1):
                if t < NT:
                    first = dve.value_load(rng[0:1, t:t + 1], min_val=0, max_val=MAX_FIRST)
                    last_turn = dve.value_load(rng[0:1, NT + t:NT + t + 1], min_val=MIN_TURNS - 1, max_val=MAX_TURNS - 1)
                    if t:
                        step(dve.tensor_scalar(iotaK[:, :], iotaK[:, :], float(P), None, ALU.add))
                    with dve.Fori(0, last_turn + 1) as i:
                        k = dve.snap(2 * (turns_before + i))
                        c = dve.snap(chunk_of(first, i))
                        for half in range(2):
                            dve.wait_ge(s_free, k + half + 1)
                            dve.tensor_tensor(ohS[:, half, :, :], iotaS[:, :, :],
                                              sl16[:, bass.ds(c + half * HU, HU)].unsqueeze(1).to_broadcast([128, 128, HU]), ALU.is_equal)
                            for j in range(half * HU, (half + 1) * HU):
                                last = dve.tensor_scalar(cnt1[:, j, :], iotaK[:, :], keyE[:, bass.ds(c + j, 1)],
                                                         powE[:, bass.ds(c + j, 1)].bitcast(F32), ALU.is_equal, ALU.mult)
                            last.then_inc(s_oh, 1)
                    turns_before = dve.snap(turns_before + last_turn + 1)
                if t:
                    dve.wait_ge(s_enc, t)
                    if t >= 3:
                        dve.wait_ge(s_at, t - 2)
                    u = (t - 1) % 2
                    dve.tensor_scalar(encB[:, u, 0, :], encI[:, u, :], NIBBLES, None, ALU.bitwise_and)
                    dve.tensor_scalar(encB[:, u, 1, :], encI[:, u, :], 4, NIBBLES, ALU.logical_shift_right, ALU.bitwise_and).then_inc(s_nib, 1)
            dve.wait_ge(s_deg, NT)
            step(dve.tensor_copy(deg[:, :], bank[6][0:P, 0:NT]))
            dve.tensor_reduce(bad[:, :], deg[:, :], axis=XYZ, op=ALU.add).then_inc(s_flagp, 1)
            dve.wait_ge(s_flagp, 2)
            dve.tensor_scalar(flag[:, :], bank[7][0:1, 0:1], float(E), None, ALU.not_equal).then_inc(s_flag, 1)
            dve.wait_ge(s_flag, 1)
            with dve.If(dve.value_load(flag[0:1, 0:1], min_val=0, max_val=1) == 1):
                gather_dve(dve, 0, None)
                dve.tensor_copy(deg[:, :], bank[6][0:P, 0:NT]).then_inc(s_flag, 1)
                dve.wait_ge(s_flag, 2)
            dve.sem_inc(s_flag2, 1)
            step(dve.tensor_scalar(deg1[:, :], deg[:, :], 1.0, None, ALU.max))
            dve.sem_inc(s_var, 1)
            dve.wait_ge(s_std, 2)
            inverse_root(dinvP[:, :], deg1[:, :], dsd[:, :], dt1[:, :])
            step(dve.scalar_tensor_tensor(dinvP[:, :], deg[:, :], 1.0, dinvP[:, :], ALU.min, ALU.mult))
            step(dve.tensor_copy(dpart[:, 0, :], dinvP[:, :]))
            step(dve.tensor_tensor(drem[:, 0, :], dinvP[:, :], dpart[:, 0, :], ALU.subtract))
            step(dve.tensor_copy(dpart[:, 1, :], drem[:, 0, :]))
            step(dve.tensor_tensor(drem[:, 1, :], drem[:, 0, :], dpart[:, 1, :], ALU.subtract))
            step(dve.tensor_copy(dpart[:, 2, :], drem[:, 1, :]))
            for t in range(NT):
                if t >= 2:
                    dve.wait_ge(s_bc, t - 1)
                dve.tensor_scalar(ddg[:, t % 2, :], ident[0:P, 0:P], dinvP[:, t:t + 1], None, ALU.mult).then_inc(s_dg, 1)
            dve.wait_ge(s_bc, NT)
            dve.sem_inc(s_dpart, 1)
            m_rows_dve(dve, lambda n: 0)
            def sources(b):
                dve.wait_ge(s_slr[b % 2], 16 * (b // 2 + 1))
                if b >= 2:
                    dve.wait_ge(s_lk, b - 1)
                dve.tensor_scalar(ohT[:, b % 2, :], slrow[:, b % 2, :], iotaP[0:P, :], None, ALU.is_equal).then_inc(s_ohT, 1)

            sources(0)
            for b in range(NLB):
                if b + 1 < NLB:
                    sources(b + 1)
                step(dve.tensor_tensor(ohs[:, b % 2, :, :], s16[:, b * LB:(b + 1) * LB].unsqueeze(2).to_broadcast([128, LB, NT]),
                                       iota25[:, :].unsqueeze(1).to_broadcast([128, LB, NT]), ALU.is_equal))
                dve.wait_ge(s_lk, b + 1)
                if b:
                    dve.wait_ge(s_ds, b)
                dve.tensor_tensor(lkt[:, :], bank[1 + b % 2][:, 0:LB * NT], ohs[:, b % 2, :, :].rearrange("p c s -> p (c s)"), ALU.mult).then_inc(s_lke, 1)
                dve.wait_ge(s_lke, b + 1)
                dve.tensor_reduce(dsrc[:, b * LB:(b + 1) * LB], lkt[:, :].rearrange("p (c s) -> p c s", s=NT), axis=XYZ, op=ALU.add).then_inc(s_ds, 1)
            dve.wait_ge(s_ds, NLB)
            step(dve.tensor_tensor(v4[:, :, :], eaE[:, :, :], dsrc[:, :].unsqueeze(2).to_broadcast([128, NCH, 4]), ALU.mult))
            step(dve.memset(w12[:, NCH:NCHP, :], 0.0))
            step(dve.tensor_copy(w12[:, 0:NCH, 0:4], v4[:, :, :]))
            step(dve.tensor_tensor(v4b[:, :, :], v4[:, :, :], w12[:, 0:NCH, 0:4], ALU.subtract))
            step(dve.tensor_copy(w12[:, 0:NCH, 4:8], v4b[:, :, :]))
            step(dve.tensor_tensor(v4[:, :, :], v4b[:, :, :], w12[:, 0:NCH, 4:8], ALU.subtract))
            dve.tensor_copy(w12[:, 0:NCH, 8:12], v4[:, :, :]).then_inc(s_w12, 1)
            dve.memset(ewT[:, :, :], 0.0)
            dve.memset(inv[:, :], 2.0 ** -H0_EXP).then_inc(s_ez, 1)
            dve.wait_ge(s_w12, 1)
            dve.wait_ge(s_ez, 1)
            zero = lambda n: 0
            turns_before = 0
            evicted = 0
            for t in range(NT):
                while evicted < H * NQ and NT * (evicted + 1) <= max(dense_before(0), dense_before(t - 1)):
                    evict(dve, zero, evicted)
                    evicted += 1
                first = dve.value_load(rng[0:1, t:t + 1], min_val=0, max_val=MAX_FIRST)
                last_turn = dve.value_load(rng[0:1, NT + t:NT + t + 1], min_val=MIN_TURNS - 1, max_val=MAX_TURNS - 1)
                step(dve.tensor_scalar(iotaD3[:, :, :], iotaD3[:, :, :], float(P), None, ALU.add))
                with dve.Fori(0, last_turn + 1) as i:
                    k = dve.snap(2 * (turns_before + i))
                    c = dve.snap(chunk_of(first, i))
                    for half in range(2):
                        dve.wait_ge(s_freeD, k + half + 1)
                        dve.tensor_tensor(ohD[:, half, :, :], iotaD3[:, :, :],
                                          dst3[:, bass.ds(c + half * HU, HU)].unsqueeze(1).to_broadcast([128, P, HU]), ALU.is_equal).then_inc(s_ohD, 1)
                turns_before = dve.snap(turns_before + last_turn + 1)
                if t:
                    s4_out(dve, t - 1)
            s4_out(dve, NT - 1)
            for g in range(evicted, H * NQ):
                evict(dve, zero, g)
            with dve.If(dve.value_load(flag[0:1, 0:1], min_val=0, max_val=1) == 1):
                gather_dve(dve, 1, 0)
            weights_dve(dve, LOADS, 0)
            attributes_dve(dve, zero)
            statistics_dve(dve, zero, False)
            with dve.Fori(0, L - 2) as i:
                base = lambda n: dve.snap(i * n + n)
                aggregate_dve(dve, base, i + 1, LOADS * (i + 2))
                statistics_dve(dve, base, False)
            base = lambda n: (L - 1) * n
            aggregate_dve(dve, base, L - 1, LOADS * L)
            statistics_dve(dve, base, True)
            if stop is None:
                experts_dve(dve, step, rounded, inverse_root)

        @block.scalar
        def _(act):
            act.wait_ge(s_var, 1)
            act.activation(xsd[:, :], xve[:, :], ACT.Sqrt).then_inc(s_std, 1)
            act.wait_ge(s_xf, 1)

            def normal(t):
                act.activation(xin[:, t, :], xin[:, t, :], ACT.Identity, scale=xrs[:, t:t + 1], bias=xsh[:, t:t + 1]).then_inc(s_xn, 1)

            normal(0)
            act.wait_ge(s_sld, 16)
            for t in range(NT + 1):
                if t < NT:
                    act.wait_ge(s_cnt, t + 1)
                    if t >= 2:
                        act.wait_ge(s_nib, t - 1)
                    for b in range(GB):
                        last = act.activation(encI[:, t % 2, b * GC:(b + 1) * GC], bank[GB * (t % 2) + b][0:P, 0:GC], ACT.Copy)
                    last.then_inc(s_enc, 1)
                    if t + 1 < NT:
                        normal(t + 1)
                    act.wait_ge(s_xT, t + 1)
                    act.activation(hT[:, :, t * P:(t + 1) * P], bank[4 + t % 2][:, 0:H * P].rearrange("p (h n) -> p h n", h=H), ACT.Copy).then_inc(s_xTe, 1)
                if t:
                    u = t - 1
                    act.wait_ge(s_nib, u + 1)
                    for odd in range(2):
                        n = (FIELDS + 1 - odd) // 2
                        byte = encB[:, u % 2, odd, 0:GROUPS * P].bitcast(U8).rearrange("p (g n k) -> p k g n", g=GROUPS, k=4)
                        for f in range(n):
                            last = act.activation(at[:, odd + 2 * f:odd + 2 * f + FIELDS * (GROUPS - 1) + 1:FIELDS, u * P:(u + 1) * P],
                                                  byte[:, f, :, :], ACT.Copy, saturate=False)
                    last.then_inc(s_at, 1)
            act.wait_ge(s_var, 2)
            act.activation(dsd[:, :], deg1[:, :], ACT.Sqrt).then_inc(s_std, 1)
            for q, (a, w) in enumerate(COLS):
                act.wait_ge(s_bc, (a + w) // P)
                act.activation(dinvB[:, a:a + w], bank[q % 2][:, 0:w], ACT.Copy).then_inc(s_dB, 1)
            m_rows_act(act, lambda n: 0)
            for q, (a, w) in enumerate(COLS):
                act.wait_ge(s_s4T, q + 1)
                act.activation(s4T[:, a:a + w], bank[1 + q % 2][0:4, 0:w], ACT.Copy).then_inc(s_s4Te, 1)
            linear_act(act, lambda n: 0)
            with act.Fori(0, L - 2) as i:
                prev, base = (lambda n: act.snap(i * n)), (lambda n: act.snap(i * n + n))
                m_rows_act(act, base, normalise_act(act, prev, False))
                linear_act(act, base)
            prev, base = (lambda n: (L - 2) * n), (lambda n: (L - 1) * n)
            m_rows_act(act, base, normalise_act(act, prev, False))
            linear_act(act, base)
            last = normalise_act(act, base, True)
            for q in range(NQ):
                last(q)
            if stop is None:
                experts_act(act)

        @block.tensor
        def _(pe):
            pe.wait_ge(s_mem, 2)
            for n, tile in enumerate((dstC, srcC)):
                pe.wait_ge(s_edges, n + 1)
                for b in range(NB):
                    pe.transpose(bank[n][:, b * CB:(b + 1) * CB], tile[:, b, :], ident[0:CB, 0:CB]).then_inc(s_tp, 1)
            pe.wait_ge(s_ea, 48)
            for j in range(4):
                for b in range(NB):
                    last = pe.transpose(bank[2 + j][:, b * CB:(b + 1) * CB], eaC[:, b, j:j + 4 * (CH - 1) + 1:4], ident[0:CB, 0:CB])
                last.then_inc(s_tp, 1)
            pe.wait_ge(s_cmm, 1)
            for n in range(2):
                for b in range(NB):
                    last = pe.matmul(bank[6 + n][0:NT, b * CB:(b + 1) * CB], cmmB[:, n * NB + b, :], ident[0:CB, 0:CB], start=True, stop=True)
                last.then_inc(s_minmax, 1)
            pe.wait_ge(s_lohi, 1)
            for n in range(2):
                last = pe.matmul(bank[0][0:1, n * NT:(n + 1) * NT], lohi2[:, n:n + 1], ident[0:NT, 0:NT], start=True, stop=True)
            last.then_inc(s_rngp, 1)
            pe.wait_ge(s_rng, 1)

            def degrees(t):
                pe.wait_ge(s_at, t + 1)
                for s in range(NT):
                    last = pe.matmul(bank[6][0:P, t:t + 1], at[:, s, t * P:(t + 1) * P], ones16[0:P, :], start=s == 0, stop=s == NT - 1)
                last.then_inc(s_deg, 1)

            turns_before = 0
            for t in range(NT):
                last_turn = pe.value_load(rng[0:1, NT + t:NT + t + 1], min_val=MIN_TURNS - 1, max_val=MAX_TURNS - 1)
                if t >= 2:
                    pe.wait_ge(s_enc, t - 1)

                def turn(i, start, stop_):
                    k = pe.snap(2 * (turns_before + i))
                    for half in range(2):
                        first_half, last_half = start and half == 0, stop_ and half == 1
                        pe.wait_ge(s_oh, k + half + 1)
                        for j in range(HU):
                            for b in range(GB):
                                last = pe.matmul(bank[GB * (t % 2) + b][:, 0:GC], ohS[:, half, :, j],
                                                 cnt1[:, half * HU + j, b * GC:(b + 1) * GC], start=first_half and j == 0, stop=last_half and j == HU - 1)
                        last.then_inc(s_cnt if last_half else s_free, 1)
                    if stop_:
                        pe.wait_ge(s_cnt, t + 1)
                        pe.sem_inc(s_free, 1)

                turn(0, True, False)
                with pe.Fori(1, last_turn) as i:
                    turn(i, False, False)
                turn(last_turn, False, True)
                pe.wait_ge(s_xn, t + 1)
                if t >= 2:
                    pe.wait_ge(s_xTe, t - 1)
                for h in range(H):
                    last = pe.transpose(bank[4 + t % 2][:, h * P:(h + 1) * P], xin[:, t, h * 128:(h + 1) * 128], ident[0:P, 0:P])
                last.then_inc(s_xT, 1)
                turns_before = pe.snap(turns_before + last_turn + 1)
                if t >= 2:
                    degrees(t - 2)
            degrees(NT - 2)
            degrees(NT - 1)
            pe.wait_ge(s_flagp, 1)
            pe.matmul(bank[7][0:1, 0:1], ones[0:P, 0:1], bad[:, :], start=True, stop=True).then_inc(s_flagp, 1)
            pe.wait_ge(s_flag, 1)
            with pe.If(pe.value_load(flag[0:1, 0:1], min_val=0, max_val=1) == 1):
                gather_pe(pe, 0, None)
            pe.wait_ge(s_enc, NT)
            for q, (a, w) in enumerate(COLS):
                if q >= 2:
                    pe.wait_ge(s_dB, q - 1)
                for t in range(a // P, (a + w) // P):
                    pe.wait_ge(s_dg, t + 1)
                    pe.matmul(bank[q % 2][:, t * P - a:(t + 1) * P - a], ones[0:P, :], ddg[:, t % 2, :], start=True, stop=True).then_inc(s_bc, 1)
            pe.wait_ge(s_dB, NQ)
            zero = lambda n: 0
            for t in range(NT):
                row_pe(pe, zero, None, t)
            pe.wait_ge(s_lo, NT)
            done = [0]

            def dense_to(n):
                for u in range(done[0], min(n, DENSE)):
                    g, t = u // NT, u % NT
                    if g >= 4 and t == 0:
                        pe.wait_ge(s_agge, g - 3)
                    dense(pe, g, t)
                done[0] = min(n, DENSE)

            pe.wait_ge(s_dpart, 1)
            for b in range(NLB):
                pe.wait_ge(s_ohT, b + 1)
                if b >= 2:
                    pe.wait_ge(s_lke, b - 1)
                for c in range(LB):
                    for k in range(3):
                        last = pe.matmul(bank[1 + b % 2][:, c * NT:(c + 1) * NT], ohT[:, b % 2, c * CH:(c + 1) * CH],
                                         dpart[:, k, :], start=k == 0, stop=k == 2)
                last.then_inc(s_lk, 1)
                dense_to(DENSE_L * (b + 1))
            dense_to(dense_before(0))
            pe.wait_ge(s_w12, 1)
            turns_before = 0
            for t in range(NT):
                first = pe.value_load(rng[0:1, t:t + 1], min_val=0, max_val=MAX_FIRST)
                last_turn = pe.value_load(rng[0:1, NT + t:NT + t + 1], min_val=MIN_TURNS - 1, max_val=MAX_TURNS - 1)
                if t >= 2:
                    pe.wait_ge(s_s4e, 2 * (t - 1) - 1)

                def turn4(i, start, stop_):
                    k = pe.snap(2 * (turns_before + i))
                    c = pe.snap(chunk_of(first, i))
                    for half in range(2):
                        first_half, last_half = start and half == 0, stop_ and half == 1
                        pe.wait_ge(s_ohD, k + half + 1)
                        for j in range(HU):
                            last = pe.matmul(bank[S4_BANKS[t % 2]][0:P, 0:12], ohD[:, half, :, j],
                                             w12[:, bass.ds(c + half * HU + j, 1), :].rearrange("p a w -> p (a w)"),
                                             start=first_half and j == 0, stop=last_half and j == HU - 1)
                        last.then_inc(s_s4 if last_half else s_freeD, 1)
                    if stop_:
                        pe.wait_ge(s_s4, t + 1)
                        pe.sem_inc(s_freeD, 1)

                turn4(0, True, False)
                with pe.Fori(1, last_turn) as i:
                    turn4(i, False, False)
                turn4(last_turn, False, True)
                turns_before = pe.snap(turns_before + last_turn + 1)
                dense_to(dense_before(t + 1))
            pe.wait_ge(s_s4e, 2 * NT)
            for q, (a, w) in enumerate(COLS):
                if q >= 2:
                    pe.wait_ge(s_s4Te, q - 1)
                for t in range(a // P, (a + w) // P):
                    last = pe.transpose(bank[1 + q % 2][0:4, t * P - a:(t + 1) * P - a], s4P[:, t, :], ident[0:P, 0:P])
                last.then_inc(s_s4T, 1)
            dense_to(DENSE)
            pe.wait_ge(s_s4Te, NQ)
            with pe.If(pe.value_load(flag[0:1, 0:1], min_val=0, max_val=1) == 1):
                gather_pe(pe, 1, 0)
            attributes_pe(pe, zero)
            linear_pe(pe, zero)
            with pe.Fori(0, L - 2) as i:
                prev, base = (lambda n: pe.snap(i * n)), (lambda n: pe.snap(i * n + n))
                aggregate_pe(pe, base, prev, i + 1)
                linear_pe(pe, base)
            prev, base = (lambda n: (L - 2) * n), (lambda n: (L - 1) * n)
            aggregate_pe(pe, base, prev, L - 1)
            linear_pe(pe, base)
            if stop is None:
                experts_pe(pe)


INPUTS = ["x", "src", "dst", "edge_attr_4", "L0_gnn_mlp_w", "L0_gnn_mlp_b", "L0_gnn_ew1", "L0_gnn_ew2", "L0_gnn_bn_g",
          "L0_gnn_bn_b", "L0_ffn_Wg", "L0_ffn_bg", "L0_ffn_bias", "L0_ffn_W1", "L0_ffn_b1", "L0_ffn_W2", "L0_ffn_b2"]


def kernel(**inputs):
    import numpy as np
    from concourse import bacc
    from concourse.bass_utils import run_bass_kernel_spmd

    nc = bacc.Bacc("TRN2", target_bir_lowering=False, num_devices=1)
    arrays, args = {}, []
    for name in INPUTS:
        a = np.ascontiguousarray(inputs[name])
        arrays["in_" + name] = a
        args.append(nc.dram_tensor("in_" + name, a.shape, mybir.dt.from_np(a.dtype), kind="ExternalInput").ap())
    out = nc.dram_tensor("out_rows", (N, D), F32, kind="ExternalOutput").ap()
    gnn_ffn_program(nc, *args, out)
    done = run_bass_kernel_spmd(nc, [arrays], core_ids=[0])
    return done.results[0]["out_rows"]
```

```python
import concourse.bass as bass
from concourse import mybir
from contextlib import ExitStack

F32 = mybir.dt.float32
I32 = mybir.dt.int32
U32 = mybir.dt.uint32
I16 = mybir.dt.int16
U8 = mybir.dt.uint8
BF16 = mybir.dt.bfloat16
F16 = mybir.dt.float16
F8 = mybir.dt.float8e4
SIZE = {F32: 4, I32: 4, U32: 4, I16: 2, U8: 1, BF16: 2, F16: 2, F8: 1}
ALU = mybir.AluOpType
ACT = mybir.ActivationFunctionType
XYZ = mybir.AxisListType.X

N = 3125
D = 256
E = 53125
L = 5
P = 125
NT = N // P
H = D // 128
CH = 128
NCH = 416
NB = 4
CB = NCH // NB
U = 6
MIN_TURNS = 3
MAX_FIRST = NCH - U * MIN_TURNS
MAX_TURNS = (NCH + U - 1) // U
NCHP = NCH + U
DST_PAD = 3500
FIELDS = 5
GROUPS = (NT + FIELDS - 1) // FIELDS
assert GROUPS * FIELDS == NT
GB = 2
GC = (GROUPS * P + GB - 1) // GB
GW = GB * GC
NIBBLES = 0x0F0F0F
KEY = 3584
MAGIC = 12582912.0
BIG = 1000.0
CQ = 500
COLS = [(q, min(CQ, N - q)) for q in range(0, N, CQ)]
NQ = len(COLS)
PARTS = 3
K4 = PARTS * PARTS * 4
LN_EPS = 1e-5
BN_EPS = 1e-5
H0_EXP = 11
LB = 13
NLB = NCH // LB
DENSE = H * NQ * NT
DENSE_L = 3
DENSE_S = 8
NE = 8
F = 512
FK = F // 128
TT = 128
J = (2 * N + NE * (TT - 1)) // TT
XB = 4
assert J % XB == 0


def gnn_ffn_program(nc, x, src, dst, edge_attr, mlp_w, mlp_b, ew1, ew2, bn_g, bn_b,
                    wg, bg, gbias, w1, b1, w2, b2, out):
    ctx = ExitStack()
    with ctx:
        base = (nc.sbuf_base + 31) // 32 * 32

        class Region:
            def __init__(self, start):
                self.at = start

            def __call__(self, name, shape, dt):
                n = SIZE[dt]
                for s in shape[1:]:
                    n *= s
                t = nc.alloc_sbuf_tensor_at(name, shape, dt, offset=base + self.at)
                self.at = (self.at + n + 31) // 32 * 32
                assert base + self.at <= nc.sbuf_usable_end, name
                return t

        def sem(name):
            return ctx.enter_context(nc.semaphore(name))

        bank = [ctx.enter_context(nc.psum_tensor(f"bank{i}", [128, 512], F32)) for i in range(8)]

        keep = Region(0)
        at = keep("at", [P, NT, N], F8)
        hT_at = keep.at
        hT = keep("hT", [128, H, N], F32)
        dinvB_at = keep.at
        dinvB = keep("dinvB", [128, N], F32)
        s4T = keep("s4T", [K4, N], BF16)
        keep.at = (dinvB_at + 2 * 4 * N + 31) // 32 * 32
        maskK = keep("maskK", [K4, PARTS], F32)
        ident = keep("ident", [128, 128], F32)
        ones = keep("ones", [128, 128], F32)
        ones16 = keep("ones16", [128, 1], BF16)
        dinvP = keep("dinvP", [P, NT], F32)
        dstE = keep("dstE", [128, NCHP], F32)
        srcX = keep("srcX", [128, NCHP], I32)
        iotaD0 = keep("iotaD0", [128, P + 1], I16)
        iotaD = keep("iotaD", [128, P + 1], I16)
        rng = keep("rng", [1, 3 * NT + 1], I32)
        flag = keep("flag", [1, 1], I32)
        zt_at = keep.at
        keep.at += 4 * 1024
        xstart = keep.at

        r = Region(xstart)
        aggT = r("aggT", [128, H, N], F32)
        w_at = r.at
        wcur = r("wcur", [128, 2 * H, D], F32)
        wraw = r("wraw", [128, 2 * H, D], F32)
        ewm = r("ewm", [K4, D], BF16)
        ewp = r("ewp", [K4, PARTS, D], BF16)
        ewr = r("ewr", [K4, 2, D], F32)
        r.at = max(r.at, (w_at + NCHP * 12 * SIZE[BF16] + 31) // 32 * 32)
        w_end = r.at
        ewT = r("ewT", [128, H, 4], F32)
        ewK = r("ewK", [128, H, K4], F32)
        prm = r("prm", [128, 3, H], F32)
        zst = r("zst", [128, H, NQ, 6], F32)
        zmv = r("zmv", [128, H, 2], F32)
        cf = r("cf", [128, 6, H], F32)
        cfi = r("cfi", [128, 2, H], I32)
        inv = r("inv", [128, H], F32)
        m_at = r.at
        m = r("m", [P, NT, 2, D], F16)

        dst3 = r("dst3", [128, NCHP], I16)
        s16 = r("s16", [128, NCH], I16)
        iota25 = r("iota25", [128, NT], I16)
        iotaP = r("iotaP", [128, 1], F32)
        iotaD3 = r("iotaD3", [128, P, U], I16)
        ohD_at = r.at
        ohD = r("ohD", [128, 3, P, U], BF16)
        nowW = r("nowW", [128, 3, U, 12], BF16)
        gsel = r("gsel", [128, U, P + 1], BF16)
        dinvT = r("dinvT", [NT, P], F32)
        s4s = r("s4s", [P, NT, 4], F32)
        s4P = r("s4P", [P, NT, 4], F32)
        end_at = r.at
        r = Region(ohD_at)
        s4K = r("s4K", [P, NT, K4], F32)
        s4h = r("s4h", [P, 2, NT, 4], BF16)
        r = Region(end_at)
        dpart = r("dpart", [P, 3, NT], BF16)

        r = Region(xstart)
        eaE = r("eaE", [128, NCH, 4], F32)
        pass1 = r.at
        slrow_at = r.at
        slrow = r("slrow", [P, 2, LB * CH], I16)
        ohT_at = r.at
        ohT = r("ohT", [P, 2, LB * CH], BF16)
        ohs = r("ohs", [128, 2, LB, NT], BF16)
        lkt = r("lkt", [128, LB * NT], F32)
        dsrc = r("dsrc", [128, NCH], F32)
        assert r.at <= w_at
        r = Region(slrow_at)
        v4 = r("v4", [128, NCH, 4], F32)
        r = Region(ohT_at)
        v4b = r("v4b", [128, NCH, 4], F32)
        r = Region(w_at)
        w12 = r("w12", [128, NCHP, 12], BF16)
        assert r.at <= w_end

        r = Region(pass1)
        keyE = r("keyE", [128, NCHP], F32)
        powE = r("powE", [128, NCHP], I32)
        sl16 = r("sl16", [128, NCHP], I16)
        iotaK = r("iotaK", [128, 2, GW], I16)
        iotaS = r("iotaS", [128, 128, U], I16)
        cnt1, ohS = [], []

        def turn_buffers(r, n):
            for _ in range(n):
                cnt1.append(r(f"cnt1_{len(cnt1)}", [128, U, GW], BF16))
                ohS.append(r(f"ohS_{len(ohS)}", [128, 128, U], BF16))

        turn_buffers(r, 2)
        deg = r("deg", [P, NT], F32)
        deg1 = r("deg1", [P, NT], F32)
        drem = r("drem", [P, 2, NT], F32)
        dsd = r("dsd", [P, NT], F32)
        dt1 = r("dt1", [P, NT], F32)
        bad = r("bad", [P, 1], F32)
        xin = r("xin", [P, NT, D], F32)
        xrs = r("xrs", [P, NT], F32)
        xsh = r("xsh", [P, NT], F32)
        assert r.at <= m_at + NT * 2 * D * 2
        r = Region(dinvB_at)
        encI = r("encI", [P, 2, GW], I32)
        encB = r("encB", [P, 2, 2, GW], I32)
        turn_buffers(r, 1)
        assert r.at <= dinvB_at + 2 * 4 * N
        r = Region(0)
        dstI = r("dstI", [CB, NB, CH], I32)
        srcI = r("srcI", [CB, NB, CH], I32)
        eaC = r("eaC", [CB, NB, CH * 4], F32)
        dstC = r("dstC", [CB, NB, CH], F32)
        srcC = r("srcC", [CB, NB, CH], F32)
        slC = r("slC", [CB, NB, CH], I16)
        ta = r("ta", [128, NB * CH], F32)
        tb = r("tb", [128, NB * CH], F32)
        tg = r("tg", [128, NCH], F32)
        cmm = r("cmm", [CB, 2, NB], F32)
        cmmB = r("cmmB", [CB, 2 * NB, NT], F32)
        cidx = r("cidx", [NT, NCH], F32)
        tlo = r("tlo", [NT, 1], F32)
        rowK = r("rowK", [K4, 2], F32)
        m1 = r("m1", [NT, NCH], F32)
        m2 = r("m2", [NT, NCH], F32)
        lohi = r("lohi", [NT, 2], F32)
        lohi2 = r("lohi2", [NT, 2], F32)
        rngf = r("rngf", [1, 3, NT], F32)
        xst = r("xst", [P, NT, 6], F32)
        xmv = r("xmv", [P, NT, 2], F32)
        xve = r("xve", [P, NT], F32)
        xsd = r("xsd", [P, NT], F32)
        xt1 = r("xt1", [P, NT], F32)

        r = Region(0)
        x2 = r("x2", [P, NT, D], F32)
        xn = r("xn", [P, NT, D], F32)
        b2B = r("b2B", [128, NE, D], F32)
        b1T = r("b1T", [128, NE, FK], F32)
        ohR_at = r.at
        ohR = r("ohR", [P, NT, TT], F32)
        after = r.at
        r = Region(ohR_at)
        lgT = r("lgT", [NE, N], F32)
        assert r.at <= after
        r = Region(after)
        h1 = r("h1", [TT, 2, F], F32)
        assert r.at <= hT_at
        r = Region(hT_at)
        w2s = r("w2s", [128, NE, FK, D], F32)
        fst = r("fst", [P, NT, 6], F32)
        fmv = r("fmv", [P, NT, 2], F32)
        fve = r("fve", [P, NT], F32)
        fsd = r("fsd", [P, NT], F32)
        frs = r("frs", [P, NT], F32)
        ft1 = r("ft1", [P, NT], F32)
        lgt = r("lgt", [P, NT, NE], F32)
        top = r("top", [P, NT, 8], F32)
        tix = r("tix", [P, NT, 8], U32)
        ef = r("ef", [P, 2, NT], F32)
        oh1 = r("oh1", [P, NT, NE], F32)
        oh2 = r("oh2", [P, NT, NE], F32)
        msk = r("msk", [P, NT, NE], F32)
        cnt = r("cnt", [P, NT, NE], F32)
        incl = r("incl", [P, NT, NE], F32)
        slm = r("slm", [P, NT, NE], F32)
        nte = r("nte", [P, 4, NE], F32)
        slf = r("slf", [P, 2, NT], F32)
        sltile = r("sltile", [P, 2, NT], F32)
        slplace = r("slplace", [P, 2, NT], F32)
        pad = r("pad", [128, J], F32)
        rowid = r("rowid", [128, J], F32)
        rowG = r("rowG", [128, J], I32)
        rowS = r("rowS", [128, J], I32)
        wS = r("wS", [128, J], F32)
        nowG = r("nowG", [128, XB], I32)
        nowS = r("nowS", [128, XB], I32)
        wts = r("wts", [P, 3, NT], F32)
        cmpJ = r("cmpJ", [1, J, NE], F32)
        teF = r("teF", [1, J], F32)
        te = r("te", [1, J], I32)
        assert r.at <= dinvB_at + 2 * 4 * N
        r = Region(m_at)
        w1s = r("w1s", [128, NE, H, F], F32)
        xtb = r("xtb", [TT, XB, D], F32)
        r = Region(xstart)
        h1T = r("h1T", [128, 2, FK, TT], F32)
        xtT = r("xtT", [128, 2, H, TT], F32)
        ytt = r("ytt", [TT, 2, D], F32)
        ytb_at = r.at
        ytb = r("ytb", [TT, XB, D], F32)
        after = r.at
        r = Region(ytb_at)
        xnT = r("xnT", [128, 2, H, CQ], F32)
        r = Region(after)
        idJ = r("idJ", [P, 2, NT, 2, J], F32)
        assert r.at <= w_end
        r = Region(zt_at)
        zt = r("zt", [TT, D], F32)
        wgs = r("wgs", [128, H, NE], F32)
        gbr = r("gbr", [NE, 2], F32)
        gbs = r("gbs", [NE, 1], F32)
        tri = r("tri", [P, P], F32)
        iota8 = r("iota8", [P, NE], F32)
        iotaJ = r("iotaJ", [P, J], F32)
        iotaT = r("iotaT", [P, TT], F32)
        iotaN = r("iotaN", [P, NT], F32)
        iotaX = r("iotaX", [128, 1], F32)
        assert r.at <= xstart

        xn_dram = nc.dram_tensor("xn_dram", (N, D), F32, kind="Internal").ap()
        r = Region(0)
        gix = r("gix", [128, U], I32)
        grow = r("grow", [128, U, 2, D], F16)
        dinv_dram = nc.dram_tensor("dinv_dram", (N,), F32, kind="Internal").ap()
        m_dram = nc.dram_tensor("m_dram", (N, 2 * D), F16, kind="Internal").ap()
        sl_dram = nc.dram_tensor("sl_dram", (NCH * CH,), I16, kind="Internal").ap()

        s_mem = sem("s_mem")
        s_src = sem("s_src")
        s_dst = sem("s_dst")
        s_ea = sem("s_ea")
        s_x = sem("s_x")
        s_edges = sem("s_edges")
        s_cmm = sem("s_cmm")
        s_tp = sem("s_tp")
        s_minmax = sem("s_minmax")
        s_lohi = sem("s_lohi")
        s_rngp = sem("s_rngp")
        s_rng = sem("s_rng")
        s_slC = sem("s_slC")
        s_sld = sem("s_sld")
        s_dv = sem("s_dv")
        s_po = sem("s_po")
        s_var = sem("s_var")
        s_std = sem("s_std")
        s_xn = sem("s_xn")
        s_xT = sem("s_xT")
        s_xTe = sem("s_xTe")
        s_oh = [sem(f"s_oh{r}") for r in range(3)]
        s_free = [sem(f"s_free{r}") for r in range(2)]
        s_cnt = sem("s_cnt")
        s_enc = sem("s_enc")
        s_iotaK = sem("s_iotaK")
        s_nib = sem("s_nib")
        s_xf = sem("s_xf")
        s_ds = sem("s_ds")
        s_at = sem("s_at")
        s_deg = sem("s_deg")
        s_bc = sem("s_bc")
        s_dB = sem("s_dB")
        s_dBd = sem("s_dBd")
        s_dpart = sem("s_dpart")
        s_slr = [sem(f"s_slr{i}") for i in range(2)]
        s_ohT = sem("s_ohT")
        s_lk = sem("s_lk")
        s_lke = sem("s_lke")
        s_w12 = sem("s_w12")
        s_ohD = [sem(f"s_ohD{r}") for r in range(3)]
        s_freeD = [sem(f"s_freeD{r}") for r in range(2)]
        s_s4 = sem("s_s4")
        s_s4e = sem("s_s4e")
        s_s4K = sem("s_s4K")
        s_s4T = sem("s_s4T")
        s_s4Te = sem("s_s4Te")
        s_w = sem("s_w")
        s_wc = sem("s_wc")
        s_ewp = sem("s_ewp")
        s_ewm = sem("s_ewm")
        s_ew = sem("s_ew")
        s_tr = sem("s_tr")
        s_hi = sem("s_hi")
        s_lo = sem("s_lo")
        s_agg = sem("s_agg")
        s_agge = sem("s_agge")
        s_mlp = sem("s_mlp")
        s_z = sem("s_z")
        s_bv = sem("s_bv")
        s_bs = sem("s_bs")
        s_bn = sem("s_bn")
        s_h = sem("s_h")
        s_ls = sem("s_ls")
        s_ez = sem("s_ez")
        s_flagp = sem("s_flagp")
        s_flag = sem("s_flag")
        s_md = sem("s_md")
        s_ix = sem("s_ix")
        s_gr = [[sem(f"s_gr{l}_{j}") for j in range(U // 2)] for l in range(L)]
        s_got = sem("s_got")
        s_gi = sem("s_gi")
        s_gs = sem("s_gs")
        s_gf = sem("s_gf")
        s_gt = sem("s_gt")
        s_ge = sem("s_ge")
        s_apart = sem("s_apart")
        s_cst = sem("s_cst")
        s_x2 = sem("s_x2")
        s_fw = sem("s_fw")
        s_w1 = sem("s_w1")
        s_w2 = sem("s_w2")
        s_oT = sem("s_oT")
        s_oTe = sem("s_oTe")
        s_fve = sem("s_fve")
        s_fsd = sem("s_fsd")
        s_fn = sem("s_fn")
        s_gT = sem("s_gT")
        s_gTe = sem("s_gTe")
        s_gl = sem("s_gl")
        s_glc = sem("s_glc")
        s_gate = sem("s_gate")
        s_gbs = sem("s_gbs")
        s_msk = sem("s_msk")
        s_rank = sem("s_rank")
        s_ex = sem("s_ex")
        s_exd = sem("s_exd")
        s_slot = sem("s_slot")
        s_xnd = sem("s_xnd")
        s_res = sem("s_res")
        s_R = sem("s_R")
        s_place = sem("s_place")
        s_tabP = sem("s_tabP")
        s_idw = sem("s_idw")
        s_tab = sem("s_tab")
        s_xt = [sem(f"s_xt{i}") for i in range(XB)]
        s_xtT = sem("s_xtT")
        s_xtc = sem("s_xtc")
        s_h1 = sem("s_h1")
        s_h1c = sem("s_h1c")
        s_hT = sem("s_hT")
        s_hTc = sem("s_hTc")
        s_y = sem("s_y")
        s_yt = sem("s_yt")
        s_yb = sem("s_yb")
        s_nowG = sem("s_nowG")
        s_nowS = sem("s_nowS")
        s_acc = sem("s_acc")

        block = ctx.enter_context(nc.Block())

        def tail_dmas(sp, tile, dram, width, s):
            full = (NB - 1) * CB * CH
            last = (CB - 1) * CH
            sp.dma_start(tile[:, 0:NB - 1, :], dram[0:full * width].rearrange("(b p e) -> p b e", b=NB - 1, p=CB)).then_inc(s, 16)
            sp.wait_ge(s_mem, 1)
            sp.dma_start(tile[0:CB - 1, NB - 1, :], dram[full * width:(full + last) * width].rearrange("(p e) -> p e", p=CB - 1)).then_inc(s, 16)
            rest = E - full - last
            sp.dma_start(tile[CB - 1:CB, NB - 1, 0:rest * width], dram[(full + last) * width:E * width].rearrange("(p e) -> p e", p=1)).then_inc(s, 16)

        S4_BANKS = (1, 2)

        def s4_out(dve, t):
            dve.wait_ge(s_s4, t + 1)
            dve.tensor_reduce(s4s[:, t, :], bank[S4_BANKS[t % 2]][0:P, 0:12].rearrange("p (k j) -> p j k", j=4), axis=XYZ, op=ALU.add).then_inc(s_s4e, 1)
            dve.wait_ge(s_s4e, 2 * t + 1)
            dve.tensor_scalar(s4P[:, t, :], s4s[:, t, :], dinvP[:, t:t + 1], None, ALU.mult).then_inc(s_s4e, 1)

        def dense_before(t):
            return 6 * NT + DENSE_S * max(t, 0)

        def chunk_of(first, i, extra=0):
            return nc.s_assert_within(first + U * i + U * extra, 0, NCH - 1, skip_runtime_bounds_check_because="a tile's turns start before its last chunk")


        def first_chunk(eng, t):
            return eng.value_load(rng[0:1, bass.ds(t, 1)], min_val=0, max_val=MAX_FIRST)

        def turns(eng, t):
            return (eng.value_load(rng[0:1, bass.ds(NT + t, 1)], min_val=MIN_TURNS - 2, max_val=MAX_TURNS - 2),
                    eng.value_load(rng[0:1, bass.ds(2 * NT + t, 1)], min_val=0, max_val=NT * MAX_TURNS))

        def tile_turns(eng, t):
            first, (middle, before) = first_chunk(eng, t), turns(eng, t)
            total = eng.value_load(rng[0:1, 3 * NT:3 * NT + 1], min_val=0, max_val=NT * MAX_TURNS)
            return first, eng.snap(middle + 1), eng.snap(before + 2 * t), eng.snap(total + 2 * NT)

        def gather_pool(pool):
            pool.wait_ge(s_flag, 1)
            with pool.If(pool.value_load(flag[0:1, 0:1], min_val=0, max_val=1) == 1):
                for l in range(L):
                    pool.wait_ge(s_lo, NT * (l + 1))
                    if l == 0:
                        pool.wait_ge(s_agg, H * NQ)
                    pool.dma_start(m_dram.rearrange("(t p) c -> p t c", p=P), m[:, :, :, :].rearrange("p t k c -> p t (k c)")).then_inc(s_md, 16)
                    pool.wait_ge(s_md, 16 * (l + 1))
                    with pool.Fori(0, NT) as t:
                        first, last_turn, before, total = tile_turns(pool, t)
                        with pool.Fori(0, last_turn + 1) as i:
                            n = pool.snap(l * total + before + i)
                            for j in range(U):
                                pool.wait_ge(s_gf, U * (n + total) + j + 1)
                                pool.tensor_copy(gix[:, j:j + 1], srcX[:, bass.ds(chunk_of(first, i) + j, 1)]).then_inc(s_ix, 1)
                                pool.wait_ge(s_ix, U * n + j + 1)
                                pool.sem_inc(s_apart, 1)
                                pool.indirect_dma_start(grow[:, j, :, :].rearrange("p k c -> p (k c)"), None, m_dram[:, :],
                                                        bass.IndirectOffsetOnAxis(ap=gix[:, j:j + 1], axis=0)).then_inc(s_gr[l][j // 2], 16)
                            for j in range(U // 2):
                                pool.wait_ge(s_gr[l][j], 32 * (before + i + 1))
                                pool.sem_inc(s_got, 2)

        def gather_dve(dve, phase, l):
            use = phase + (0 if l is None else l)
            if phase == 0:
                dve.sem_inc(s_gf, U)
                dve.sem_inc(s_ge, 1)
            dve.tensor_copy(iotaD[:, :], iotaD0[:, :]).then_inc(s_gi, 1)
            with dve.Fori(0, NT) as t:
                first, last_turn, before, total = tile_turns(dve, t)
                dve.wait_ge(s_gi, (NT + 1) * use + t + 1)
                dve.tensor_scalar(iotaD[:, :], iotaD[:, :], float(P), None, ALU.add).then_inc(s_gi, 1)
                dve.wait_ge(s_gi, (NT + 1) * use + t + 2)
                dve.sem_inc(s_apart, 1)
                with dve.Fori(0, last_turn + 1) as i:
                    n = dve.snap(use * total + before + i)
                    c = chunk_of(first, i)
                    for j in range(U):
                        dve.wait_ge(s_gf, U * n + j + 1)
                        dve.tensor_scalar(gsel[:, j, :], iotaD[:, :], dstE[:, bass.ds(c + j, 1)], None, ALU.is_equal).then_inc(s_gs, 1)
                dve.wait_ge(s_gt, NT * use + t + 1)
                if phase:
                    tile = bass.ds(t * P, P)
                    dve.tensor_tensor(aggT[:, 0, tile], bank[0][:, 0:P], dinvB[:, tile], ALU.mult)
                    dve.tensor_tensor(aggT[:, 1, tile], bank[1][:, 0:P], dinvB[:, tile], ALU.mult).then_inc(s_ge, 1)
                else:
                    dve.sem_inc(s_ge, 1)

        def gather_pe(pe, phase, l):
            use = phase + (0 if l is None else l)
            with pe.Fori(0, NT) as t:
                first, last_turn, before, total = tile_turns(pe, t)
                pe.wait_ge(s_ge, NT * use + t + 1)

                def turn(i, start, stop_):
                    n = pe.snap(use * total + before + i)
                    for j in range(U):
                        a, b = start and j == 0, stop_ and j == U - 1
                        pe.wait_ge(s_gs, U * n + j + 1)
                        if phase:
                            pe.wait_ge(s_got, U * (l * total + before + i) + j + 1)
                            for h in range(H):
                                for k in range(2):
                                    last = pe.matmul(bank[h][:, 0:P], grow[:, j, k, h * 128:(h + 1) * 128], gsel[:, j, 0:P],
                                                     start=a and k == 0, stop=b and k == 1)
                        else:
                            last = pe.matmul(bank[6][0:P, bass.ds(t, 1)], gsel[:, j, 0:P], ones16[:, :], start=a, stop=b)
                        last.then_inc(s_gt if b else s_gf, 1)
                    if stop_:
                        pe.wait_ge(s_gt, NT * use + t + 1)
                        pe.sem_inc(s_gf, 1)

                turn(0, True, False)
                with pe.Fori(1, last_turn) as i:
                    turn(i, False, False)
                turn(last_turn, False, True)
            if phase:
                pe.wait_ge(s_ge, NT * (use + 1) + 1)


        def load_layer(sp, l):
            row = lambda a: a[bass.ds(l, 1), :]
            sp.dma_start(wraw[:, :, :], mlp_w[bass.ds(l, 1), :, :].rearrange("a (k p) c -> p (a k) c", p=128)).then_inc(s_w, 16)
            with nc.allow_non_contiguous_dma(reason="a few values for each channel"):
                for n, a in enumerate((mlp_b, bn_g, bn_b)):
                    sp.dma_start(prm[:, n, :], row(a).rearrange("a (h p) -> p (a h)", p=128)).then_inc(s_w, 16)
                sp.dma_start(ewT[:, 0, 3:4], ew1[bass.ds(l, 1), :, :].rearrange("a j c -> c (a j)")).then_inc(s_w, 16)
                sp.dma_start(ewT[:, 1, 0:3], ew2[bass.ds(l, 1), :, :].rearrange("a j c -> c (a j)")).then_inc(s_w, 16)

        LOADS = 6

        def m_rows_dve(dve, base):
            for t in range(NT):
                dve.wait_ge(s_hi, base(NT) + t + 1)
                dve.scalar_tensor_tensor(m[:, t, 1, :], bank[t % 4][0:P, 0:D], dinvP[:, t:t + 1], m[:, t, 0, :],
                                         ALU.mult, ALU.subtract).then_inc(s_lo, 1)

        def m_rows_act(act, base, normalise=None):
            if normalise:
                normalise(0)
            for t in range(NT):
                if normalise and t % (CQ // P) == 1 and t // (CQ // P) + 1 < NQ:
                    normalise(t // (CQ // P) + 1)
                act.wait_ge(s_tr, base(NT) + t + 1)
                act.activation(m[:, t, 0, :], bank[t % 4][0:P, 0:D], ACT.Copy, scale=dinvP[:, t:t + 1]).then_inc(s_hi, 1)

        def row_pe(pe, base, prev, t):
            if prev and t % (CQ // P) == 0:
                pe.wait_ge(s_h, prev(NQ) + t // (CQ // P) + 1)
            if t >= 4:
                pe.wait_ge(s_lo, base(NT) + t - 3)
            for h in range(H):
                last = pe.transpose(bank[t % 4][0:P, h * 128:(h + 1) * 128], hT[:, h, t * P:(t + 1) * P], ident[:, :])
            last.then_inc(s_tr, 1)

        LATER_BANKS = [4 + g % 4 for g in range(H * NQ)]
        FIRST_BANKS = [4, 5, 6, 7, 0, 3] + [4 + g % 4 for g in range(H * NQ - 6)]

        def dense(pe, g, s, banks=LATER_BANKS):
            (a, w), h = COLS[g // H], g % H
            for k in range(2):
                last = pe.matmul(bank[banks[g]][:, 0:w], m[:, s, k, h * 128:(h + 1) * 128], at[:, s, a:a + w],
                                 start=s == 0 and k == 0, stop=s == NT - 1 and k == 1)
            if s == NT - 1:
                last.then_inc(s_agg, 1)

        def evict(dve, base, g, banks=LATER_BANKS):
            (a, w), h = COLS[g // H], g % H
            dve.wait_ge(s_agg, base(H * NQ) + g + 1)
            dve.tensor_tensor(aggT[:, h, a:a + w], bank[banks[g]][:, 0:w], dinvB[:, a:a + w], ALU.mult).then_inc(s_agge, 1)

        def attributes_pe(pe, base):
            pe.wait_ge(s_wc, base(1) + 1)
            for h in range(H):
                last = pe.matmul(bank[3][0:K4, 0:D], ewK[:, h, :], wraw[:, H + h, :], start=h == 0, stop=h == H - 1)
            last.then_inc(s_ewp, 1)

        EW_STEPS = 8

        def attributes_dve(dve, base):
            dve.wait_ge(s_ewp, base(1) + 1)
            n = [0]

            def step(ins):
                n[0] += 1
                ins.then_inc(s_ew, 1)
                dve.wait_ge(s_ew, base(EW_STEPS) + n[0])

            v = bank[3][0:K4, 0:D]
            step(dve.tensor_copy(ewp[:, 0, :], v))
            step(dve.tensor_tensor(ewr[:, 0, :], v, ewp[:, 0, :], ALU.subtract))
            step(dve.tensor_copy(ewp[:, 1, :], ewr[:, 0, :]))
            step(dve.tensor_tensor(ewr[:, 1, :], ewr[:, 0, :], ewp[:, 1, :], ALU.subtract))
            step(dve.tensor_copy(ewp[:, 2, :], ewr[:, 1, :]))
            step(dve.tensor_scalar(ewr[:, 0, :], ewp[:, 0, :], maskK[:, 0:1], None, ALU.mult))
            step(dve.scalar_tensor_tensor(ewr[:, 1, :], ewp[:, 1, :], maskK[:, 1:2], ewr[:, 0, :], ALU.mult, ALU.add))
            step(dve.scalar_tensor_tensor(ewm[:, :], ewp[:, 2, :], maskK[:, 2:3], ewr[:, 1, :], ALU.mult, ALU.add))
            assert n[0] == EW_STEPS
            dve.sem_inc(s_ewm, 1)

        def aggregate_pe(pe, base, prev, l):
            gathers = pe.value_load(flag[0:1, 0:1], min_val=0, max_val=1)
            with pe.If(gathers == 1):
                for t in range(NT):
                    row_pe(pe, base, prev, t)
                pe.wait_ge(s_lo, base(NT) + NT)
                pe.sem_inc(s_apart, 1)
                gather_pe(pe, 1, l)
                attributes_pe(pe, base)
                pe.sem_inc(s_agg, H * NQ)
            with pe.If(gathers == 0):
                behind = 2
                for t in range(NT + behind):
                    if t < NT:
                        row_pe(pe, base, prev, t)
                    if t >= behind:
                        pe.wait_ge(s_lo, base(NT) + t - behind + 1)
                        pe.sem_inc(s_apart, 1)
                        for g in range(4):
                            dense(pe, g, t - behind)
                attributes_pe(pe, base)
                for g in range(4, H * NQ):
                    pe.wait_ge(s_agge, base(H * NQ) + g - 3)
                    pe.sem_inc(s_apart, 1)
                    for t in range(NT):
                        dense(pe, g, t)

        def linear_pe(pe, base):
            for q, (a, w) in enumerate(COLS):
                pe.wait_ge(s_agge, base(H * NQ) + H * (q + 1))
                if q >= 2:
                    pe.wait_ge(s_z, base(NQ) + q - 1)
                for h in range(H):
                    o = bank[2 * (q % 2) + h][:, 0:w]
                    for k in range(2 * H):
                        rhs = (hT if k < H else aggT)[:, k % H, a:a + w]
                        pe.matmul(o, wcur[:, k, h * 128:(h + 1) * 128], rhs, start=k == 0, stop=False)
                    if q == 0 and h == 0:
                        pe.wait_ge(s_ewm, base(1) + 1)
                    last = pe.matmul(o, ewm[:, h * 128:(h + 1) * 128], s4T[:, a:a + w], start=False, stop=True)
                last.then_inc(s_mlp, 1)

        def weights_dve(dve, loads):
            dve.wait_ge(s_w, 16 * loads)
            for k in range(2 * H):
                dve.tensor_scalar(wcur[:, k, :], wraw[:, k, :], inv[:, k % H:k % H + 1], None, ALU.mult)
            last = dve.tensor_copy(ewK[:, :, :].rearrange("p h (k j) -> p h k j", j=4), ewT[:, :, :].unsqueeze(2).to_broadcast([128, H, K4 // 4, 4]))
            last.then_inc(s_wc, 1)

        def aggregate_dve(dve, base, l, loads):
            m_rows_dve(dve, base)
            weights_dve(dve, loads)
            gathers = dve.value_load(flag[0:1, 0:1], min_val=0, max_val=1)
            with dve.If(gathers == 1):
                gather_dve(dve, 1, l)
                attributes_dve(dve, base)
                dve.sem_inc(s_agge, H * NQ)
            with dve.If(gathers == 0):
                for g in range(H * NQ):
                    evict(dve, base, g)
                    if g == 3:
                        attributes_dve(dve, base)

        def statistics_dve(dve, base, last_layer):
            count = [0]

            def step(ins):
                count[0] += 1
                ins.then_inc(s_ls, 1)
                dve.wait_ge(s_ls, base(LAYER_STEPS) + count[0])

            gain, offset = prm[:, 1, :], prm[:, 2, :]
            ve, sd, rt, tmp = (cf[:, n, :] for n in (0, 1, 2, 3))
            if not last_layer:
                step(dve.scalar_tensor_tensor(tmp, gain, -1.0, gain, ALU.mult, ALU.max))
                step(dve.scalar_tensor_tensor(sd, offset, -1.0, offset, ALU.mult, ALU.max))
                step(dve.scalar_tensor_tensor(tmp, tmp, 56.0, sd, ALU.mult, ALU.add))
                step(dve.tensor_scalar(tmp, tmp, 2.0 ** -80, 2.0 ** 100, ALU.max, ALU.min))
                step(dve.tensor_scalar(cfi[:, 0, :], tmp.bitcast(I32), 0x7F800000, None, ALU.bitwise_and))
                step(dve.tensor_scalar(cfi[:, 1, :], cfi[:, 0, :], -1.0, float((254 + 14) << 23), ALU.mult, ALU.add))
                step(dve.tensor_scalar(inv[:, :].bitcast(I32), cfi[:, 0, :], float(-(14 << 23)), None, ALU.add))
                step(dve.tensor_tensor(gain, gain, cfi[:, 1, :].bitcast(F32), ALU.mult))
                step(dve.tensor_tensor(offset, offset, cfi[:, 1, :].bitcast(F32), ALU.mult))
            for q, (a, w) in enumerate(COLS):
                dve.wait_ge(s_z, base(NQ) + q + 1)
                for h in range(H):
                    last = dve.bn_stats(zst[:, h, q, :], hT[:, h, a:a + w])
            step(last)
            dve.sem_inc(s_apart, 1)
            for h in range(H):
                last = dve.bn_aggr(zmv[:, h, :], zst[:, h, :, :].rearrange("p q s -> p (q s)"))
            step(last)
            dve.tensor_scalar(ve, zmv[:, :, 1], BN_EPS, None, ALU.add).then_inc(s_bv, 1)
            dve.wait_ge(s_bs, base(1) + 1)
            step(dve.reciprocal(rt, sd))
            step(dve.tensor_tensor(tmp, rt, rt, ALU.mult))
            step(dve.tensor_tensor(tmp, tmp, ve, ALU.mult))
            step(dve.tensor_scalar(tmp, tmp, -0.5, 1.5, ALU.mult, ALU.add))
            step(dve.tensor_tensor(rt, rt, tmp, ALU.mult))
            slope, shift = cf[:, 4, :], cf[:, 5, :]
            step(dve.tensor_tensor(slope, rt, gain, ALU.mult))
            step(dve.tensor_tensor(tmp, zmv[:, :, 0], slope, ALU.mult))
            step(dve.tensor_tensor(shift, offset, tmp, ALU.subtract))
            if not last_layer:
                assert count[0] == LAYER_STEPS, count
            dve.sem_inc(s_bn, 1)

        def normalise_act(act, prev, last_layer):
            def normalise(q):
                if q == 0:
                    act.wait_ge(s_bn, prev(1) + 1)
                a, w = COLS[q]
                for h in range(H):
                    last = act.activation(hT[:, h, a:a + w], hT[:, h, a:a + w], ACT.Identity if last_layer else ACT.Relu,
                                          bias=cf[:, 5, h:h + 1], scale=cf[:, 4, h:h + 1])
                last.then_inc(s_h, 1)
            return normalise

        def linear_act(act, base):
            for q, (a, w) in enumerate(COLS):
                act.wait_ge(s_mlp, base(NQ) + q + 1)
                for h in range(H):
                    last = act.activation(hT[:, h, a:a + w], bank[2 * (q % 2) + h][:, 0:w], ACT.Relu, bias=prm[:, 0, h:h + 1])
                last.then_inc(s_z, 1)
            act.wait_ge(s_bv, base(1) + 1)
            act.activation(cf[:, 1, :], cf[:, 0, :], ACT.Sqrt).then_inc(s_bs, 1)

        LAYER_STEPS = 19


        FW = 16 * (3 + 1 + NE)
        R_PIECES = ((0, NT // 2), (NT // 2, NT))

        def experts_sp(sp):
            sp.wait_ge(s_agg, L * H * NQ)
            sp.dma_start(x2[:, :, :], x.rearrange("(t p) d -> p t d", p=P)).then_inc(s_x2, 16)
            sp.dma_start(b2B[:, :, :], b2.rearrange("(a e) f -> a e f", a=1).to_broadcast([128, NE, D])).then_inc(s_fw, 16)
            with nc.allow_non_contiguous_dma(reason="a few values for each hidden channel"):
                for e in range(NE):
                    sp.dma_start(b1T[:, e, :], b1[e:e + 1, :].rearrange("a (k p) -> p (a k)", p=128)).then_inc(s_fw, 16)
            sp.wait_ge(s_h, L * NQ)
            sp.dma_start(w1s[:, :, :, :].rearrange("p e k f -> p (e k) f"), w1.rearrange("e (k p) f -> p (e k) f", p=128)).then_inc(s_w1, 16)
            sp.wait_ge(s_oT, NT)
            sp.dma_start(w2s[:, :, :, :].rearrange("p e k d -> p (e k) d"), w2.rearrange("e (k p) d -> p (e k) d", p=128)).then_inc(s_w2, 16)
            sp.wait_ge(s_oTe, NT)
            sp.dma_start(out[0:N, :].rearrange("(t p) d -> p t d", p=P), x2[:, :, :]).then_inc(s_res, 16)
            sp.wait_ge(s_cst, 1)
            sp.dma_start(out[N:N + TT, :], zt[:, :]).then_inc(s_res, 16)
            sp.wait_ge(s_fn, NT)
            sp.dma_start(xn_dram.rearrange("(t p) d -> p t d", p=P), xn[:, :, :]).then_inc(s_xnd, 16)

        def experts_pool(pool, step):
            for n in range(2):
                pool.wait_ge(s_place, n + 1)
                byJ = idJ[:, n, :, 0, :]
                step(pool.tensor_tensor(idJ[:, n, :, 1, :], byJ, wts[:, 2 - n, :].unsqueeze(2).to_broadcast([P, NT, J]), ALU.mult))
                pool.tensor_tensor(byJ, byJ, iotaN[:, :].unsqueeze(2).to_broadcast([P, NT, J]), ALU.mult).then_inc(s_tabP, 1)
            pool.wait_ge(s_xnd, 16)
            pool.wait_ge(s_tab, 1)

            def gather(j, k):
                pool.tensor_copy(nowG[:, k:k + 1], rowG[:, bass.ds(j, 1)]).then_inc(s_nowG, 1)
                pool.wait_ge(s_nowG, j + 1)
                pool.sem_inc(s_apart, 1)
                pool.indirect_dma_start(xtb[:, k, :], None, xn_dram[:, :], bass.IndirectOffsetOnAxis(ap=nowG[:, k:k + 1], axis=0)).then_inc(s_xt[k], 16)

            def accumulate(j, k):
                pool.tensor_copy(nowS[:, k:k + 1], rowS[:, bass.ds(j, 1)]).then_inc(s_nowS, 1)
                pool.wait_ge(s_nowS, j + 1)
                pool.wait_ge(s_yb, j + 1)
                pool.sem_inc(s_apart, 1)
                pool.indirect_dma_start(out[:, :], bass.IndirectOffsetOnAxis(ap=nowS[:, k:k + 1], axis=0), ytb[:, k, :], None,
                                        compute_op=ALU.add).then_inc(s_acc, 16)

            def group(g, first, last):
                for k in range(XB):
                    j = XB * g + k
                    if not last:
                        pool.wait_ge(s_xtT, j + 1)
                        gather(j + XB, k)
                    if not (first and k == 0):
                        pool.wait_ge(s_acc, 16 * j)
                    accumulate(j, k)

            for k in range(XB):
                gather(k, k)
            pool.wait_ge(s_res, 32)
            pool.wait_ge(s_tab, 2)
            group(0, True, False)
            with pool.Fori(1, J // XB - 1) as g:
                group(g, False, False)
            group(J // XB - 1, False, True)
            pool.wait_ge(s_acc, 16 * J)

        def experts_act(act):
            act.wait_ge(s_fve, 1)
            act.activation(fsd[:, :], fve[:, :], ACT.Sqrt).then_inc(s_fsd, 1)
            per = CQ // P

            def logits(q):
                a, w = COLS[q]
                act.wait_ge(s_gl, q + 1)
                act.activation(lgT[:, a:a + w], bank[4 + q % 2][0:NE, 0:w], ACT.Identity, bias=gbs[:, :]).then_inc(s_glc, 1)

            for t in range(NT):
                q = t // per
                if q >= 2 and t % per == 0:
                    act.wait_ge(s_gl, q - 1)
                act.wait_ge(s_gT, t + 1)
                act.activation(xnT[:, q % 2, :, t % per * P:(t % per + 1) * P], bank[t % 4][:, 0:H * P].rearrange("p (h n) -> p h n", h=H), ACT.Copy).then_inc(s_gTe, 1)
                if q == 1 and t % per == 0:
                    act.wait_ge(s_gbs, 1)
                if q and t % per == 1:
                    logits(q - 1)
            if NT % per == 1:
                logits(NQ - 2)
            logits(NQ - 1)
            act.wait_ge(s_ex, 1)
            act.activation(wts[:, 1, :], wts[:, 0, :], ACT.Exp).then_inc(s_exd, 1)

            def rows(j, u):
                act.wait_ge(s_xtT, j + 1)
                act.activation(xtT[:, u, :, :], bank[u][:, 0:H * TT].rearrange("p (h n) -> p h n", h=H), ACT.Copy).then_inc(s_xtc, 1)

            def hidden(j, u):
                e = act.value_load(te[0:1, bass.ds(j, 1)], min_val=0, max_val=NE - 1)
                act.wait_ge(s_hT, j + 1)
                for k in range(FK):
                    last = act.activation(h1T[:, u, k, :], bank[4 + u][:, k * TT:(k + 1) * TT], ACT.Relu,
                                          bias=b1T[:, bass.ds(e, 1), k:k + 1].rearrange("p a b -> p (a b)"))
                last.then_inc(s_hTc, 1)

            act.wait_ge(s_slot, 1)
            act.wait_ge(s_fw, FW)
            rows(0, 0)
            rows(1, 1)
            hidden(0, 0)
            with act.Fori(0, (J - 2) // 2) as i:
                for u in range(2):
                    j = act.snap(2 * i + u)
                    rows(j + 2, u)
                    hidden(j + 1, 1 - u)
            hidden(J - 1, 1)

        def experts_dve(dve, step, rounded, inverse_root):
            dve.wait_ge(s_x2, 16)
            for t in range(NT):
                dve.wait_ge(s_oT, t + 1)
                dve.tensor_tensor(x2[:, t, :], x2[:, t, :], bank[t % 4][0:P, 0:D], ALU.add).then_inc(s_oTe, 1)
                if t:
                    dve.wait_ge(s_oTe, t)
                    dve.bn_stats(fst[:, t - 1, :], x2[:, t - 1, :])
            dve.wait_ge(s_oTe, NT)
            step(dve.bn_stats(fst[:, NT - 1, :], x2[:, NT - 1, :]))
            for t in range(NT):
                last = dve.bn_aggr(fmv[:, t, :], fst[:, t, :])
            step(last)
            dve.tensor_scalar(fve[:, :], fmv[:, :, 1], LN_EPS, None, ALU.add).then_inc(s_fve, 1)
            dve.wait_ge(s_fsd, 1)
            inverse_root(frs[:, :], fve[:, :], fsd[:, :], ft1[:, :])
            dve.wait_ge(s_fw, FW)
            dve.tensor_tensor(gbs[:, :], gbr[:, 0:1], gbr[:, 1:2], ALU.add).then_inc(s_gbs, 1)
            for t in range(NT):
                dve.tensor_scalar(xn[:, t, :], x2[:, t, :], fmv[:, t, 0:1], frs[:, t:t + 1], ALU.subtract, ALU.mult).then_inc(s_fn, 1)
            dve.wait_ge(s_cst, 2)
            dve.wait_ge(s_gate, 1)
            step(dve.tensor_copy(lgt[:, :, :].rearrange("p t e -> p (t e)"), bank[6][0:P, 0:NT * NE]))
            for t in range(NT):
                last = dve.max(top[:, t, :], lgt[:, t, :])
            step(last)
            for t in range(NT):
                last = dve.max_index(tix[:, t, :], top[:, t, :], lgt[:, t, :])
            step(last)
            dve.tensor_tensor(wts[:, 0, :], top[:, :, 1], top[:, :, 0], ALU.subtract).then_inc(s_ex, 1)
            step(dve.tensor_copy(ef[:, 0, :], tix[:, :, 0]))
            step(dve.tensor_copy(ef[:, 1, :], tix[:, :, 1]))
            by8 = iota8[:, :].unsqueeze(1).to_broadcast([P, NT, NE])
            for n, o in enumerate((oh1, oh2)):
                step(dve.tensor_tensor(o[:, :, :], ef[:, n, :].unsqueeze(2).to_broadcast([P, NT, NE]), by8, ALU.is_equal))
            dve.tensor_tensor(msk[:, :, :], oh1[:, :, :], oh2[:, :, :], ALU.add).then_inc(s_msk, 1)
            dve.wait_ge(s_exd, 1)
            step(dve.tensor_scalar(wts[:, 0, :], wts[:, 1, :], 1.0, None, ALU.add))
            step(dve.reciprocal(wts[:, 2, :], wts[:, 0, :]))
            step(dve.tensor_tensor(wts[:, 1, :], wts[:, 1, :], wts[:, 2, :], ALU.mult))
            dve.wait_ge(s_rank, 1)
            step(dve.tensor_copy(cnt[:, :, :].rearrange("p t e -> p (t e)"), bank[1][0:P, 0:NT * NE]))
            for e in range(NE):
                last = dve.tensor_tensor_scan(incl[:, :, e], ones[0:P, 0:NT], cnt[:, :, e], 0.0, ALU.mult, ALU.add)
            step(last)
            total, tiles, end, start = (nte[:, n, :] for n in range(4))
            step(dve.tensor_scalar(total, incl[:, NT - 1, :], 1.0 / TT, (TT - 1) / (2 * TT), ALU.mult, ALU.add))
            rounded(tiles, total, start)
            step(dve.tensor_tensor_scan(end, ones[0:P, 0:NE], tiles, 0.0, ALU.mult, ALU.add))
            step(dve.tensor_tensor(start, end, tiles, ALU.subtract))
            step(dve.tensor_scalar(start, start, float(TT), None, ALU.mult))
            step(dve.tensor_tensor(slm[:, :, :], incl[:, :, :], cnt[:, :, :], ALU.subtract))
            step(dve.tensor_tensor(slm[:, :, :].rearrange("p t e -> p (t e)"), slm[:, :, :].rearrange("p t e -> p (t e)"), bank[0][0:P, 0:NT * NE], ALU.add))
            step(dve.tensor_tensor(slm[:, :, :], slm[:, :, :], start.unsqueeze(1).to_broadcast([P, NT, NE]), ALU.add))
            for n, o in enumerate((oh1, oh2)):
                step(dve.tensor_tensor(o[:, :, :], o[:, :, :], slm[:, :, :], ALU.mult))
                step(dve.tensor_reduce(slf[:, n, :], o[:, :, :], axis=XYZ, op=ALU.add))
            step(dve.tensor_tensor(cmpJ[:, :, :], nte[0:1, 2, :].unsqueeze(1).to_broadcast([1, J, NE]),
                                   iotaJ[0:1, :].unsqueeze(2).to_broadcast([1, J, NE]), ALU.is_le))
            step(dve.tensor_reduce(teF[:, :], cmpJ[:, :, :], axis=XYZ, op=ALU.add))
            dve.tensor_scalar(te[:, :], teF[:, :], float(NE - 1), None, ALU.min).then_inc(s_slot, 1)
            step(dve.tensor_scalar(sltile[:, :, :], slf[:, :, :], -(TT - 1) / 2, 1.0 / TT, ALU.add, ALU.mult))
            rounded(sltile[:, :, :], sltile[:, :, :], slplace[:, :, :])
            step(dve.scalar_tensor_tensor(slplace[:, :, :], sltile[:, :, :], float(-TT), slf[:, :, :], ALU.mult, ALU.add))
            for n in range(2):
                dve.tensor_tensor(idJ[:, n, :, 0, :], iotaJ[:, :].unsqueeze(1).to_broadcast([P, NT, J]),
                                  sltile[:, n, :].unsqueeze(2).to_broadcast([P, NT, J]), ALU.is_equal).then_inc(s_place, 1)
            for n in range(2):
                for k, (a, b) in enumerate(R_PIECES):
                    if n:
                        dve.wait_ge(s_idw, k + 1)
                    dve.tensor_tensor(ohR[:, a:b, :], iotaT[:, :].unsqueeze(1).to_broadcast([P, b - a, TT]),
                                      slplace[:, n, a:b].unsqueeze(2).to_broadcast([P, b - a, TT]), ALU.is_equal).then_inc(s_R, 1)
            dve.wait_ge(s_idw, 2 * len(R_PIECES))
            ids = bank[2][:, 0:J]
            dve.tensor_scalar(rowG[:, :], ids, -1.0, 0.0, ALU.add, ALU.max).then_inc(s_tab, 1)
            step(dve.tensor_copy(wS[:, :], bank[2][:, J:2 * J]))
            step(dve.tensor_scalar(rowid[:, :], ids, -1.0, None, ALU.add))
            step(dve.tensor_scalar(pad[:, :], ids, 0.0, iotaX[:, :], ALU.is_equal, ALU.mult))
            dve.tensor_tensor(rowS[:, :], rowid[:, :], pad[:, :], ALU.add).then_inc(s_tab, 1)

            def result(j, u, k, free):
                e = dve.value_load(te[0:1, bass.ds(j, 1)], min_val=0, max_val=NE - 1)
                dve.wait_ge(s_y, j + 1)
                dve.tensor_tensor(ytt[:, u, :], bank[6 + u][:, 0:D], b2B[:, bass.ds(e, 1), :].rearrange("p a f -> p (a f)"), ALU.add).then_inc(s_yt, 1)
                dve.wait_ge(s_yt, j + 1)
                if free is not None:
                    dve.wait_ge(s_acc, free)
                dve.tensor_scalar(ytb[:, k, :], ytt[:, u, :], wS[:, bass.ds(j, 1)], None, ALU.mult).then_inc(s_yb, 1)

            def hidden(j, u):
                dve.wait_ge(s_h1, j + 1)
                dve.tensor_copy(h1[:, u, :], bank[2 + u][:, :]).then_inc(s_h1c, 1)

            def group(g, first, last):
                for k in range(XB):
                    j = XB * g + k
                    if not (last and k == XB - 1):
                        hidden(j + 1, (k + 1) % 2)
                    result(j, k % 2, k, None if first else 16 * (XB * before + k + 1))

            hidden(0, 0)
            group(0, True, False)
            with dve.Fori(0, J // XB - 2) as before:
                group(before + 1, False, False)
            before = J // XB - 2
            group(J // XB - 1, False, True)

        def experts_pe(pe):
            for t in range(NT):
                if t % (CQ // P) == 0:
                    pe.wait_ge(s_h, NQ * (L - 1) + t // (CQ // P) + 1)
                if t >= 4:
                    pe.wait_ge(s_oTe, t - 3)
                for h in range(H):
                    last = pe.transpose(bank[t % 4][0:P, h * 128:(h + 1) * 128], hT[:, h, t * P:(t + 1) * P], ident[:, :])
                last.then_inc(s_oT, 1)

            def rows_up(t):
                pe.wait_ge(s_fn, t + 1)
                if t >= 4:
                    pe.wait_ge(s_gTe, t - 3)
                for h in range(H):
                    last = pe.transpose(bank[t % 4][:, h * P:(h + 1) * P], xn[:, t, h * 128:(h + 1) * 128], ident[0:P, 0:P])
                last.then_inc(s_gT, 1)

            def block_up(q):
                for t in range(COLS[q][0] // P, sum(COLS[q]) // P):
                    rows_up(t)

            def back(q):
                pe.wait_ge(s_glc, q + 1)
                for t in range(COLS[q][0] // P, sum(COLS[q]) // P):
                    last = pe.transpose(bank[6][0:P, t * NE:(t + 1) * NE], lgT[:, t * P:(t + 1) * P], ident[0:NE, 0:NE])
                return last

            block_up(0)
            for q, (a, w) in enumerate(COLS):
                if q + 1 < NQ:
                    block_up(q + 1)
                pe.wait_ge(s_gTe, (a + w) // P)
                if q >= 2:
                    pe.wait_ge(s_glc, q - 1)
                for h in range(H):
                    last = pe.matmul(bank[4 + q % 2][0:NE, 0:w], wgs[:, h, :], xnT[:, q % 2, h, 0:w], start=h == 0, stop=h == H - 1)
                last.then_inc(s_gl, 1)
                if q:
                    back(q - 1)
            back(NQ - 1).then_inc(s_gate, 1)
            pe.wait_ge(s_msk, 1)
            flat = msk[:, :, :].rearrange("p t e -> p (t e)")
            pe.matmul(bank[0][0:P, 0:NT * NE], tri[:, :], flat, start=True, stop=True)
            pe.matmul(bank[1][0:P, 0:NT * NE], ones[0:P, 0:P], flat, start=True, stop=True).then_inc(s_rank, 1)
            for n in range(2):
                pe.wait_ge(s_tabP, n + 1)
                for k, (a, b) in enumerate(R_PIECES):
                    pe.wait_ge(s_R, len(R_PIECES) * n + k + 1)
                    for t in range(a, b):
                        last = pe.matmul(bank[2][:, 0:2 * J], ohR[:, t, :], idJ[:, n, t, :, :].rearrange("p a j -> p (a j)"),
                                         start=n == 0 and t == 0, stop=n == 1 and t == NT - 1)
                    last.then_inc(s_idw, 1)
            pe.wait_ge(s_slot, 1)
            pe.wait_ge(s_tab, 2)
            pe.wait_ge(s_w1, 16)
            pe.wait_ge(s_w2, 16)

            def rows(j, u, k, gathered):
                pe.wait_ge(s_xt[k], gathered)
                for h in range(H):
                    last = pe.transpose(bank[u][:, h * TT:(h + 1) * TT], xtb[:, k, h * 128:(h + 1) * 128], ident[:, :])
                last.then_inc(s_xtT, 1)

            def up(j, u):
                e = pe.value_load(te[0:1, bass.ds(j, 1)], min_val=0, max_val=NE - 1)
                pe.wait_ge(s_xtc, j + 1)
                for h in range(H):
                    last = pe.matmul(bank[2 + u][:, :], xtT[:, u, h, :], w1s[:, bass.ds(e, 1), h, :].rearrange("p a f -> p (a f)"), start=h == 0, stop=h == H - 1)
                last.then_inc(s_h1, 1)

            def across(j, u):
                pe.wait_ge(s_h1c, j + 1)
                for k in range(FK):
                    last = pe.transpose(bank[4 + u][:, k * TT:(k + 1) * TT], h1[:, u, k * 128:(k + 1) * 128], ident[:, :])
                last.then_inc(s_hT, 1)

            def down(j, u, free):
                e = pe.value_load(te[0:1, bass.ds(j, 1)], min_val=0, max_val=NE - 1)
                pe.wait_ge(s_hTc, j + 1)
                if free is not None:
                    pe.wait_ge(s_yb, free)
                for k in range(FK):
                    last = pe.matmul(bank[6 + u][:, 0:D], h1T[:, u, k, :], w2s[:, bass.ds(e, 1), k, :].rearrange("p a f -> p (a f)"), start=k == 0, stop=k == FK - 1)
                last.then_inc(s_y, 1)

            def group(g, first, last_group):
                for k in range(XB):
                    j = XB * g + k
                    u = k % 2
                    if not (last_group and k == XB - 1):
                        up(j + 1, 1 - u)
                    if not (last_group and k >= XB - 2):
                        n = k + 2
                        rows(j + 2, u, n % XB, 16 * (g + n // XB + 1))
                    down(j, u, None if first and k < 2 else j - 1)
                    if not (last_group and k == XB - 1):
                        across(j + 1, 1 - u)

            rows(0, 0, 0, 16)
            rows(1, 1, 1, 16)
            up(0, 0)
            across(0, 0)
            group(0, True, False)
            with pe.Fori(1, J // XB - 1) as g:
                group(g, False, False)
            group(J // XB - 1, False, True)

        @block.sync
        def _(sp):
            tail_dmas(sp, dstI, dst, 1, s_dst)
            tail_dmas(sp, srcI, src, 1, s_src)
            tail_dmas(sp, eaC, edge_attr.rearrange("e j -> (e j)"), 4, s_ea)
            sp.dma_start(xin[:, :, :], x.rearrange("(t p) d -> p t d", p=P)).then_inc(s_x, 16)
            sp.dma_start(wgs[:, :, :], wg.rearrange("(h p) e -> p h e", p=128)).then_inc(s_fw, 16)
            sp.dma_start(gbr[:, 0:1], bg.rearrange("(e a) -> e a", a=1)).then_inc(s_fw, 16)
            sp.dma_start(gbr[:, 1:2], gbias.rearrange("(e a) -> e a", a=1)).then_inc(s_fw, 16)
            sp.wait_ge(s_slC, 1)
            sp.dma_start(sl_dram.rearrange("(b p e) -> p b e", b=NB, p=CB), slC[:, :, :]).then_inc(s_sld, 16)
            sp.wait_ge(s_sld, 16)
            sp.wait_ge(s_dpart, 1)
            row = sl_dram.rearrange("(b e) -> b e", b=NLB)

            def places(b):
                sp.dma_start(slrow[:, b % 2, :], row[b:b + 1, :].to_broadcast([P, LB * CH])).then_inc(s_slr[b % 2], 16)

            places(0)
            places(1)
            sp.wait_ge(s_dB, 1)
            sp.dma_start(dinv_dram.rearrange("(t p) -> t p", p=P), dinvT[:, :]).then_inc(s_dBd, 16)
            sp.wait_ge(s_dBd, 16)
            sp.dma_start(dinvB[:, :], dinv_dram.rearrange("(a n) -> a n", a=1).to_broadcast([128, N])).then_inc(s_dBd, 16)
            for b in range(2, NLB):
                sp.wait_ge(s_ohT, b - 1)
                places(b)
            sp.wait_ge(s_s4, NT)
            sp.wait_ge(s_ez, 1)
            load_layer(sp, 0)
            with sp.Fori(1, L) as l:
                sp.wait_ge(s_bn, l)
                load_layer(sp, l)
            experts_sp(sp)

        @block.gpsimd
        def _(pool):
            done = [0]

            def step(ins):
                done[0] += 1
                ins.then_inc(s_po, 1)
                pool.wait_ge(s_po, done[0])

            pool.memset(dstI[:, NB - 1, :], DST_PAD)
            pool.memset(srcI[:, NB - 1, :], 0)
            pool.memset(eaC[:, NB - 1, :], 0.0).then_inc(s_mem, 1)
            step(pool.memset(ident[:, :], 0.0))
            pool.affine_select(out=ident[:, :], in_=ident[:, :], compare_op=ALU.not_equal, fill=1.0, base=0,
                               pattern=[[-1, 128]], channel_multiplier=1)
            pool.memset(ones[:, :], 1.0)
            pool.memset(ones16[:, :], 1.0).then_inc(s_mem, 1)
            pool.iota(cidx[:, :], pattern=[[1, NCH]], base=0, channel_multiplier=0, allow_small_or_imprecise_dtypes=True)
            pool.iota(tlo[:, :], pattern=[[0, 1]], base=0, channel_multiplier=P, allow_small_or_imprecise_dtypes=True)
            pool.iota(iotaP[:, :], pattern=[[0, 1]], base=0, channel_multiplier=1, allow_small_or_imprecise_dtypes=True)
            pool.iota(iotaK[:, 0, 0:GROUPS * P], pattern=[[KEY, GROUPS], [1, P]], base=0, channel_multiplier=0)
            pool.iota(iotaK[:, 1, 0:GROUPS * P], pattern=[[KEY, GROUPS], [1, P]], base=P, channel_multiplier=0)
            pool.memset(iotaK[:, :, GROUPS * P:GW], -32000)
            pool.iota(iotaS[:, :, :], pattern=[[1, 128], [0, U]], base=0, channel_multiplier=0)
            pool.iota(iotaD3[:, :, :], pattern=[[1, P], [0, U]], base=-P, channel_multiplier=0)
            pool.iota(iotaD0[:, :], pattern=[[1, P + 1]], base=-P, channel_multiplier=0)
            pool.iota(iota25[:, :], pattern=[[1, NT]], base=0, channel_multiplier=0).then_inc(s_mem, 1)
            pool.memset(zt[:, :], 0.0).then_inc(s_cst, 1)
            step(pool.memset(tri[:, :], 1.0))
            pool.affine_select(out=tri[:, :], in_=tri[:, :], compare_op=ALU.is_gt, fill=0.0, base=0,
                               pattern=[[1, P]], channel_multiplier=-1)
            pool.iota(iota8[:, :], pattern=[[1, NE]], base=0, channel_multiplier=0, allow_small_or_imprecise_dtypes=True)
            pool.iota(iotaT[:, :], pattern=[[1, TT]], base=0, channel_multiplier=0, allow_small_or_imprecise_dtypes=True)
            pool.iota(iotaN[:, :], pattern=[[P, NT]], base=1, channel_multiplier=1, allow_small_or_imprecise_dtypes=True)
            pool.iota(iotaX[:, :], pattern=[[0, 1]], base=N + 1, channel_multiplier=1, allow_small_or_imprecise_dtypes=True)
            pool.iota(iotaJ[:, :], pattern=[[1, J]], base=0, channel_multiplier=0, allow_small_or_imprecise_dtypes=True).then_inc(s_cst, 1)
            for t in range(2, NT):
                pool.wait_ge(s_oh[2], t - 1)
                pool.iota(iotaK[:, t % 2, 0:GROUPS * P], pattern=[[KEY, GROUPS], [1, P]], base=P * t, channel_multiplier=0).then_inc(s_iotaK, 1)
            gather_pool(pool)
            experts_pool(pool, step)

        @block.vector
        def _(dve):
            done = [0]

            def step(ins):
                done[0] += 1
                ins.then_inc(s_dv, 1)
                dve.wait_ge(s_dv, done[0])

            def inverse_root(root, v, sd, tmp):
                step(dve.reciprocal(root, sd))
                step(dve.tensor_tensor(tmp, root, root, ALU.mult))
                step(dve.tensor_tensor(tmp, tmp, v, ALU.mult))
                step(dve.tensor_scalar(tmp, tmp, -0.5, 1.5, ALU.mult, ALU.add))
                step(dve.tensor_tensor(root, root, tmp, ALU.mult))

            def rounded(dst_ap, src_ap, tmp):
                step(dve.tensor_scalar(tmp, src_ap, MAGIC, None, ALU.add))
                step(dve.tensor_scalar(dst_ap, tmp, MAGIC, None, ALU.subtract))

            dve.wait_ge(s_dst, 48)
            dve.tensor_copy(dstC[:, :, :], dstI[:, :, :]).then_inc(s_edges, 1)
            dve.wait_ge(s_src, 48)
            dve.tensor_copy(srcC[:, :, :], srcI[:, :, :]).then_inc(s_edges, 1)
            dve.wait_ge(s_edges, 2)
            dve.tensor_reduce(cmm[:, 0, :], dstC[:, :, :], axis=XYZ, op=ALU.min)
            step(dve.tensor_reduce(cmm[:, 1, :], dstC[:, :, :], axis=XYZ, op=ALU.max))
            dve.tensor_copy(cmmB[:, :, :], cmm[:, :, :].rearrange("p a b -> p (a b)").unsqueeze(2).to_broadcast([CB, 2 * NB, NT])).then_inc(s_cmm, 1)
            sc = srcC[:, :, :].rearrange("p b e -> p (b e)")
            step(dve.tensor_scalar(ta[0:CB, :], sc, float(-(P // 2)), 1.0 / P, ALU.add, ALU.mult))
            rounded(tb[0:CB, :], ta[0:CB, :], ta[0:CB, :])
            dve.scalar_tensor_tensor(slC[:, :, :].rearrange("p b e -> p (b e)"), tb[0:CB, :], float(-P), sc, ALU.mult, ALU.add).then_inc(s_slC, 1)
            dve.wait_ge(s_tp, 8)
            srcE = ta[:, 0:NCH]
            step(dve.memset(srcX[:, NCH:NCHP], 0))
            step(dve.tensor_copy(srcX[:, 0:NCH], bank[1][:, 0:NCH]))
            tileE = tb[:, 0:NCH]
            step(dve.memset(dstE[:, NCH:NCHP], float(DST_PAD)))
            step(dve.memset(keyE[:, NCH:NCHP], float(DST_PAD)))
            step(dve.memset(powE[:, NCH:NCHP], 0))
            step(dve.memset(sl16[:, NCH:NCHP], 0))
            step(dve.memset(dst3[:, NCH:NCHP], DST_PAD))
            step(dve.tensor_copy(dst3[:, 0:NCH], bank[0][:, 0:NCH]))
            step(dve.tensor_copy(dstE[:, 0:NCH], bank[0][:, 0:NCH]))
            step(dve.tensor_copy(srcE, bank[1][:, 0:NCH]))
            step(dve.tensor_scalar(tg[:, :], srcE, float(-(P // 2)), 1.0 / P, ALU.add, ALU.mult))
            rounded(tileE, tg[:, :], tg[:, :])
            step(dve.scalar_tensor_tensor(sl16[:, 0:NCH], tileE, float(-P), srcE, ALU.mult, ALU.add))
            step(dve.tensor_copy(s16[:, :], tileE))
            step(dve.tensor_scalar(srcE, tileE, -(FIELDS - 1) / 2, 1.0 / FIELDS, ALU.add, ALU.mult))
            rounded(tg[:, :], srcE, srcE)
            step(dve.scalar_tensor_tensor(keyE[:, 0:NCH], tg[:, :], float(KEY), dstE[:, 0:NCH], ALU.mult, ALU.add))
            step(dve.scalar_tensor_tensor(srcE, tg[:, :], float(-FIELDS), tileE, ALU.mult, ALU.add))
            step(dve.tensor_scalar(srcE, srcE, 4.0, 127.0, ALU.mult, ALU.add))
            step(dve.tensor_scalar(powE[:, 0:NCH], srcE, float(2 ** 23), None, ALU.mult))
            dve.wait_ge(s_tp, 12)
            for j in range(4):
                dve.wait_ge(s_tp, 9 + j)
                dve.tensor_copy(eaE[:, :, j], bank[2 + j][:, 0:NCH])
            dve.wait_ge(s_mem, 3)
            step(dve.tensor_scalar(rowK[:, 0:1], iotaP[0:K4, :], -(K4 // PARTS - 1) / 2, PARTS / K4, ALU.add, ALU.mult))
            rounded(rowK[:, 0:1], rowK[:, 0:1], rowK[:, 1:2])
            for a in range(PARTS):
                dve.tensor_scalar(maskK[:, a:a + 1], rowK[:, 0:1], float(a), None, ALU.is_equal)
            dve.wait_ge(s_minmax, 2)
            step(dve.tensor_scalar(lohi2[:, 0:1], tlo[:, :], float(P - 1), None, ALU.add))
            step(dve.tensor_scalar(m1[:, :], bank[6][0:NT, 0:NCH], lohi2[:, 0:1], None, ALU.is_le))
            step(dve.tensor_scalar(m2[:, :], bank[7][0:NT, 0:NCH], tlo[:, :], None, ALU.is_ge))
            step(dve.tensor_tensor(m1[:, :], m1[:, :], m2[:, :], ALU.mult))
            step(dve.scalar_tensor_tensor(m2[:, :], m1[:, :], -BIG, cidx[:, :], ALU.mult, ALU.add))
            step(dve.tensor_reduce(lohi[:, 0:1], m2[:, :], axis=XYZ, op=ALU.min))
            step(dve.scalar_tensor_tensor(m2[:, :], cidx[:, :], 1.0, m1[:, :], ALU.add, ALU.mult))
            step(dve.tensor_reduce(lohi[:, 1:2], m2[:, :], axis=XYZ, op=ALU.max))
            step(dve.tensor_scalar(lohi2[:, 0:1], lohi[:, 0:1], BIG, float(MAX_FIRST), ALU.add, ALU.min))
            step(dve.tensor_tensor(lohi[:, 1:2], lohi[:, 1:2], lohi2[:, 0:1], ALU.subtract))
            step(dve.tensor_scalar(lohi[:, 1:2], lohi[:, 1:2], 1.0 / U, (U - 1) / (2 * U) - 2.0, ALU.mult, ALU.add))
            rounded(lohi2[:, 1:2], lohi[:, 1:2], lohi[:, 1:2])
            dve.tensor_scalar(lohi2[:, 1:2], lohi2[:, 1:2], float(MIN_TURNS - 2), None, ALU.max).then_inc(s_lohi, 1)
            dve.wait_ge(s_rngp, 1)
            row = rngf[:, :, :].rearrange("p a t -> p (a t)")
            step(dve.tensor_copy(row[:, 0:2 * NT], bank[0][0:1, 0:2 * NT]))
            step(dve.tensor_copy(rng[:, 0:2 * NT], row[:, 0:2 * NT]))
            step(dve.tensor_tensor_scan(rngf[:, 2, :], ones[0:1, 0:NT], rngf[:, 1, :], 0.0, ALU.mult, ALU.add))
            step(dve.tensor_copy(rng[:, 3 * NT:3 * NT + 1], rngf[:, 2, NT - 1:NT]))
            dve.tensor_tensor(rng[:, 2 * NT:3 * NT], rngf[:, 2, :], rngf[:, 1, :], ALU.subtract).then_inc(s_rng, 1)
            dve.wait_ge(s_x, 16)
            for t in range(NT):
                last = dve.bn_stats(xst[:, t, :], xin[:, t, :])
            step(last)
            for t in range(NT):
                last = dve.bn_aggr(xmv[:, t, :], xst[:, t, :])
            step(last)
            dve.tensor_scalar(xve[:, :], xmv[:, :, 1], LN_EPS, None, ALU.add).then_inc(s_var, 1)
            dve.wait_ge(s_std, 1)
            inverse_root(xrs[:, :], xve[:, :], xsd[:, :], xt1[:, :])
            step(dve.tensor_scalar(xrs[:, :], xrs[:, :], float(2 ** H0_EXP), None, ALU.mult))
            dve.scalar_tensor_tensor(xsh[:, :], xmv[:, :, 0], -1.0, xrs[:, :], ALU.mult, ALU.mult).then_inc(s_xf, 1)

            dve.wait_ge(s_rng, 1)
            dve.wait_ge(s_xf, 1)
            dve.sem_inc(s_free[1], 1)
            dve.sem_inc(s_freeD[1], 1)
            for t in range(NT + 1):
                if t < NT:
                    first, (middle, before) = first_chunk(dve, t), turns(dve, t)
                    if t >= 2:
                        dve.wait_ge(s_iotaK, t - 1)

                    def rows(c, r):
                        dve.tensor_tensor(ohS[r][:, :, :], iotaS[:, :, :],
                                          sl16[:, bass.ds(c, U)].unsqueeze(1).to_broadcast([128, 128, U]), ALU.is_equal)
                        for j in range(U):
                            last = dve.tensor_scalar(cnt1[r][:, j, :], iotaK[:, t % 2, :], keyE[:, bass.ds(c + j, 1)],
                                                     powE[:, bass.ds(c + j, 1)].bitcast(F32), ALU.is_equal, ALU.mult)
                        last.then_inc(s_oh[r], 1)

                    if t:
                        dve.wait_ge(s_free[0], t)
                    rows(first, 0)
                    with dve.Fori(0, middle) as i:
                        dve.wait_ge(s_free[1], before + i + 1)
                        rows(dve.snap(chunk_of(first, i, 1)), 1)
                    if t:
                        dve.wait_ge(s_cnt, t)
                    rows(dve.snap(chunk_of(first, middle, 1)), 2)
                if t:
                    dve.wait_ge(s_enc, t)
                    if t >= 3:
                        dve.wait_ge(s_at, t - 2)
                    u = (t - 1) % 2
                    dve.tensor_scalar(encB[:, u, 0, :], encI[:, u, :], NIBBLES, None, ALU.bitwise_and)
                    dve.tensor_scalar(encB[:, u, 1, :], encI[:, u, :], 4, NIBBLES, ALU.logical_shift_right, ALU.bitwise_and).then_inc(s_nib, 1)
            dve.wait_ge(s_deg, NT)
            step(dve.tensor_copy(deg[:, :], bank[6][0:P, 0:NT]))
            dve.tensor_reduce(bad[:, :], deg[:, :], axis=XYZ, op=ALU.add).then_inc(s_flagp, 1)
            dve.wait_ge(s_flagp, 2)
            dve.tensor_scalar(flag[:, :], bank[7][0:1, 0:1], float(E), None, ALU.not_equal).then_inc(s_flag, 1)
            dve.wait_ge(s_flag, 1)
            with dve.If(dve.value_load(flag[0:1, 0:1], min_val=0, max_val=1) == 1):
                gather_dve(dve, 0, None)
                dve.tensor_copy(deg[:, :], bank[6][0:P, 0:NT]).then_inc(s_flag, 1)
                dve.wait_ge(s_flag, 2)
            step(dve.tensor_scalar(deg1[:, :], deg[:, :], 1.0, None, ALU.max))
            dve.sem_inc(s_var, 1)
            dve.wait_ge(s_std, 2)
            inverse_root(dinvP[:, :], deg1[:, :], dsd[:, :], dt1[:, :])
            step(dve.scalar_tensor_tensor(dinvP[:, :], deg[:, :], 1.0, dinvP[:, :], ALU.min, ALU.mult))
            step(dve.tensor_copy(dpart[:, 0, :], dinvP[:, :]))
            step(dve.tensor_tensor(drem[:, 0, :], dinvP[:, :], dpart[:, 0, :], ALU.subtract))
            step(dve.tensor_copy(dpart[:, 1, :], drem[:, 0, :]))
            step(dve.tensor_tensor(drem[:, 1, :], drem[:, 0, :], dpart[:, 1, :], ALU.subtract))
            step(dve.tensor_copy(dpart[:, 2, :], drem[:, 1, :]))
            dve.sem_inc(s_dpart, 1)
            m_rows_dve(dve, lambda n: 0)
            def sources(b):
                dve.wait_ge(s_slr[b % 2], 16 * (b // 2 + 1))
                if b >= 2:
                    dve.wait_ge(s_lk, b - 1)
                dve.tensor_scalar(ohT[:, b % 2, :], slrow[:, b % 2, :], iotaP[0:P, :], None, ALU.is_equal).then_inc(s_ohT, 1)

            sources(0)
            for b in range(NLB):
                if b + 1 < NLB:
                    sources(b + 1)
                step(dve.tensor_tensor(ohs[:, b % 2, :, :], s16[:, b * LB:(b + 1) * LB].unsqueeze(2).to_broadcast([128, LB, NT]),
                                       iota25[:, :].unsqueeze(1).to_broadcast([128, LB, NT]), ALU.is_equal))
                dve.wait_ge(s_lk, b + 1)
                if b:
                    dve.wait_ge(s_ds, b)
                dve.tensor_tensor(lkt[:, :], bank[1 + b % 2][:, 0:LB * NT], ohs[:, b % 2, :, :].rearrange("p c s -> p (c s)"), ALU.mult).then_inc(s_lke, 1)
                dve.wait_ge(s_lke, b + 1)
                dve.tensor_reduce(dsrc[:, b * LB:(b + 1) * LB], lkt[:, :].rearrange("p (c s) -> p c s", s=NT), axis=XYZ, op=ALU.add).then_inc(s_ds, 1)
            dve.wait_ge(s_ds, NLB)
            step(dve.tensor_tensor(v4[:, :, :], eaE[:, :, :], dsrc[:, :].unsqueeze(2).to_broadcast([128, NCH, 4]), ALU.mult))
            step(dve.memset(w12[:, NCH:NCHP, :], 0.0))
            step(dve.tensor_copy(w12[:, 0:NCH, 0:4], v4[:, :, :]))
            step(dve.tensor_tensor(v4b[:, :, :], v4[:, :, :], w12[:, 0:NCH, 0:4], ALU.subtract))
            step(dve.tensor_copy(w12[:, 0:NCH, 4:8], v4b[:, :, :]))
            step(dve.tensor_tensor(v4[:, :, :], v4b[:, :, :], w12[:, 0:NCH, 4:8], ALU.subtract))
            dve.tensor_copy(w12[:, 0:NCH, 8:12], v4[:, :, :]).then_inc(s_w12, 1)
            dve.memset(ewT[:, :, :], 0.0)
            dve.memset(inv[:, :], 2.0 ** -H0_EXP).then_inc(s_ez, 1)
            dve.wait_ge(s_w12, 1)
            dve.wait_ge(s_ez, 1)
            zero = lambda n: 0
            evicted = 0
            dve.wait_ge(s_dBd, 32)
            ahead = first_chunk(dve, 0), *turns(dve, 0)
            for t in range(NT):
                first, middle, before = ahead
                step(dve.tensor_scalar(iotaD3[:, :, :], iotaD3[:, :, :], float(P), None, ALU.add))

                def rows(c, r):
                    dve.tensor_tensor(ohD[:, r, :, :], iotaD3[:, :, :],
                                      dst3[:, bass.ds(c, U)].unsqueeze(1).to_broadcast([128, P, U]), ALU.is_equal)
                    dve.tensor_copy(nowW[:, r, :, :], w12[:, bass.ds(c, U), :]).then_inc(s_ohD[r], 1)

                if t:
                    dve.wait_ge(s_freeD[0], t)
                rows(first, 0)
                with dve.Fori(0, middle) as i:
                    dve.wait_ge(s_freeD[1], before + i + 1)
                    rows(dve.snap(chunk_of(first, i, 1)), 1)
                if t:
                    dve.wait_ge(s_s4, t)
                rows(dve.snap(chunk_of(first, middle, 1)), 2)
                if t + 1 < NT:
                    ahead = first_chunk(dve, t + 1), *turns(dve, t + 1)
                while NT * (evicted + 1) <= min(DENSE, dense_before(t - 1)):
                    evict(dve, zero, evicted, FIRST_BANKS)
                    evicted += 1
                if t:
                    s4_out(dve, t - 1)
            s4_out(dve, NT - 1)
            dve.wait_ge(s_s4e, 2 * NT)
            part = [s4K[:, :, :].rearrange("p t (a b j) -> p t a b j", a=PARTS, j=4)[:, :, :, b, :] for b in range(PARTS)]
            def thrice(v):
                return v.unsqueeze(2).to_broadcast([P, NT, PARTS, 4])
            step(dve.tensor_copy(s4h[:, 0, :, :], s4P[:, :, :]))
            step(dve.tensor_copy(part[0], thrice(s4h[:, 0, :, :])))
            step(dve.tensor_tensor(s4s[:, :, :], s4P[:, :, :], s4h[:, 0, :, :], ALU.subtract))
            step(dve.tensor_copy(s4h[:, 1, :, :], s4s[:, :, :]))
            step(dve.tensor_copy(part[1], thrice(s4h[:, 1, :, :])))
            step(dve.tensor_tensor(s4P[:, :, :], s4s[:, :, :], s4h[:, 1, :, :], ALU.subtract))
            dve.tensor_copy(part[2], thrice(s4P[:, :, :])).then_inc(s_s4K, 1)
            for g in range(evicted, H * NQ):
                evict(dve, zero, g, FIRST_BANKS)
            with dve.If(dve.value_load(flag[0:1, 0:1], min_val=0, max_val=1) == 1):
                gather_dve(dve, 1, 0)
            weights_dve(dve, LOADS)
            attributes_dve(dve, zero)
            statistics_dve(dve, zero, False)
            with dve.Fori(0, L - 2) as i:
                base = lambda n: dve.snap(i * n + n)
                aggregate_dve(dve, base, i + 1, LOADS * (i + 2))
                statistics_dve(dve, base, False)
            base = lambda n: (L - 1) * n
            aggregate_dve(dve, base, L - 1, LOADS * L)
            statistics_dve(dve, base, True)
            experts_dve(dve, step, rounded, inverse_root)

        @block.scalar
        def _(act):
            act.wait_ge(s_var, 1)
            act.activation(xsd[:, :], xve[:, :], ACT.Sqrt).then_inc(s_std, 1)
            act.wait_ge(s_xf, 1)

            def normal(t):
                act.activation(xin[:, t, :], xin[:, t, :], ACT.Identity, scale=xrs[:, t:t + 1], bias=xsh[:, t:t + 1]).then_inc(s_xn, 1)

            normal(0)
            act.wait_ge(s_sld, 16)
            for t in range(NT + 1):
                if t < NT:
                    act.wait_ge(s_cnt, t + 1)
                    if t >= 2:
                        act.wait_ge(s_nib, t - 1)
                    for b in range(GB):
                        last = act.activation(encI[:, t % 2, b * GC:(b + 1) * GC], bank[GB * (t % 2) + b][0:P, 0:GC], ACT.Copy)
                    last.then_inc(s_enc, 1)
                    if t + 1 < NT:
                        normal(t + 1)
                    act.wait_ge(s_xT, t + 1)
                    act.activation(hT[:, :, t * P:(t + 1) * P], bank[4 + t % 2][:, 0:H * P].rearrange("p (h n) -> p h n", h=H), ACT.Copy).then_inc(s_xTe, 1)
                if t:
                    u = t - 1
                    act.wait_ge(s_nib, u + 1)
                    for odd in range(2):
                        n = (FIELDS + 1 - odd) // 2
                        byte = encB[:, u % 2, odd, 0:GROUPS * P].bitcast(U8).rearrange("p (g n k) -> p k g n", g=GROUPS, k=4)
                        for f in range(n):
                            last = act.activation(at[:, odd + 2 * f:odd + 2 * f + FIELDS * (GROUPS - 1) + 1:FIELDS, u * P:(u + 1) * P],
                                                  byte[:, f, :, :], ACT.Copy, saturate=False)
                    last.then_inc(s_at, 1)
            act.wait_ge(s_var, 2)
            act.activation(dsd[:, :], deg1[:, :], ACT.Sqrt).then_inc(s_std, 1)
            act.wait_ge(s_bc, 1)
            act.activation(dinvT[:, :], bank[5][0:NT, 0:P], ACT.Copy).then_inc(s_dB, 1)
            m_rows_act(act, lambda n: 0)
            for q, (a, w) in enumerate(COLS):
                act.wait_ge(s_s4T, q + 1)
                act.activation(s4T[:, a:a + w], bank[1 + q % 2][0:K4, 0:w], ACT.Copy).then_inc(s_s4Te, 1)
            linear_act(act, lambda n: 0)
            with act.Fori(0, L - 2) as i:
                prev, base = (lambda n: act.snap(i * n)), (lambda n: act.snap(i * n + n))
                m_rows_act(act, base, normalise_act(act, prev, False))
                linear_act(act, base)
            prev, base = (lambda n: (L - 2) * n), (lambda n: (L - 1) * n)
            m_rows_act(act, base, normalise_act(act, prev, False))
            linear_act(act, base)
            last = normalise_act(act, base, True)
            for q in range(NQ):
                last(q)
            experts_act(act)

        @block.tensor
        def _(pe):
            pe.wait_ge(s_mem, 2)
            for n, tile in enumerate((dstC, srcC)):
                pe.wait_ge(s_edges, n + 1)
                for b in range(NB):
                    pe.transpose(bank[n][:, b * CB:(b + 1) * CB], tile[:, b, :], ident[0:CB, 0:CB]).then_inc(s_tp, 1)
            pe.wait_ge(s_ea, 48)
            for j in range(4):
                for b in range(NB):
                    last = pe.transpose(bank[2 + j][:, b * CB:(b + 1) * CB], eaC[:, b, j:j + 4 * (CH - 1) + 1:4], ident[0:CB, 0:CB])
                last.then_inc(s_tp, 1)
            pe.wait_ge(s_cmm, 1)
            for n in range(2):
                for b in range(NB):
                    last = pe.matmul(bank[6 + n][0:NT, b * CB:(b + 1) * CB], cmmB[:, n * NB + b, :], ident[0:CB, 0:CB], start=True, stop=True)
                last.then_inc(s_minmax, 1)
            pe.wait_ge(s_lohi, 1)
            for n in range(2):
                last = pe.matmul(bank[0][0:1, n * NT:(n + 1) * NT], lohi2[:, n:n + 1], ident[0:NT, 0:NT], start=True, stop=True)
            last.then_inc(s_rngp, 1)
            pe.wait_ge(s_rng, 1)

            def degrees(t):
                pe.wait_ge(s_at, t + 1)
                for s in range(NT):
                    last = pe.matmul(bank[6][0:P, t:t + 1], at[:, s, t * P:(t + 1) * P], ones16[0:P, :], start=s == 0, stop=s == NT - 1)
                last.then_inc(s_deg, 1)

            for t in range(NT):
                middle, before = turns(pe, t)
                if t >= 2:
                    pe.wait_ge(s_enc, t - 1)

                def products(r, s_done):
                    for j in range(U):
                        for b in range(GB):
                            last = pe.matmul(bank[GB * (t % 2) + b][:, 0:GC], ohS[r][:, :, j], cnt1[r][:, j, b * GC:(b + 1) * GC],
                                             start=r == 0 and j == 0, stop=r == 2 and j == U - 1)
                    last.then_inc(s_done, 1)

                pe.wait_ge(s_oh[0], t + 1)
                products(0, s_free[0])
                with pe.Fori(0, middle) as i:
                    pe.wait_ge(s_oh[1], before + i + 1)
                    products(1, s_free[1])
                pe.wait_ge(s_oh[2], t + 1)
                products(2, s_cnt)
                pe.wait_ge(s_xn, t + 1)
                if t >= 2:
                    pe.wait_ge(s_xTe, t - 1)
                for h in range(H):
                    last = pe.transpose(bank[4 + t % 2][:, h * P:(h + 1) * P], xin[:, t, h * 128:(h + 1) * 128], ident[0:P, 0:P])
                last.then_inc(s_xT, 1)
                if t >= 2:
                    degrees(t - 2)
            degrees(NT - 2)
            degrees(NT - 1)
            pe.wait_ge(s_flagp, 1)
            pe.matmul(bank[7][0:1, 0:1], ones[0:P, 0:1], bad[:, :], start=True, stop=True).then_inc(s_flagp, 1)
            pe.wait_ge(s_flag, 1)
            with pe.If(pe.value_load(flag[0:1, 0:1], min_val=0, max_val=1) == 1):
                gather_pe(pe, 0, None)
            pe.wait_ge(s_dpart, 1)
            pe.transpose(bank[5][0:NT, 0:P], dinvP[:, :], ident[0:P, 0:P]).then_inc(s_bc, 1)
            pe.wait_ge(s_enc, NT)
            pe.wait_ge(s_xTe, NT)
            zero = lambda n: 0
            for t in range(NT):
                row_pe(pe, zero, None, t)
            pe.wait_ge(s_lo, NT)
            done = [0]

            def dense_to(n):
                for u in range(done[0], min(n, DENSE)):
                    g, t = u // NT, u % NT
                    before = [n for n in range(g) if FIRST_BANKS[n] == FIRST_BANKS[g]]
                    if before and t == 0:
                        pe.wait_ge(s_agge, before[-1] + 1)
                    dense(pe, g, t, FIRST_BANKS)
                done[0] = min(n, DENSE)

            for b in range(NLB):
                pe.wait_ge(s_ohT, b + 1)
                if b >= 2:
                    pe.wait_ge(s_lke, b - 1)
                for c in range(LB):
                    for k in range(3):
                        last = pe.matmul(bank[1 + b % 2][:, c * NT:(c + 1) * NT], ohT[:, b % 2, c * CH:(c + 1) * CH],
                                         dpart[:, k, :], start=k == 0, stop=k == 2)
                last.then_inc(s_lk, 1)
                dense_to(DENSE_L * (b + 1))
            dense_to(dense_before(0))
            pe.wait_ge(s_w12, 1)
            for t in range(NT):
                middle, before = turns(pe, t)
                if t >= 2:
                    pe.wait_ge(s_s4e, 2 * (t - 1) - 1)

                def products(r, s_done):
                    for j in range(U):
                        last = pe.matmul(bank[S4_BANKS[t % 2]][0:P, 0:12], ohD[:, r, :, j],
                                         nowW[:, r, j, :],
                                         start=r == 0 and j == 0, stop=r == 2 and j == U - 1)
                    last.then_inc(s_done, 1)

                pe.wait_ge(s_ohD[0], t + 1)
                products(0, s_freeD[0])
                with pe.Fori(0, middle) as i:
                    pe.wait_ge(s_ohD[1], before + i + 1)
                    products(1, s_freeD[1])
                pe.wait_ge(s_ohD[2], t + 1)
                products(2, s_s4)
                dense_to(dense_before(t + 1))
            pe.wait_ge(s_s4K, 1)
            for q, (a, w) in enumerate(COLS):
                if q >= 2:
                    pe.wait_ge(s_s4Te, q - 1)
                for t in range(a // P, (a + w) // P):
                    last = pe.transpose(bank[1 + q % 2][0:K4, t * P - a:(t + 1) * P - a], s4K[:, t, :], ident[0:P, 0:P])
                last.then_inc(s_s4T, 1)
            dense_to(DENSE)
            pe.wait_ge(s_s4Te, NQ)
            with pe.If(pe.value_load(flag[0:1, 0:1], min_val=0, max_val=1) == 1):
                gather_pe(pe, 1, 0)
            attributes_pe(pe, zero)
            linear_pe(pe, zero)
            with pe.Fori(0, L - 2) as i:
                prev, base = (lambda n: pe.snap(i * n)), (lambda n: pe.snap(i * n + n))
                aggregate_pe(pe, base, prev, i + 1)
                linear_pe(pe, base)
            prev, base = (lambda n: (L - 2) * n), (lambda n: (L - 1) * n)
            aggregate_pe(pe, base, prev, L - 1)
            linear_pe(pe, base)
            experts_pe(pe)


INPUTS = ["x", "src", "dst", "edge_attr_4", "L0_gnn_mlp_w", "L0_gnn_mlp_b", "L0_gnn_ew1", "L0_gnn_ew2", "L0_gnn_bn_g",
          "L0_gnn_bn_b", "L0_ffn_Wg", "L0_ffn_bg", "L0_ffn_bias", "L0_ffn_W1", "L0_ffn_b1", "L0_ffn_W2", "L0_ffn_b2"]


def kernel(**inputs):
    import numpy as np
    from concourse import bacc
    from concourse.bass_utils import run_bass_kernel_spmd

    nc = bacc.Bacc("TRN2", target_bir_lowering=False, num_devices=1)
    arrays, args = {}, []
    for name in INPUTS:
        a = np.ascontiguousarray(inputs[name])
        arrays["in_" + name] = a
        args.append(nc.dram_tensor("in_" + name, a.shape, mybir.dt.from_np(a.dtype), kind="ExternalInput").ap())
    out = nc.dram_tensor("out_rows", (N + TT, D), F32, kind="ExternalOutput").ap()
    gnn_ffn_program(nc, *args, out)
    done = run_bass_kernel_spmd(nc, [arrays], core_ids=[0])
    return done.results[0]["out_rows"][:N]
```
